# Optimizing a Trainium2 kernel written in Bass

```python
import numpy as np
import jax
import jax.numpy as jnp

def _softmax(x, axis=-1):
    return jax.nn.softmax(x, axis=axis)

def _gelu(x):
    return jax.nn.gelu(x, approximate=True)

def _silu(x):
    return jax.nn.silu(x)

def _sigmoid(x):
    return jax.nn.sigmoid(x)

def _layernorm(x, axis=-1, eps=1e-05):
    m = jnp.mean(x, axis=axis, keepdims=True)
    v = jnp.var(x, axis=axis, keepdims=True)
    return (x - m) / jnp.sqrt(v + eps)

def _scatter_add(tgt, idx, src, axis=0):
    return tgt.at[idx].add(src)

def _segment_sum(src, seg, n):
    return jax.ops.segment_sum(src, seg, n)
kernel_name = 'mk_adaln_d2_jaxref_r8_e0b873'

def setup_inputs(seed: int=0):
    np.random.seed(seed)
    _w = jnp.asarray

    def _L0_attn_setup():
        import math
        import jax, jax.numpy as jnp
        import numpy as np
        H = 32
        NOPE = 64
        ROPE = 64
        VD = 128
        QHD = NOPE + ROPE
        KVR = 32
        EPS = 1e-06

        def _yarn_cos_sin(seq_len, dim=ROPE, base=10000.0, factor=128.0, beta_fast=32.0, beta_slow=1.0, orig_max=1024, mscale=1.0, mscale_all_dim=1.0):

            def corr_dim(r):
                return dim * math.log(orig_max / (r * 2 * math.pi)) / (2 * math.log(base))
            low = max(math.floor(corr_dim(beta_fast)), 0)
            high = min(math.ceil(corr_dim(beta_slow)), dim - 1)
            hi = high + 0.001 if low == high else float(high)
            ramp = np.clip((np.arange(dim // 2, dtype=np.float32) - low) / (hi - low), 0.0, 1.0)
            inv_freq_mask = 1.0 - ramp
            freq_extra = 1.0 / base ** (np.arange(0, dim, 2, dtype=np.float32) / dim)
            freq_inter = freq_extra / factor
            inv_freq = freq_inter * (1.0 - inv_freq_mask) + freq_extra * inv_freq_mask
            t = np.arange(seq_len, dtype=np.float32)
            freqs = np.outer(t, inv_freq)
            emb = np.concatenate([freqs, freqs], axis=-1)

            def gm(s, m):
                return 1.0 if s <= 1 else 0.1 * m * math.log(s) + 1.0
            ms = gm(factor, mscale) / gm(factor, mscale_all_dim)
            return (jnp.asarray(np.cos(emb) * ms), jnp.asarray(np.sin(emb) * ms))

        def _rmsnorm(x, w, eps=EPS):
            var = jnp.mean(jnp.square(x), axis=-1, keepdims=True)
            return x * jax.lax.rsqrt(var + eps) * w

        def _deinterleave(x):
            d = x.shape[-1]
            x = x.reshape(*x.shape[:-1], d // 2, 2)
            return jnp.concatenate([x[..., 0], x[..., 1]], axis=-1)

        def _rotate_half(x):
            d = x.shape[-1] // 2
            return jnp.concatenate([-x[..., d:], x[..., :d]], axis=-1)

        def _apply_rope(x, cos, sin):
            return x * cos + _rotate_half(x) * sin
        key = jax.random.key(seed)
        ks = jax.random.split(key, 6)
        B, S, D = (1, 256, 512)
        std = 0.02
        return {'x': jax.random.normal(ks[0], (B, S, D), dtype=jnp.float32), 'wq_a': jax.random.normal(ks[1], (128, D), dtype=jnp.float32) * std, 'q_a_ln_w': jnp.ones((128,), dtype=jnp.float32), 'wq_b': jax.random.normal(ks[2], (H * QHD, 128), dtype=jnp.float32) * std, 'wkv_a': jax.random.normal(ks[3], (KVR + ROPE, D), dtype=jnp.float32) * std, 'kv_a_ln_w': jnp.ones((KVR,), dtype=jnp.float32), 'wkv_b': jax.random.normal(ks[4], (H * (NOPE + VD), KVR), dtype=jnp.float32) * std, 'wo': jax.random.normal(ks[5], (D, H * VD), dtype=jnp.float32) * std}
    _L0_attn_in = _L0_attn_setup()

    def _L0_ffn_setup():
        import jax, jax.numpy as jnp
        import numpy as np

        def sparsemax(z):
            E = z.shape[-1]
            z_sorted = -jnp.sort(-z, axis=-1)
            z_cum = jnp.cumsum(z_sorted, axis=-1)
            k = jnp.arange(1, E + 1, dtype=z.dtype)
            support = 1.0 + k * z_sorted > z_cum
            k_z = jnp.sum(support, axis=-1, keepdims=True)
            tau_sum = jnp.take_along_axis(z_cum, k_z.astype(jnp.int32) - 1, axis=-1)
            tau = (tau_sum - 1.0) / k_z.astype(z.dtype)
            return jnp.maximum(z - tau, 0.0)
        key = jax.random.key(seed)
        ks = jax.random.split(key, 6)
        B, S, D_IN, D_OUT, E, R = (8, 256, 512, 512, 8, 16)
        x = jax.random.normal(ks[0], (B, S, D_IN), dtype=jnp.float32)
        W_base = jax.random.normal(ks[1], (D_OUT, D_IN), dtype=jnp.float32) * D_IN ** (-0.5)
        b_base = jax.random.normal(ks[2], (D_OUT,), dtype=jnp.float32) * 0.01
        W_router = jax.random.normal(ks[3], (E, D_IN), dtype=jnp.float32) * D_IN ** (-0.5)
        b_router = jnp.zeros((E,), dtype=jnp.float32)
        lora_A = jax.random.normal(ks[4], (E, D_IN, R), dtype=jnp.float32) * D_IN ** (-0.5)
        lora_B = jnp.zeros((E, R, D_OUT), dtype=jnp.float32)
        return {'x': x, 'W_base': W_base, 'b_base': b_base, 'W_router': W_router, 'b_router': b_router, 'lora_A': lora_A, 'lora_B': lora_B}
    _L0_ffn_in = _L0_ffn_setup()
    _L0_c = _w((lambda *s: np.random.randn(*s).astype(np.float32) * 0.05)(2, 512))
    _L0_wmod = _w((lambda *s: np.random.randn(*s).astype(np.float32) * 0.05)(512, 6 * 512) * 512 ** (-0.5))

    def _L1_attn_setup():
        import jax, jax.numpy as jnp
        import numpy as np
        DIM = 512
        N_HEADS = 32
        HEAD_DIM = DIM // N_HEADS
        key = jax.random.key(seed)
        k0, k1, k2, k3, k4 = jax.random.split(key, 5)
        B, T = (2, 256)
        x = jax.random.normal(k0, (B, T, DIM), dtype=jnp.float32)
        s = 1.0 / np.sqrt(DIM)
        wq = jax.random.normal(k1, (DIM, DIM), dtype=jnp.float32) * s
        wk = jax.random.normal(k2, (DIM, HEAD_DIM), dtype=jnp.float32) * s
        wv = jax.random.normal(k3, (DIM, HEAD_DIM), dtype=jnp.float32) * s
        wo = jax.random.normal(k4, (DIM, DIM), dtype=jnp.float32) * s
        return {'x': x, 'wq': wq, 'wk': wk, 'wv': wv, 'wo': wo}
    _L1_attn_in = _L1_attn_setup()

    def _L1_ffn_setup():
        import math
        import jax, jax.numpy as jnp
        import numpy as np
        SCALING = 16.0 / 32.0

        def real_fourier_orthogonal_multiply(c):
            n = c.shape[-1]
            sqrt_n = math.sqrt(n)
            pair_scale = math.sqrt(n / 2.0)
            max_f = (n - 1) // 2
            work = c.astype(jnp.float32)
            dc = (work[..., 0] * sqrt_n)[..., None].astype(jnp.complex64)
            cos = work[..., 1:1 + 2 * max_f:2] * pair_scale
            sin = work[..., 2:2 + 2 * max_f:2] * pair_scale
            mid = (cos - 1j * sin).astype(jnp.complex64)
            parts = [dc, mid]
            if n % 2 == 0:
                parts.append((work[..., -1] * sqrt_n)[..., None].astype(jnp.complex64))
            spectrum = jnp.concatenate(parts, axis=-1)
            return jnp.fft.irfft(spectrum, n=n, axis=-1).astype(c.dtype)
        key = jax.random.key(seed)
        ks = jax.random.split(key, 9)
        B, S, D_in, D_out, R0, R1, E = (4, 256, 512, 512, 32, 8, 3)
        x = jax.random.normal(ks[0], (B, S, D_in), dtype=jnp.float32)
        W_base = jax.random.normal(ks[1], (D_out, D_in), dtype=jnp.float32) * 0.02
        b_base = jax.random.normal(ks[2], (D_out,), dtype=jnp.float32) * 0.02
        enc0 = jax.random.normal(ks[3], (R0, D_in), dtype=jnp.float32) * 0.02
        enc1 = jax.random.normal(ks[4], (R1, D_in), dtype=jnp.float32) * 0.02
        coefs0 = jax.random.normal(ks[5], (E, D_out, R0), dtype=jnp.float32) * 0.02
        coefs1 = jax.random.normal(ks[6], (E, D_out, R1), dtype=jnp.float32) * 0.02
        mask0 = jax.random.randint(ks[7], (E, D_out, R0), 0, 2).astype(bool)
        mask1 = jax.random.randint(ks[8], (E, D_out, R1), 0, 2).astype(bool)
        return dict(x=x, W_base=W_base, b_base=b_base, enc0=enc0, enc1=enc1, coefs0=coefs0, coefs1=coefs1, mask0=mask0, mask1=mask1)
    _L1_ffn_in = _L1_ffn_setup()
    _L1_c = _w((lambda *s: np.random.randn(*s).astype(np.float32) * 0.05)(2, 512))
    _L1_wmod = _w((lambda *s: np.random.randn(*s).astype(np.float32) * 0.05)(512, 6 * 512) * 512 ** (-0.5))
    _d = {'L0_attn_x': _L0_attn_in['x'], 'L0_attn_wq_a': _L0_attn_in['wq_a'], 'L0_attn_q_a_ln_w': _L0_attn_in['q_a_ln_w'], 'L0_attn_wq_b': _L0_attn_in['wq_b'], 'L0_attn_wkv_a': _L0_attn_in['wkv_a'], 'L0_attn_kv_a_ln_w': _L0_attn_in['kv_a_ln_w'], 'L0_attn_wkv_b': _L0_attn_in['wkv_b'], 'L0_attn_wo': _L0_attn_in['wo'], 'L0_ffn_W_base': _L0_ffn_in['W_base'], 'L0_ffn_b_base': _L0_ffn_in['b_base'], 'L0_ffn_W_router': _L0_ffn_in['W_router'], 'L0_ffn_b_router': _L0_ffn_in['b_router'], 'L0_ffn_lora_A': _L0_ffn_in['lora_A'], 'L0_ffn_lora_B': _L0_ffn_in['lora_B'], 'L0_c': _L0_c, 'L0_wmod': _L0_wmod, 'L1_attn_wq': _L1_attn_in['wq'], 'L1_attn_wk': _L1_attn_in['wk'], 'L1_attn_wv': _L1_attn_in['wv'], 'L1_attn_wo': _L1_attn_in['wo'], 'L1_ffn_W_base': _L1_ffn_in['W_base'], 'L1_ffn_b_base': _L1_ffn_in['b_base'], 'L1_ffn_enc0': _L1_ffn_in['enc0'], 'L1_ffn_enc1': _L1_ffn_in['enc1'], 'L1_ffn_coefs0': _L1_ffn_in['coefs0'], 'L1_ffn_coefs1': _L1_ffn_in['coefs1'], 'L1_ffn_mask0': _L1_ffn_in['mask0'], 'L1_ffn_mask1': _L1_ffn_in['mask1'], 'L1_c': _L1_c, 'L1_wmod': _L1_wmod}
    _x0 = _d['L0_attn_x']
    _d['L0_attn_x'] = jax.random.normal(jax.random.fold_in(jax.random.key(seed), 1), (2, 1024, 512), dtype=_x0.dtype)
    del _x0
    return _d

def reference(L0_attn_x, L0_attn_wq_a, L0_attn_q_a_ln_w, L0_attn_wq_b, L0_attn_wkv_a, L0_attn_kv_a_ln_w, L0_attn_wkv_b, L0_attn_wo, L0_ffn_W_base, L0_ffn_b_base, L0_ffn_W_router, L0_ffn_b_router, L0_ffn_lora_A, L0_ffn_lora_B, L0_c, L0_wmod, L1_attn_wq, L1_attn_wk, L1_attn_wv, L1_attn_wo, L1_ffn_W_base, L1_ffn_b_base, L1_ffn_enc0, L1_ffn_enc1, L1_ffn_coefs0, L1_ffn_coefs1, L1_ffn_mask0, L1_ffn_mask1, L1_c, L1_wmod):

    def _L0_attn_ref(x, wq_a, q_a_ln_w, wq_b, wkv_a, kv_a_ln_w, wkv_b, wo):
        import math
        import jax, jax.numpy as jnp
        import numpy as np
        H = 32
        NOPE = 64
        ROPE = 64
        VD = 128
        QHD = NOPE + ROPE
        KVR = 32
        EPS = 1e-06

        def _yarn_cos_sin(seq_len, dim=ROPE, base=10000.0, factor=128.0, beta_fast=32.0, beta_slow=1.0, orig_max=1024, mscale=1.0, mscale_all_dim=1.0):

            def corr_dim(r):
                return dim * math.log(orig_max / (r * 2 * math.pi)) / (2 * math.log(base))
            low = max(math.floor(corr_dim(beta_fast)), 0)
            high = min(math.ceil(corr_dim(beta_slow)), dim - 1)
            hi = high + 0.001 if low == high else float(high)
            ramp = np.clip((np.arange(dim // 2, dtype=np.float32) - low) / (hi - low), 0.0, 1.0)
            inv_freq_mask = 1.0 - ramp
            freq_extra = 1.0 / base ** (np.arange(0, dim, 2, dtype=np.float32) / dim)
            freq_inter = freq_extra / factor
            inv_freq = freq_inter * (1.0 - inv_freq_mask) + freq_extra * inv_freq_mask
            t = np.arange(seq_len, dtype=np.float32)
            freqs = np.outer(t, inv_freq)
            emb = np.concatenate([freqs, freqs], axis=-1)

            def gm(s, m):
                return 1.0 if s <= 1 else 0.1 * m * math.log(s) + 1.0
            ms = gm(factor, mscale) / gm(factor, mscale_all_dim)
            return (jnp.asarray(np.cos(emb) * ms), jnp.asarray(np.sin(emb) * ms))

        def _rmsnorm(x, w, eps=EPS):
            var = jnp.mean(jnp.square(x), axis=-1, keepdims=True)
            return x * jax.lax.rsqrt(var + eps) * w

        def _deinterleave(x):
            d = x.shape[-1]
            x = x.reshape(*x.shape[:-1], d // 2, 2)
            return jnp.concatenate([x[..., 0], x[..., 1]], axis=-1)

        def _rotate_half(x):
            d = x.shape[-1] // 2
            return jnp.concatenate([-x[..., d:], x[..., :d]], axis=-1)

        def _apply_rope(x, cos, sin):
            return x * cos + _rotate_half(x) * sin
        B, S, D = x.shape
        m = 0.1 * 1.0 * math.log(128.0) + 1.0
        softmax_scale = QHD ** (-0.5) * m * m
        q = _rmsnorm(x @ wq_a.T, q_a_ln_w) @ wq_b.T
        q = q.reshape(B, S, H, QHD)
        q_nope, q_pe = (q[..., :NOPE], q[..., NOPE:])
        ckv_kpe = x @ wkv_a.T
        ckv, k_pe = (ckv_kpe[..., :KVR], ckv_kpe[..., KVR:])
        kv = _rmsnorm(ckv, kv_a_ln_w) @ wkv_b.T
        kv = kv.reshape(B, S, H, NOPE + VD)
        k_nope, v = (kv[..., :NOPE], kv[..., NOPE:])
        cos, sin = _yarn_cos_sin(S)
        q_pe = _apply_rope(_deinterleave(q_pe), cos[None, :, None, :], sin[None, :, None, :])
        k_pe = _apply_rope(_deinterleave(k_pe), cos[None, :, :], sin[None, :, :])
        q_full = jnp.concatenate([q_nope, q_pe], axis=-1)
        k_full = jnp.concatenate([k_nope, jnp.broadcast_to(k_pe[:, :, None, :], (B, S, H, ROPE))], axis=-1)
        scores = jnp.einsum('bqhd,bkhd->bhqk', q_full, k_full) * softmax_scale
        causal = jnp.tril(jnp.ones((S, S), dtype=bool))
        scores = jnp.where(causal[None, None], scores, jnp.finfo(scores.dtype).min)
        attn = jax.nn.softmax(scores, axis=-1)
        out = jnp.einsum('bhqk,bkhd->bqhd', attn, v).reshape(B, S, H * VD)
        return out @ wo.T

    def _L0_ffn_ref(x, W_base, b_base, W_router, b_router, lora_A, lora_B):
        import jax, jax.numpy as jnp
        import numpy as np

        def sparsemax(z):
            E = z.shape[-1]
            z_sorted = -jnp.sort(-z, axis=-1)
            z_cum = jnp.cumsum(z_sorted, axis=-1)
            k = jnp.arange(1, E + 1, dtype=z.dtype)
            support = 1.0 + k * z_sorted > z_cum
            k_z = jnp.sum(support, axis=-1, keepdims=True)
            tau_sum = jnp.take_along_axis(z_cum, k_z.astype(jnp.int32) - 1, axis=-1)
            tau = (tau_sum - 1.0) / k_z.astype(z.dtype)
            return jnp.maximum(z - tau, 0.0)
        base_out = jnp.einsum('bsd,od->bso', x, W_base) + b_base
        logits = jnp.einsum('bsd,ed->bse', x, W_router) + b_router
        weights = sparsemax(logits)
        h = jnp.einsum('bsd,edr->bser', x, lora_A)
        expert_out = jnp.einsum('bser,bse,ero->bso', h, weights, lora_B)
        return base_out + expert_out

    def _L1_attn_ref(x, wq, wk, wv, wo):
        import jax, jax.numpy as jnp
        import numpy as np
        DIM = 512
        N_HEADS = 32
        HEAD_DIM = DIM // N_HEADS
        B, T, C = x.shape
        q = (x @ wq).reshape(B, T, N_HEADS, HEAD_DIM)
        k = x @ wk
        v = x @ wv
        scale = 1.0 / jnp.sqrt(jnp.asarray(HEAD_DIM, dtype=x.dtype))
        scores = jnp.einsum('bqhd,bkd->bhqk', q, k) * scale
        causal = jnp.tril(jnp.ones((T, T), dtype=bool))
        scores = jnp.where(causal[None, None], scores, -jnp.inf)
        probs = jax.nn.softmax(scores.astype(jnp.float32), axis=-1).astype(x.dtype)
        out = jnp.einsum('bhqk,bkd->bqhd', probs, v).reshape(B, T, C)
        return out @ wo

    def _L1_ffn_ref(x, W_base, b_base, enc0, enc1, coefs0, coefs1, mask0, mask1):
        import math
        import jax, jax.numpy as jnp
        import numpy as np
        SCALING = 16.0 / 32.0

        def real_fourier_orthogonal_multiply(c):
            n = c.shape[-1]
            sqrt_n = math.sqrt(n)
            pair_scale = math.sqrt(n / 2.0)
            max_f = (n - 1) // 2
            work = c.astype(jnp.float32)
            dc = (work[..., 0] * sqrt_n)[..., None].astype(jnp.complex64)
            cos = work[..., 1:1 + 2 * max_f:2] * pair_scale
            sin = work[..., 2:2 + 2 * max_f:2] * pair_scale
            mid = (cos - 1j * sin).astype(jnp.complex64)
            parts = [dc, mid]
            if n % 2 == 0:
                parts.append((work[..., -1] * sqrt_n)[..., None].astype(jnp.complex64))
            spectrum = jnp.concatenate(parts, axis=-1)
            return jnp.fft.irfft(spectrum, n=n, axis=-1).astype(c.dtype)
        base = jnp.einsum('bsd,od->bso', x, W_base) + b_base
        e0 = jnp.einsum('bsd,rd->bsr', x, enc0)
        e1 = jnp.einsum('bsd,rd->bsr', x, enc1)
        w0 = coefs0 * mask0.astype(coefs0.dtype)
        w1 = coefs1 * mask1.astype(coefs1.dtype)
        decoded = jnp.einsum('bsr,eor->ebso', e0, w0) + jnp.einsum('bsr,eor->ebso', e1, w1)
        transformed = real_fourier_orthogonal_multiply(decoded)
        update = transformed.sum(axis=0)
        return base + update * SCALING
    x = L0_attn_x
    mod = (_silu(L0_c) @ L0_wmod).reshape(L0_c.shape[0], 6, 1, -1)
    sa, ca, ga, sb, cb, gb = (mod[:, 0], mod[:, 1], mod[:, 2], mod[:, 3], mod[:, 4], mod[:, 5])
    ga = (2 * (ga >= 0) - 1) * jnp.maximum(jnp.abs(ga), 0.25)
    gb = (2 * (gb >= 0) - 1) * jnp.maximum(jnp.abs(gb), 0.25)
    h = _layernorm(x, axis=-1) * (1 + ca) + sa
    x = x + ga * _L0_attn_ref(h, L0_attn_wq_a, L0_attn_q_a_ln_w, L0_attn_wq_b, L0_attn_wkv_a, L0_attn_kv_a_ln_w, L0_attn_wkv_b, L0_attn_wo)
    h = _layernorm(x, axis=-1) * (1 + cb) + sb
    x = x + gb * _L0_ffn_ref(h, L0_ffn_W_base, L0_ffn_b_base, L0_ffn_W_router, L0_ffn_b_router, L0_ffn_lora_A, L0_ffn_lora_B)
    mod = (_silu(L1_c) @ L1_wmod).reshape(L1_c.shape[0], 6, 1, -1)
    sa, ca, ga, sb, cb, gb = (mod[:, 0], mod[:, 1], mod[:, 2], mod[:, 3], mod[:, 4], mod[:, 5])
    ga = (2 * (ga >= 0) - 1) * jnp.maximum(jnp.abs(ga), 0.25)
    gb = (2 * (gb >= 0) - 1) * jnp.maximum(jnp.abs(gb), 0.25)
    h = _layernorm(x, axis=-1) * (1 + ca) + sa
    x = x + ga * _L1_attn_ref(h, L1_attn_wq, L1_attn_wk, L1_attn_wv, L1_attn_wo)
    h = _layernorm(x, axis=-1) * (1 + cb) + sb
    x = x + gb * _L1_ffn_ref(h, L1_ffn_W_base, L1_ffn_b_base, L1_ffn_enc0, L1_ffn_enc1, L1_ffn_coefs0, L1_ffn_coefs1, L1_ffn_mask0, L1_ffn_mask1)
    return x

_drawn_inputs = setup_inputs


def setup_inputs(seed=0):
    import zlib

    import numpy as np

    out = dict(_drawn_inputs(seed))
    spreads = {'L0_attn_q_a_ln_w': (1.0, 0.6),
     'L0_attn_kv_a_ln_w': (1.0, 0.6),
     'L0_ffn_b_router': (0.0, 2.0),
     'L0_ffn_lora_B': (0.0, 0.295)}
    factors = {'L0_attn_wq_a': 8.0,
     'L0_attn_wq_b': 8.0,
     'L0_attn_wkv_a': 8.0,
     'L0_attn_wkv_b': 8.0,
     'L0_attn_wo': 8.0,
     'L0_ffn_b_base': 64.0,
     'L1_ffn_b_base': 34.693,
     'L1_ffn_enc0': 7.507,
     'L1_ffn_enc1': 8.0,
     'L1_ffn_coefs0': 7.486,
     'L1_ffn_coefs1': 8.0,
     'L1_attn_wq': 6.43,
     'L1_attn_wk': 6.363,
     'L1_attn_wv': 3.662,
     'L1_attn_wo': 3.786}
    for name, (base, spread) in spreads.items():
        noise = np.random.default_rng([zlib.crc32(name.encode()), seed]).standard_normal(out[name].shape)
        drawn = base * np.exp(spread * noise) if base else spread * noise
        out[name] = jnp.asarray(drawn.astype(out[name].dtype))
    for name, factor in factors.items():
        out[name] = (out[name] * factor).astype(out[name].dtype)
    return out
```

```python
import math
from contextlib import ExitStack

import numpy as np

import concourse.bass as bass
from concourse import mybir

F32 = mybir.dt.float32
F32R = mybir.dt.float32r
U8 = mybir.dt.uint8
I32 = mybir.dt.int32
ALU = mybir.AluOpType
ACT = mybir.ActivationFunctionType
AX_X = mybir.AxisListType.X

P = 128
B, S, D = 2, 1024, 512
C = D // P
H = 32
NOPE, ROPE, VD, LAT = 64, 64, 128, 32
RH = ROPE // 2
QA = 128
HD = 16
G = 4
NG = H // G
TILES = S // P
HALF = 512
E, R = 8, 16
R0, R1, E1 = 32, 8, 3
LOW = R0 + R1
LN_EPS, RMS_EPS = 1e-5, 1e-6
MSCALE = 0.1 * math.log(128.0) + 1.0
SCALE0 = (NOPE + ROPE) ** -0.5 * MSCALE * MSCALE
SCALE1 = HD ** -0.5
ADAPT = 16.0 / 32.0
LOWEST = -3.0e38
BELOW = -1.0e38
KR = LAT + ROPE
MR = KR
CREDIT = 64


def at(n):
    return n + CREDIT


def semaphores(ctx, nc, prefix, names):
    return {name: ctx.enter_context(nc.semaphore(prefix + name)) for name in names.split()}


def words(ap):
    return ap.bitcast(F32)


def apart(eng, passed):
    eng.sem_inc(passed)


def in_pairs(eng, first, last, body):
    if last - first >= 4:
        with eng.Fori(0, (last - first) // 2) as i:
            for slot in (0, 1):
                body(i * 2 + (first + slot), slot, i + first // 2)
    else:
        for k in range(first, last):
            body(k, k % 2, k // 2)


def modulation(nc, name, c_t, wmod, mod_t, gates):
    with ExitStack() as ctx:
        sb = lambda n, s, d=F32: ctx.enter_context(nc.sbuf_tensor(name + n, s, d))
        s = semaphores(ctx, nc, name, "c_in w_in exp_done one_plus sigm silu_done spread gate_psum gate_max gate_min "
                 "gate_pos gate_neg gate_done cols_psum cols_done ones_set")
        cin, ex, sg = sb("cin", [P, C, B]), sb("ex", [P, C, B]), sb("sg", [P, C, B])
        silu = sb("silu", [P, C, B])
        rep = sb("rep", [P, B, C, P])
        w = sb("w", [P, C, 6 * D])
        hi, lo = sb("hi", [P, 4, D]), sb("lo", [P, 4, D])
        gps = ctx.enter_context(nc.psum_tensor(name + "gps", [P, 4, D], F32))
        cps = ctx.enter_context(nc.psum_tensor(name + "cps", [P, D], F32))
        KIND = (0, 1, 3, 4)
        GATE = (2, 5)
        with nc.Block() as block:
            @block.sync
            def _(sp):
                sp.dma_start(cin[:], c_t).then_inc(s["c_in"], 16)
                for k in range(C):
                    sp.dma_start(w[:, k, :], wmod[k * P:(k + 1) * P, :]).then_inc(s["w_in"], 16)

            @block.scalar
            def _(act):
                act.wait_ge(s["c_in"], 16)
                nc.scalar.activation(ex[:], cin[:], ACT.Exp, scale=-1.0).then_inc(s["exp_done"], 1)

            @block.vector
            def _(dve):
                dve.wait_ge(s["exp_done"], 1)
                nc.vector.tensor_scalar(ex[:], ex[:], 1.0, None, ALU.add).then_inc(s["one_plus"], 1)
                dve.wait_ge(s["one_plus"], 1)
                nc.vector.reciprocal(sg[:], ex[:]).then_inc(s["sigm"], 1)
                dve.wait_ge(s["sigm"], 1)
                nc.vector.tensor_tensor(silu[:], cin[:], sg[:], ALU.mult).then_inc(s["silu_done"], 1)
                dve.wait_ge(s["silu_done"], 1)
                for b in range(B):
                    for k in range(C):
                        nc.vector.tensor_copy(rep[:, b, k, :], silu[:, k, b:b + 1].to_broadcast([P, P])).then_inc(s["spread"], 1)
                for n in range(4):
                    g = gps[:, n, :]
                    dve.wait_ge(s["gate_psum"], n + 1)
                    nc.vector.tensor_scalar(hi[:, n, :], g, 0.25, None, ALU.max).then_inc(s["gate_max"], 1)
                    nc.vector.tensor_scalar(lo[:, n, :], g, -0.25, None, ALU.min).then_inc(s["gate_min"], 1)
                    dve.wait_ge(s["gate_max"], n + 1)
                    nc.vector.scalar_tensor_tensor(out=hi[:, n, :], in0=g, scalar=0.0, in1=hi[:, n, :],
                                                   op0=ALU.is_ge, op1=ALU.mult).then_inc(s["gate_pos"], 1)
                    dve.wait_ge(s["gate_min"], n + 1)
                    nc.vector.scalar_tensor_tensor(out=lo[:, n, :], in0=g, scalar=0.0, in1=lo[:, n, :],
                                                   op0=ALU.is_lt, op1=ALU.mult).then_inc(s["gate_neg"], 1)
                    dve.wait_ge(s["gate_pos"], n + 1)
                    dve.wait_ge(s["gate_neg"], n + 1)
                    nc.vector.tensor_tensor(gates[:, n // B, n % B, :], hi[:, n, :], lo[:, n, :], ALU.add).then_inc(s["gate_done"], 1)
                dve.wait_ge(s["cols_psum"], 1)
                cols = cps[:, 0:4 * C * B].rearrange("p (q k b) -> p q k b", q=4, k=C)
                for q in range(4):
                    nc.vector.tensor_scalar(mod_t[:, q, :, :], cols[:, q, :, :], float(q % 2), None, ALU.add).then_inc(s["cols_done"], 1)

            @block.tensor
            def _(pe):
                pe.wait_ge(s["w_in"], 16 * C)
                pe.wait_ge(s["spread"], B * C)
                for n in range(4):
                    for k in range(C):
                        mm = nc.tensor.matmul(gps[:, n, :], rep[:, n % B, k, :], w[:, k, GATE[n // B] * D:(GATE[n // B] + 1) * D],
                                              start=(k == 0), stop=(k == C - 1))
                    mm.then_inc(s["gate_psum"], 1)
                for q in range(4):
                    for m in range(C):
                        o = (q * C + m) * B
                        for k in range(C):
                            mm = nc.tensor.matmul(cps[:, o:o + B], w[:, k, KIND[q] * D + m * P:KIND[q] * D + (m + 1) * P],
                                                  silu[:, k, :], start=(k == 0), stop=(k == C - 1))
                mm.then_inc(s["cols_psum"], 1)
        clear(nc, s)


def join_weights(nc, t, wq_dram, wout_dram):
    with ExitStack() as ctx:
        sb = lambda n, s, d=F32: ctx.enter_context(nc.sbuf_tensor("jw_" + n, s, d))
        s = semaphores(ctx, nc, "jw_", "small_in wo_in0 wo_in1 lat_psum lat_done rope_done wq_out vo_psum vo_done vo_out0 vo_out1")
        wo_in, vo_out = (s["wo_in0"], s["wo_in1"]), (s["vo_out0"], s["vo_out1"])
        nope = sb("nope", [NOPE, H, QA])
        wk = sb("wk", [NOPE, H, LAT])
        wv = sb("wv", [VD, H, LAT])
        rope = sb("rope", [QA, NG, 2, P])
        lnw = sb("lnw", [QA, 1])
        wo = sb("wo", [VD, 2, G, D])
        wq = sb("wq", [QA, NG, 3, P])
        vo = sb("vo", [P, 2, D])
        lps = ctx.enter_context(nc.psum_tensor("jw_lps", [P, 2, 512], F32))
        vps = ctx.enter_context(nc.psum_tensor("jw_vps", [P, 2, 512], F32))
        with nc.Block() as block:
            @block.sync
            def _(sp):
                for dst, src in ((nope, t["wqb_nope"]), (wk, t["wk_b"]), (wv, t["wv_b"]), (rope, t["wqb_rope"]), (lnw, t["q_ln"])):
                    sp.dma_start(dst[:], src).then_inc(s["small_in"], 16)
                def store(g):
                    sp.wait_ge(s["vo_done"], g + 1)
                    sp.dma_start(wout_dram[g], vo[:, g % 2, :]).then_inc(vo_out[g % 2], 16)

                for g in range(NG):
                    if g >= 2:
                        sp.wait_ge(s["vo_psum"], g - 1)
                    sp.dma_start(wo[:, g % 2, :, :], t["wo_t"][g * G:(g + 1) * G].rearrange("h p n -> p h n")).then_inc(wo_in[g % 2], 16)
                    if g >= 2:
                        store(g - 2)
                for g in range(NG - 2, NG):
                    store(g)
                sp.wait_ge(s["lat_done"], 2)
                sp.wait_ge(s["rope_done"], 1)
                sp.dma_start(wq_dram.rearrange("g p n -> p g n"), wq[:].rearrange("p g a n -> p g (a n)")).then_inc(s["wq_out"], 16)
                for sem in vo_out:
                    sp.wait_ge(sem, 16 * NG // 2)
                sp.wait_ge(s["wq_out"], 16)

            @block.tensor
            def _(pe):
                pe.wait_ge(s["small_in"], 80)
                for h in range(H):
                    o = (h % 16) * LAT
                    mm = nc.tensor.matmul(lps[:, h // 16, o:o + LAT], nope[:, h, :], wk[:, h, :], start=True, stop=True)
                mm.then_inc(s["lat_psum"], 1)
                for g in range(NG):
                    pe.wait_ge(wo_in[g % 2], 16 * (g // 2 + 1))
                    if g >= 2:
                        pe.wait_ge(s["vo_done"], g - 1)
                    for j in range(G):
                        mm = nc.tensor.matmul(vps[LAT * j:LAT * (j + 1), g % 2, :], wv[:, g * G + j, :], wo[:, g % 2, j, :],
                                              start=True, stop=True)
                    mm.then_inc(s["vo_psum"], 1)

            @block.vector
            def _(dve):
                dve.wait_ge(s["small_in"], 80)
                nc.vector.tensor_scalar(wq[:, :, 1:3, :], rope[:], lnw[:, 0:1], SCALE0, ALU.mult, ALU.mult).then_inc(s["rope_done"], 1)
                dve.wait_ge(s["lat_psum"], 1)
                for c in range(2):
                    nc.vector.tensor_scalar(wq[:, 4 * c:4 * c + 4, 0, :], lps[:, c, :].rearrange("p (g n) -> p g n", n=P),
                                            lnw[:, 0:1], SCALE0, ALU.mult, ALU.mult).then_inc(s["lat_done"], 1)

            @block.scalar
            def _(act):
                for g in range(NG):
                    act.wait_ge(s["vo_psum"], g + 1)
                    if g >= 2:
                        act.wait_ge(vo_out[g % 2], 16 * (g // 2))
                    nc.scalar.activation(vo[:, g % 2, :], vps[:, g % 2, :], ACT.Copy).then_inc(s["vo_done"], 1)
        clear(nc, s)


NORM_SEMS = "passed stats_done meanvar_done std_done rstd_done xn_done h_psum h_done"


def norm_vector(nc, dve, s, n, slot, x, st, mv, xn):
    nc.vector.bn_stats(st[:, slot, :], x).then_inc(s["stats_done"], 1)
    dve.wait_ge(s["stats_done"], at(n + 1))
    apart(dve, s["passed"])
    nc.vector.bn_aggr(mv[:, slot, 0:2], st[:, slot, :]).then_inc(s["meanvar_done"], 1)
    dve.wait_ge(s["std_done"], at(n + 1))
    nc.vector.reciprocal(mv[:, slot, 3:4], mv[:, slot, 2:3]).then_inc(s["rstd_done"], 1)
    dve.wait_ge(s["rstd_done"], at(n + 1))
    dve.wait_ge(s["h_psum"], at(n - 1))
    nc.vector.tensor_scalar(xn[:, slot, :], x, mv[:, slot, 0:1], mv[:, slot, 3:4],
                            ALU.subtract, ALU.mult).then_inc(s["xn_done"], 1)


def norm_scalar(nc, act, s, n, slot, mv, eps):
    act.wait_ge(s["meanvar_done"], at(n + 1))
    nc.scalar.activation(mv[:, slot, 2:3], mv[:, slot, 1:2], ACT.Sqrt, bias=eps[:, 0:1]).then_inc(s["std_done"], 1)


def norm_tensor(nc, pe, s, n, slot, xn, ident, hps):
    pe.wait_ge(s["xn_done"], at(n + 1))
    pe.wait_ge(s["h_done"], at(C * n))
    for c in range(C):
        tr = nc.tensor.transpose(hps[:, c, :], xn[:, slot, c * P:(c + 1) * P], ident[:])
    tr.then_inc(s["h_psum"], 1)


def modulate(nc, act, s, n, slot, hps, h_t, mod_t, kind, b, used):
    act.wait_ge(s["h_psum"], at(n + 1))
    act.wait_ge(used, at(n - 1))
    for c in range(C):
        nc.scalar.activation(h_t[:, slot, c, :], hps[:, c, :], ACT.Identity, bias=mod_t[:, kind, c, b:b + 1],
                             scale=mod_t[:, kind + 1, c, b:b + 1]).then_inc(s["h_done"], 1)


def clear(nc, *groups):
    with nc.Block() as block:
        @block.sync
        def _(sp):
            for sems in groups:
                for sem in sems.values():
                    sp.sem_clear(sem)


def prime(nc, sems):
    with nc.Block() as block:
        @block.sync
        def _(sp):
            for name, sem in sems.items():
                if "_in" not in name:
                    sp.sem_inc(sem, CREDIT)


IN0 = (NORM_SEMS + " a_psum ss_done ms_done rms_done rr_done qa_done c_done cn_done ropes_done k_done "
       "lat_t_psum qat_done khi_done klo_done")


def latents(nc, s, x_in, b, t, k):
    with ExitStack() as ctx:
        nm = f"la{b}_"
        sb = lambda n, sh, d=F32: ctx.enter_context(nc.sbuf_tensor(nm + n, sh, d))
        ps = lambda n, sh: ctx.enter_context(nc.psum_tensor(nm + n, sh, F32))
        own = semaphores(ctx, nc, nm, "w_in x_in0 x_in1")
        w_in, x_sem = own["w_in"], (own["x_in0"], own["x_in1"])
        W = QA + LAT + ROPE
        w = sb("w", [P, C, W])
        xt, xn = sb("xt", [P, 2, D]), sb("xn", [P, 2, D])
        st, mv = sb("st", [P, 2, 6]), sb("mv", [P, 2, 4])
        h_t = sb("h_t", [P, 2, C, P])
        sq = sb("sq", [P, 2, P])
        ss, rr = sb("ss", [P, 2, 2]), sb("rr", [P, 2, 4])
        qa = sb("qa", [P, 2, QA])
        kk = sb("kk", [P, 2, KR])
        tm = sb("tm", [P, 2, 4, RH])
        hps, aps, tps = ps("hps", [P, C, P]), ps("aps", [P, 2, 512]), ps("tps", [P, 2, 512])
        X1, X2 = QA + LAT, QA + LAT + RH
        with nc.Block() as block:
            @block.sync
            def _(sp):
                sp.dma_start(w[:], t["w_a"].rearrange("(k p) n -> p k n", p=P)).then_inc(w_in, 16)

                def load(n, slot, turn):
                    sp.wait_ge(s["xn_done"], at(n + b * TILES - 1))
                    sp.dma_start(xt[:, slot, :], x_in[bass.ds((n + b * TILES) * P, P), :]).then_inc(x_sem[slot], 16)
                in_pairs(sp, 0, TILES, load)

            @block.tensor
            def _(pe):
                pe.wait_ge(w_in, 16)

                def tile(n0, slot, turn):
                    n = n0 + b * TILES
                    norm_tensor(nc, pe, s, n, slot, xn, k.ident, hps)
                    pe.wait_ge(s["h_done"], at(C * n + C))
                    pe.wait_ge(s["qa_done"], at(n - 1))
                    pe.wait_ge(s["ropes_done"], at(4 * n - 4))
                    for c in range(C):
                        mm = nc.tensor.matmul(aps[:, slot, 0:W], h_t[:, slot, c, :], w[:, c, :], start=(c == 0), stop=(c == C - 1))
                    mm.then_inc(s["a_psum"], 1)
                    pe.wait_ge(s["qa_done"], at(n + 1))
                    pe.wait_ge(s["k_done"], at(2 * n + 2))
                    pe.wait_ge(s["cn_done"], at(2 * n + 2))
                    pe.wait_ge(s["qat_done"], at(n - 1))
                    pe.wait_ge(s["klo_done"], at(n - 1))
                    nc.tensor.transpose(tps[:, slot, 0:P], qa[:, slot, :], k.ident[:])
                    nc.tensor.transpose(tps[0:KR, slot, P:2 * P], kk[:, slot, :], k.ident[:]).then_inc(s["lat_t_psum"], 1)
                in_pairs(pe, 0, TILES, tile)

            @block.scalar
            def _(act):
                def tile(n0, slot, turn):
                    n = n0 + b * TILES
                    norm_scalar(nc, act, s, n, slot, mv, k.ln_eps)
                    modulate(nc, act, s, n, slot, hps, h_t, k.mod_t, 0, b, s["a_psum"])
                    act.wait_ge(s["a_psum"], at(n + 1))
                    nc.scalar.activation(sq[:, 0, :], aps[:, slot, 0:QA], ACT.Square, accum_out=ss[:, slot, 0:1]).then_inc(s["ss_done"], 1)
                    nc.scalar.activation(sq[:, 1, 0:LAT], aps[:, slot, QA:QA + LAT], ACT.Square, accum_out=ss[:, slot, 1:2]).then_inc(s["ss_done"], 1)
                    act.wait_ge(s["ms_done"], at(2 * n + 2))
                    nc.scalar.activation(rr[:, slot, 2:4], rr[:, slot, 0:2], ACT.Sqrt).then_inc(s["rms_done"], 1)
                    act.wait_ge(s["lat_t_psum"], at(n + 1))
                    nc.scalar.activation(k.qa_t[:, bass.ds(n0 * P, P)], tps[:, slot, 0:P], ACT.Copy).then_inc(s["qat_done"], 1)
                in_pairs(act, 0, TILES, tile)

            @block.vector
            def _(dve):
                def tile(n0, slot, turn):
                    n = n0 + b * TILES
                    dve.wait_ge(x_sem[slot], turn * 16 + 16)
                    norm_vector(nc, dve, s, n, slot, xt[:, slot, :], st, mv, xn)
                    dve.wait_ge(s["ss_done"], at(2 * n + 2))
                    nc.vector.tensor_scalar(rr[:, slot, 0:1], ss[:, slot, 0:1], 1.0 / QA, RMS_EPS, ALU.mult, ALU.add).then_inc(s["ms_done"], 1)
                    nc.vector.tensor_scalar(rr[:, slot, 1:2], ss[:, slot, 1:2], 1.0 / LAT, RMS_EPS, ALU.mult, ALU.add).then_inc(s["ms_done"], 1)
                    dve.wait_ge(s["k_done"], at(2 * n))
                    x1, x2 = aps[:, slot, X1:X1 + RH], aps[:, slot, X2:X2 + RH]
                    cs, sn = k.cos_n[:, bass.ds(n0, 1), :].rearrange("p a n -> p (a n)"), k.sin_n[:, bass.ds(n0, 1), :].rearrange("p a n -> p (a n)")
                    for m, (a, c) in enumerate(((x1, cs), (x2, sn), (x2, cs), (x1, sn))):
                        nc.vector.tensor_tensor(tm[:, slot, m, :], a, c, ALU.mult).then_inc(s["ropes_done"], 1)
                    dve.wait_ge(s["ropes_done"], at(4 * n + 4))
                    dve.wait_ge(s["lat_t_psum"], at(n - 1))
                    nc.vector.tensor_tensor(kk[:, slot, LAT:LAT + RH], tm[:, slot, 0, :], tm[:, slot, 1, :], ALU.subtract).then_inc(s["k_done"], 1)
                    nc.vector.tensor_tensor(kk[:, slot, LAT + RH:KR], tm[:, slot, 2, :], tm[:, slot, 3, :], ALU.add).then_inc(s["k_done"], 1)
                    dve.wait_ge(s["rms_done"], at(n + 1))
                    nc.vector.reciprocal(rr[:, slot, 0:2], rr[:, slot, 2:4]).then_inc(s["rr_done"], 1)
                    dve.wait_ge(s["rr_done"], at(n + 1))
                    c_raw = aps[:, slot, QA:QA + LAT]
                    for dst in (kk[:, slot, 0:LAT], k.cn[:, bass.ds(n0, 1), :].rearrange("p a n -> p (a n)")):
                        nc.vector.scalar_tensor_tensor(out=dst, in0=c_raw, scalar=rr[:, slot, 1:2], in1=k.kv_ln[:],
                                                       op0=ALU.mult, op1=ALU.mult).then_inc(s["cn_done"], 1)
                    nc.vector.tensor_scalar(qa[:, slot, :], aps[:, slot, 0:QA], rr[:, slot, 0:1], None, ALU.mult).then_inc(s["qa_done"], 1)
                    dve.wait_ge(s["lat_t_psum"], at(n + 1))
                    dve.wait_ge(s["qat_done"], at(n + 1))
                    kt = tps[0:KR, slot, P:2 * P]
                    nc.vector.tensor_copy(k.khi[0:KR, bass.ds(n0 * P, P)], kt).then_inc(s["khi_done"], 1)
                    dve.wait_ge(s["khi_done"], at(n + 1))
                    nc.vector.tensor_tensor(k.klo[0:KR, bass.ds(n0 * P, P)], kt, k.khi[0:KR, bass.ds(n0 * P, P)].bitcast(F32),
                                            ALU.subtract).then_inc(s["klo_done"], 1)
                in_pairs(dve, 0, TILES, tile)
        clear(nc, own)


UNITS = G * (4 + 8)
QUADS = UNITS // G
RING = 12
BANKS = 3
QK = [(qc, kt) for qc in range(2) for kt in range(4 * qc + 4)]
MU = [(j, qt, part) for j in range(G) for qt in range(TILES) for part in range(1 + qt // 4)]
M_AT = {2: 6, 3: 6, 4: 6, 5: 6, 6: 6, 7: 6, 8: 6, 9: 6}
P_AT = {4: (0,), 5: (1,), 6: (2,), 7: (3,), 8: (4,), 9: (5,)}
PJ = 6

ATT0 = ("q_in0 q_in1 lo_in0 lo_in1 m_in0 m_in1 wq_in0 wq_in1 "
        "passed sc_ready exp_done pv_done o_copied d_copied rd_done out_done mx_ready mx_done mx_joined "
        "mt_ready mrow_done pj_ready terms_done rot_done qhi_done qlo_done lat_hi lat_lo")


def steps(eng, step):
    step(-2, 0, -1, False, False, True)
    step(-1, 1, -1, False, True, True)
    in_pairs(eng, 0, NG - 2, lambda t, slot, turn: step(t, slot, turn, True, True, True))
    step(NG - 2, 0, NG // 2 - 1, True, True, False)
    step(NG - 1, 1, NG // 2 - 1, True, False, False)


def work(n, max_at, scores, maxima, queries):
    lo = sum(max_at.get(i, 0) for i in range(n))
    units = [("max", u, *MU[u]) for u in range(lo, lo + max_at.get(n, 0))] if maxima else []
    pieces = [("queries", u) for u in queries]
    for j in range(G):
        if scores and n < QUADS:
            pieces.append(("score", j))
        pieces += units[:2 if j == 0 else 1]
        units = units[2 if j == 0 else 1:]
    for bank in range(2):
        if scores and n >= 2:
            pieces.append(("values", bank))
        pieces += units[:1]
        units = units[1:]
    return pieces + units


def attention0(nc, s, k, b, wq_dram):
    with ExitStack() as ctx:
        nm = f"at{b}_"
        sb = lambda n, sh, d=F32: ctx.enter_context(nc.sbuf_tensor(nm + n, sh, d))
        ps = lambda n, sh: ctx.enter_context(nc.psum_tensor(nm + n, sh, F32))
        qhi = [sb(f"qhi{i}", [KR + 1, G, S], F32R) for i in range(2)]
        qlo = [sb(f"qlo{i}", [KR, G, S], F32R) for i in range(2)]
        shi, slo = sb("shi", [P, 3, S], F32R), sb("slo", [P, 3, S], F32R)
        tm = sb("tm", [P, 4, HALF])
        wq = sb("wq", [QA, 2, 3, P])
        prob = sb("prob", [P, RING, HALF])
        junk = sb("junk", [P, 2, HALF])
        mxd, mxf = sb("mxd", [P, G, TILES]), sb("mxf", [P, G, TILES // 2])
        mrow = sb("mrow", [G * TILES, P], F32R)
        o_sb, d_sb = sb("o_sb", [P, HALF]), sb("d_sb", [P, HALF])
        scp = [ps(f"scp{i}", [P, HALF]) for i in range(BANKS)]
        mxp = [ps(f"mxp{i}", [P, HALF]) for i in range(2)]
        op, dp, pj = ps("op", [P, HALF]), ps("dp", [P, HALF]), ps("pj", [P, HALF])
        q_in, lo_in, m_in, wq_in = (s["q_in0"], s["q_in1"]), (s["lo_in0"], s["lo_in1"]), (s["m_in0"], s["m_in1"]), (s["wq_in0"], s["wq_in1"])
        g0 = b * NG
        MOVES = 16 * 3 * G

        def moved(slot, turn):
            return 1 - slot, MOVES * (turn + b * NG // 2 + slot + 1)

        with nc.Block() as block:
            @block.sync
            def _(sp):
                def step(t, slot, turn, scores, maxima, project):
                    if project:
                        sp.wait_ge(s["pj_ready"], at(PJ * (t + g0 + 1)))
                        sp.dma_start(wq[:, slot, :, :].rearrange("p a n -> p (a n)"),
                                     wq_dram[bass.ds(t + 2, 1)].rearrange("g p n -> p (g n)")).then_inc(wq_in[slot], 16)
                    if maxima:
                        o, t = 1 - slot, t + g0
                        sp.wait_ge(s["sc_ready"], at(t * UNITS))
                        sp.wait_ge(s["lat_hi"], at(2 * t + 4))
                        sp.wait_ge(s["qhi_done"], at(4 * t + 8))
                        for j in range(G):
                            for blk in range(3):
                                sp.dma_start(words(qhi[o][LAT * blk:LAT * (blk + 1), j, :]), words(shi[LAT * j:LAT * (j + 1), blk, :])).then_inc(q_in[o], 16)
                        sp.wait_ge(s["lat_lo"], at(2 * t + 4))
                        sp.wait_ge(s["qlo_done"], at(4 * t + 8))
                        for j in range(G):
                            for blk in range(3):
                                sp.dma_start(words(qlo[o][LAT * blk:LAT * (blk + 1), j, :]), words(slo[LAT * j:LAT * (j + 1), blk, :])).then_inc(lo_in[o], 16)
                        sp.wait_ge(s["mrow_done"], at(t + 2))
                        sp.dma_start(words(qhi[o][MR:MR + 1, :, :]), words(mrow[:])).then_inc(m_in[o], 16)
                steps(sp, step)

            @block.gpsimd
            def _(pool):
                def rotate(t, hf, slot, turn, maxima):
                    n = 2 * t + hf
                    cols = slice(HALF * hf, HALF * (hf + 1))
                    pool.wait_ge(s["terms_done"], at(4 * n + 4))
                    nc.gpsimd.tensor_tensor(tm[:, 0, :], tm[:, 0, :], tm[:, 2, :], ALU.subtract).then_inc(s["rot_done"], 1)
                    nc.gpsimd.tensor_tensor(tm[:, 1, :], tm[:, 1, :], tm[:, 3, :], ALU.add).then_inc(s["rot_done"], 1)
                    if maxima:
                        o, count = moved(slot, turn)
                        pool.wait_ge(lo_in[o], count)
                    pool.wait_ge(s["qhi_done"], at(2 * n + 2))
                    for m in range(2):
                        nc.gpsimd.tensor_tensor(slo[:, 1 + m, cols], tm[:, m, :], shi[:, 1 + m, cols].bitcast(F32),
                                                ALU.subtract).then_inc(s["qlo_done"], 1)

                def step(t, slot, turn, scores, maxima, project):
                    t = t + g0
                    for n in range(QUADS):
                        for u in P_AT.get(n, ()) if project else ():
                            if u % 3 == 2:
                                rotate(t + 2, u // 3, slot, turn, maxima)
                steps(pool, step)

            @block.scalar
            def _(act):
                def copy_out(t, hf):
                    act.wait_ge(s["pv_done"], at(t * QUADS + (12 if hf else 4)))
                    act.wait_ge(s["out_done"], at(2 * t + hf))
                    nc.scalar.activation(d_sb[:], dp[:], ACT.Copy).then_inc(s["d_copied"], 1)
                    nc.scalar.activation(o_sb[:], op[:], ACT.Copy).then_inc(s["o_copied"], 1)

                def step(t, slot, turn, scores, maxima, project):
                    t = t + g0
                    for n in range(QUADS):
                        qc, kt = QK[n]
                        if maxima and n == QUADS - 1:
                            act.wait_ge(s["mt_ready"], at(t + 2))
                            if scores:
                                act.wait_ge(m_in[slot], 16 * (turn + b * NG // 2 + 1))
                            nc.scalar.activation(mrow[:], pj[0:G * TILES, 0:P], ACT.Copy, scale=-1.0).then_inc(s["mrow_done"], 1)
                        if scores:
                            act.wait_ge(s["pv_done"], at(t * QUADS + n - 2))
                            for u in range(G * n, G * n + G):
                                c0 = max(kt - 4 * qc, 0) * P
                                act.wait_ge(s["sc_ready"], at(t * UNITS + u + 1))
                                nc.scalar.activation(prob[:, u % RING, c0:HALF], scp[u % BANKS][:, c0:HALF], ACT.Exp).then_inc(s["exp_done"], 1)
                        for u in P_AT.get(n - 1, ()) if project else ():
                            if u % 3 == 2:
                                m = 2 * (t + 2) + u // 3
                                act.wait_ge(s["rot_done"], at(2 * m + 2))
                                if maxima:
                                    o, count = moved(slot, turn)
                                    act.wait_ge(q_in[o], count)
                                for r in range(2):
                                    nc.scalar.activation(shi[:, 1 + r, HALF * (u // 3):HALF * (u // 3 + 1)], tm[:, r, :], ACT.Copy).then_inc(s["qhi_done"], 1)
                        if scores and n == 5:
                            copy_out(t, 0)
                    if scores:
                        copy_out(t, 1)
                steps(act, step)

            @block.vector
            def _(dve):
                def maximum(t, u, j, qt, part):
                    w = (qt % 4 + 1) * P
                    if u == 0:
                        dve.wait_ge(s["mt_ready"], at(t))
                    dve.wait_ge(s["mx_ready"], at(t * UNITS + u + 1))
                    if qt >= 4 and part == 0:
                        nc.vector.reduce_max(mxf[:, j, qt - 4:qt - 3], mxp[u % 2][:], AX_X).then_inc(s["mx_done"], 1)
                    else:
                        dve.wait_ge(s["mx_done"], at(t * UNITS + u - 1))
                        apart(dve, s["passed"])
                        nc.vector.tensor_tensor_reduce(out=junk[:, u % 2, 0:w], in0=mxp[u % 2][:, 0:w], in1=k.causal[:, HALF - w:HALF],
                                                       scale=1.0, scalar=LOWEST, op0=ALU.add, op1=ALU.max,
                                                       accum_out=mxd[:, j, qt:qt + 1]).then_inc(s["mx_done"], 1)

                def projected(t, u, slot, turn, maxima):
                    hf, part = u // 3, u % 3
                    n = 2 * t + hf
                    cols = slice(HALF * hf, HALF * (hf + 1))
                    dve.wait_ge(s["pj_ready"], at(PJ * t + u + 1))
                    if part == 0:
                        if maxima:
                            o, count = moved(slot, turn)
                            dve.wait_ge(q_in[o], count)
                            dve.wait_ge(lo_in[o], count)
                        nc.vector.tensor_copy(shi[:, 0, cols], pj[:]).then_inc(s["lat_hi"], 1)
                        dve.wait_ge(s["lat_hi"], at(n + 1))
                        nc.vector.tensor_tensor(slo[:, 0, cols], pj[:], shi[:, 0, cols].bitcast(F32), ALU.subtract).then_inc(s["lat_lo"], 1)
                    else:
                        if part == 1:
                            dve.wait_ge(s["qlo_done"], at(2 * n))
                        for place, tab in ((0, k.cos_t), (3, k.sin_t)) if part == 1 else ((2, k.sin_t), (1, k.cos_t)):
                            nc.vector.tensor_tensor(tm[:, place, :], pj[:], tab[:, cols], ALU.mult).then_inc(s["terms_done"], 1)

                def finish(t, hf):
                    m = 2 * (t + g0) + hf
                    dve.wait_ge(s["d_copied"], at(m + 1))
                    nc.vector.reciprocal(d_sb[:], d_sb[:]).then_inc(s["rd_done"], 1)
                    dve.wait_ge(s["rd_done"], at(m + 1))
                    dve.wait_ge(s["o_copied"], at(m + 1))
                    nc.vector.tensor_tensor(k.o_t[:, bass.ds(t, 1), HALF * hf:HALF * (hf + 1)].rearrange("p a n -> p (a n)"),
                                            o_sb[:], d_sb[:], ALU.mult).then_inc(s["out_done"], 1)

                def step(t, slot, turn, scores, maxima, project):
                    for n in range(QUADS):
                        for kind, *piece in work(n, M_AT, scores, maxima, P_AT.get(n, ()) if project else ()):
                            if kind == "queries":
                                projected(t + g0 + 2, piece[0], slot, turn, maxima)
                            if kind == "max":
                                maximum(t + g0 + 1, *piece)
                        if maxima and n == max(M_AT):
                            dve.wait_ge(s["mx_done"], at((t + g0 + 2) * UNITS))
                            nc.vector.tensor_tensor(mxd[:, :, TILES // 2:TILES], mxd[:, :, TILES // 2:TILES], mxf[:], ALU.max).then_inc(s["mx_joined"], 1)
                        if scores and n == 10:
                            finish(t, 0)
                    if scores:
                        finish(t, 1)
                steps(dve, step)

            @block.tensor
            def _(pe):
                def score(t, slot, n, j):
                    qc, kt = QK[n]
                    u = G * n + j
                    c0 = min(max(kt - 4 * qc, 0) * P, HALF - 2 * P)
                    cols = slice(HALF * qc + c0, HALF * (qc + 1))
                    ks = slice(kt * P, (kt + 1) * P)
                    out = scp[u % BANKS][:, c0:HALF]
                    pe.wait_ge(s["exp_done"], at(t * UNITS + u + 1 - BANKS))
                    nc.tensor.matmul(out, k.khi[0:KR + 1, ks], qhi[slot][0:KR + 1, j, cols], start=True, stop=False)
                    if kt >= 4 * qc:
                        first = P if kt % 4 < 3 else 0
                        nc.tensor.matmul(out[:, 0:2 * P], k.ident_r[:], k.after_r[:, first:first + 2 * P], start=False, stop=False)
                    nc.tensor.matmul(out, k.khi[0:KR, ks], qlo[slot][0:KR, j, cols], start=False, stop=False)
                    nc.tensor.matmul(out, k.klo[0:KR, ks], qhi[slot][0:KR, j, cols], start=False, stop=True).then_inc(s["sc_ready"], 1)

                def maximum(t, slot, u, j, qt, part):
                    k0 = HALF if qt >= 4 and part == 1 else 0
                    w = HALF if qt >= 4 and part == 0 else max((qt % 4 + 1) * P, 2 * P)
                    pe.wait_ge(s["mx_done"], at(t * UNITS + u - 1))
                    nc.tensor.matmul(mxp[u % 2][:, 0:w], qhi[slot][0:KR, j, qt * P:(qt + 1) * P], k.khi[0:KR, k0:k0 + w],
                                     start=True, stop=True).then_inc(s["mx_ready"], 1)

                def values(t, n, part):
                    qc, kt = QK[n]
                    c0 = max(kt - 4 * qc, 0) * P
                    bank, left = ((op, k.cn[:, kt, :]), (dp, k.ones[:]))[part]
                    pe.wait_ge(s["exp_done"], at(t * UNITS + G * n + G))
                    if kt == 0:
                        pe.wait_ge((s["o_copied"], s["d_copied"])[part], at(2 * t + qc))
                    for j in range(G):
                        mm = nc.tensor.matmul(bank[LAT * j:LAT * (j + 1), c0:HALF], left, prob[:, (G * n + j) % RING, c0:HALF],
                                              start=(kt == 0), stop=(kt == 4 * qc + 3))
                    if part == 1:
                        mm.then_inc(s["pv_done"], 1)

                def project_q(t, slot, turn, u):
                    hf, part = u // 3, u % 3
                    pe.wait_ge(s["mrow_done"], at(t - 1))
                    if part == 1:
                        pe.wait_ge(s["lat_lo"], at(2 * t + hf + 1))
                    else:
                        pe.wait_ge(s["terms_done"], at(4 * (2 * t + hf) + (2 if part else 0)))
                    if u == 0:
                        pe.wait_ge(wq_in[slot], 16 * (turn + b * NG // 2 + 2))
                    nc.tensor.matmul(pj[:], wq[:, slot, part, :], k.qa_t[:, HALF * hf:HALF * (hf + 1)], start=True, stop=True).then_inc(s["pj_ready"], 1)

                def step(t, slot, turn, scores, maxima, project):
                    t = t + g0
                    for n in range(QUADS + 2):
                        if maxima and n == QUADS - 1:
                            pe.wait_ge(s["mx_joined"], at(t + 2))
                            pe.wait_ge(s["terms_done"], at(8 * (t + (3 if project else 2))))
                            nc.tensor.transpose(pj[0:G * TILES, 0:P], mxd[:].rearrange("p j q -> p (j q)"), k.ident[:]).then_inc(s["mt_ready"], 1)
                        if scores and n == 0:
                            pe.wait_ge(q_in[slot], MOVES * (turn + b * NG // 2 + 1))
                            pe.wait_ge(lo_in[slot], MOVES * (turn + b * NG // 2 + 1))
                            pe.wait_ge(m_in[slot], 16 * (turn + b * NG // 2 + 1))
                        for kind, *piece in work(n, M_AT, scores, maxima, P_AT.get(n, ()) if project else ()):
                            if kind == "queries":
                                project_q(t + 2, slot, turn, piece[0])
                            if kind == "score":
                                score(t, slot, n, piece[0])
                            if kind == "max":
                                if piece[0] == 0:
                                    o, count = moved(slot, turn)
                                    pe.wait_ge(q_in[o], count)
                                maximum(t + 1, 1 - slot, *piece)
                            if kind == "values":
                                values(t, n - 2, piece[0])
                steps(pe, step)


OUT_SEMS = " y_psum gated x1_done f_psum biased gated2 x2_done x2_out"
FF0 = (NORM_SEMS + OUT_SEMS + " l_psum z_done zs_done cum_done kz_done sup_done kn_done sel_done ts_done rk_done tau_done "
       "ew_done lw_done lt_psum lt_done")


def feed0(nc, s, k, b, x_in, wout_dram, t, x_out):
    with ExitStack() as ctx:
        nm = f"ff{b}_"
        sb = lambda n, sh, d=F32: ctx.enter_context(nc.sbuf_tensor(nm + n, sh, d))
        ps = lambda n, sh: ctx.enter_context(nc.psum_tensor(nm + n, sh, F32))
        own = semaphores(ctx, nc, nm, "w_in x_in0 x_in1 o_in0 o_in1 x_out0 x_out1")
        w_in, x_sem, o_sem, st_sem = own["w_in"], (own["x_in0"], own["x_in1"]), (own["o_in0"], own["o_in1"]), (own["x_out0"], own["x_out1"])
        wo = sb("wo", [P, NG, D])
        wb, wl, lb = sb("wb", [P, C, D]), sb("wl", [P, C, P + E]), sb("lb", [P, D])
        bias, rbias = sb("bias", [P, D]), sb("rbias", [P, E])
        ot = sb("ot", [P, 2, NG, P])
        xt, x1, xn = sb("xt", [P, 2, D]), sb("x1", [P, 2, D]), sb("xn", [P, 2, D])
        fo = sb("fo", [P, 2, D])
        st, mv = sb("st", [P, 2, 6]), sb("mv", [P, 2, 4])
        h_t = sb("h_t", [P, 2, C, P])
        r = sb("r", [P, 2, 8, E])
        rc = sb("rc", [P, 2, 4])
        low, low_t = sb("low", [P, 2, P]), sb("low_t", [P, 2, P])
        yps = ps("yps", [P, 2, D])
        hps, lps, tps = ps("hps", [P, C, P]), ps("lps", [P, 512]), ps("tps", [P, 512])
        fps = ps("fps", [P, 2, D])
        with nc.Block() as block:
            @block.sync
            def _(sp):
                for sem in st_sem:
                    sp.sem_inc(sem, 16)
                sp.dma_start(wo[:], wout_dram.rearrange("g p n -> p g n")).then_inc(w_in, 16)
                for dst, name in ((wb, "w_base0"), (wl, "w_low0")):
                    sp.dma_start(dst[:], t[name].rearrange("(k p) n -> p k n", p=P)).then_inc(w_in, 16)
                for dst, name in ((lb, "lora_b"), (bias, "b_base0"), (rbias, "b_router")):
                    sp.dma_start(dst[:], t[name]).then_inc(w_in, 16)

                def load(n0, slot, turn):
                    n = n0 + b * TILES
                    sp.wait_ge(s["y_psum"], at(n - 1))
                    sp.dma_start(ot[:, slot, :, :], k.o_t[:, :, bass.ds(n0 * P, P)]).then_inc(o_sem[slot], 16)
                    sp.wait_ge(s["x1_done"], at(n - 1))
                    sp.dma_start(xt[:, slot, :], x_in[bass.ds(n * P, P), :]).then_inc(x_sem[slot], 16)

                def store(n0, slot):
                    n = n0 + b * TILES
                    sp.wait_ge(s["x2_done"], at(n + 1))
                    sp.dma_start(x_out[bass.ds(n * P, P), :], fo[:, slot, :]).then_inc(st_sem[slot], 16)

                def load_store(n0, slot, turn):
                    load(n0, slot, turn)
                    store(n0 - 2, slot)
                for n0 in range(2):
                    load(n0, n0, 0)
                in_pairs(sp, 2, TILES, load_store)
                for n0 in range(TILES - 2, TILES):
                    store(n0, n0 % 2)
                for sem in st_sem:
                    sp.wait_ge(sem, 16 * TILES // 2 + 16)

            @block.tensor
            def _(pe):
                def project(n0, slot, turn):
                    n = n0 + b * TILES
                    pe.wait_ge(o_sem[slot], turn * 16 + 16)
                    pe.wait_ge(s["gated"], at(n - 1))
                    for g in range(NG):
                        mm = nc.tensor.matmul(yps[:, slot, :], ot[:, slot, g, :], wo[:, g, :], start=(g == 0), stop=(g == NG - 1))
                    mm.then_inc(s["y_psum"], 1)

                def feed(n0, slot, turn):
                    n = n0 + b * TILES
                    norm_tensor(nc, pe, s, n, slot, xn, k.ident, hps)
                    pe.wait_ge(s["h_done"], at(C * n + C))
                    pe.wait_ge(s["z_done"], at(n))
                    pe.wait_ge(s["lw_done"], at(n))
                    for c in range(C):
                        mm = nc.tensor.matmul(lps[:, 0:P + E], h_t[:, slot, c, :], wl[:, c, :], start=(c == 0), stop=(c == C - 1))
                    mm.then_inc(s["l_psum"], 1)
                    pe.wait_ge(s["biased"], at(n - 1))
                    for c in range(C):
                        nc.tensor.matmul(fps[:, slot, :], h_t[:, slot, c, :], wb[:, c, :], start=(c == 0), stop=False)
                    pe.wait_ge(s["lw_done"], at(n + 1))
                    pe.wait_ge(s["lt_done"], at(n))
                    nc.tensor.transpose(tps[:, 0:P], low[:, slot, :], k.ident[:]).then_inc(s["lt_psum"], 1)
                    pe.wait_ge(s["lt_done"], at(n + 1))
                    nc.tensor.matmul(fps[:, slot, :], low_t[:, slot, :], lb[:], start=False, stop=True).then_inc(s["f_psum"], 1)

                def both(n0, slot, turn):
                    project(n0 + 1, 1 - slot, turn + slot)
                    feed(n0, slot, turn)
                pe.wait_ge(w_in, 16 * 6)
                project(0, 0, 0)
                in_pairs(pe, 0, TILES - 2, both)
                both(TILES - 2, 0, TILES // 2 - 1)
                feed(TILES - 1, 1, TILES // 2 - 1)

            @block.scalar
            def _(act):
                def tile(n0, slot, turn):
                    n = n0 + b * TILES
                    norm_scalar(nc, act, s, n, slot, mv, k.ln_eps)
                    modulate(nc, act, s, n, slot, hps, h_t, k.mod_t, 2, b, s["f_psum"])
                    act.wait_ge(s["lt_psum"], at(n + 1))
                    nc.scalar.activation(low_t[:, slot, :], tps[:, 0:P], ACT.Copy).then_inc(s["lt_done"], 1)
                in_pairs(act, 0, TILES, tile)

            @block.vector
            def _(dve):
                def experts(n, slot):
                    z, zs, cum, kz, sup, sel, ew = (r[:, slot, i, :] for i in range(7))
                    kn, ts, rk, tau = (rc[:, slot, i:i + 1] for i in range(4))
                    dve.wait_ge(s["l_psum"], at(n + 1))
                    nc.vector.tensor_tensor(z, lps[:, P:P + E], rbias[:], ALU.add).then_inc(s["z_done"], 1)
                    dve.wait_ge(s["z_done"], at(n + 1))
                    apart(dve, s["passed"])
                    nc.vector.max(zs, z).then_inc(s["zs_done"], 1)
                    dve.wait_ge(s["zs_done"], at(n + 1))
                    nc.vector.tensor_tensor_scan(cum, zs, k.zeros[:, 0:E], 0.0, ALU.add, ALU.add).then_inc(s["cum_done"], 1)
                    nc.vector.tensor_tensor(kz, zs, k.count[:], ALU.mult).then_inc(s["kz_done"], 1)
                    dve.wait_ge(s["cum_done"], at(n + 1))
                    dve.wait_ge(s["kz_done"], at(n + 1))
                    nc.vector.scalar_tensor_tensor(out=sup, in0=kz, scalar=1.0, in1=cum, op0=ALU.add, op1=ALU.is_gt).then_inc(s["sup_done"], 1)
                    dve.wait_ge(s["sup_done"], at(n + 1))
                    nc.vector.reduce_sum(kn, sup, AX_X).then_inc(s["kn_done"], 1)
                    dve.wait_ge(s["kn_done"], at(n + 1))
                    nc.vector.reciprocal(rk, kn).then_inc(s["rk_done"], 1)
                    nc.vector.scalar_tensor_tensor(out=sel, in0=k.count[:], scalar=kn, in1=cum, op0=ALU.is_equal, op1=ALU.mult).then_inc(s["sel_done"], 1)
                    dve.wait_ge(s["sel_done"], at(n + 1))
                    nc.vector.reduce_sum(ts, sel, AX_X).then_inc(s["ts_done"], 1)
                    dve.wait_ge(s["ts_done"], at(n + 1))
                    dve.wait_ge(s["rk_done"], at(n + 1))
                    nc.vector.tensor_scalar(tau, ts, -1.0, rk, ALU.add, ALU.mult).then_inc(s["tau_done"], 1)
                    dve.wait_ge(s["tau_done"], at(n + 1))
                    nc.vector.tensor_scalar(ew, z, tau, 0.0, ALU.subtract, ALU.max).then_inc(s["ew_done"], 1)
                    dve.wait_ge(s["ew_done"], at(n + 1))
                    dve.wait_ge(s["lt_psum"], at(n - 1))
                    nc.vector.tensor_tensor(low[:, slot, :].rearrange("p (e r) -> p e r", r=R), lps[:, 0:P].rearrange("p (e r) -> p e r", r=R),
                                            ew.unsqueeze(2).to_broadcast([P, E, R]), ALU.mult).then_inc(s["lw_done"], 1)

                def tile(n0, slot, turn):
                    n = n0 + b * TILES
                    x1s, fos = x1[:, slot, :], fo[:, slot, :]
                    dve.wait_ge(s["y_psum"], at(n + 1))
                    nc.vector.tensor_tensor(x1s, yps[:, slot, :], k.gates[:, 0, b, :], ALU.mult).then_inc(s["gated"], 1)
                    dve.wait_ge(s["gated"], at(n + 1))
                    dve.wait_ge(x_sem[slot], turn * 16 + 16)
                    nc.vector.tensor_tensor(x1s, x1s, xt[:, slot, :], ALU.add).then_inc(s["x1_done"], 1)
                    dve.wait_ge(s["x1_done"], at(n + 1))
                    norm_vector(nc, dve, s, n, slot, x1s, st, mv, xn)
                    experts(n, slot)
                    dve.wait_ge(s["f_psum"], at(n + 1))
                    dve.wait_ge(st_sem[slot], turn * 16 + 16)
                    nc.vector.tensor_tensor(fos, fps[:, slot, :], bias[:], ALU.add).then_inc(s["biased"], 1)
                    dve.wait_ge(s["biased"], at(n + 1))
                    nc.vector.tensor_tensor(fos, fos, k.gates[:, 1, b, :], ALU.mult).then_inc(s["gated2"], 1)
                    dve.wait_ge(s["gated2"], at(n + 1))
                    nc.vector.tensor_tensor(fos, fos, x1s, ALU.add).then_inc(s["x2_done"], 1)
                dve.wait_ge(w_in, 16 * 6)
                in_pairs(dve, 0, TILES, tile)
        clear(nc, own)


def join_feed1(nc, t, w_dram):
    with ExitStack() as ctx:
        sb = lambda n, sh, d=F32: ctx.enter_context(nc.sbuf_tensor("jf_" + n, sh, d))
        s = semaphores(ctx, nc, "jf_", "in_done mask_done w_done sum_done g_psum g_done d_psum d_done w_out")
        co, mw, mf = sb("co", [P, E1, C, LOW]), sb("mw", [P, E1, C, LOW // 4], I32), sb("mf", [P, E1, C, LOW])
        fo, wb, wj = sb("fo", [P, C, D]), sb("wb", [P, C, D]), sb("wj", [P, C, D])
        enc, gs = sb("enc", [LOW, D]), sb("gs", [LOW, D])
        gps = ctx.enter_context(nc.psum_tensor("jf_gps", [LOW, D], F32))
        dps = ctx.enter_context(nc.psum_tensor("jf_dps", [P, C, D], F32))
        with nc.Block() as block:
            @block.sync
            def _(sp):
                for dst, src in ((co, t["coefs"]), (mw, t["masks"]), (enc, t["enc"]), (fo, t["fourier"].rearrange("(k p) n -> p k n", p=P)),
                                 (wb, t["w_base1"].rearrange("(k p) n -> p k n", p=P))):
                    sp.dma_start(dst[:], src).then_inc(s["in_done"], 16)
                sp.wait_ge(s["d_done"], C)
                sp.dma_start(w_dram.rearrange("(k p) n -> p k n", p=P), wj[:]).then_inc(s["w_out"], 16)
                sp.wait_ge(s["w_out"], 16)

            @block.vector
            def _(dve):
                dve.wait_ge(s["in_done"], 80)
                nc.vector.tensor_copy(mf[:].rearrange("p e c r -> p (e c r)"), mw[:].rearrange("p e c r -> p (e c r)").bitcast(U8)).then_inc(s["mask_done"], 1)
                dve.wait_ge(s["mask_done"], 1)
                nc.vector.tensor_tensor(mf[:], mf[:], co[:], ALU.mult).then_inc(s["w_done"], 1)
                dve.wait_ge(s["w_done"], 1)
                for e in range(1, E1):
                    nc.vector.tensor_tensor(mf[:, 0], mf[:, 0], mf[:, e], ALU.add).then_inc(s["sum_done"], 1)
                    dve.wait_ge(s["sum_done"], e)
                dve.wait_ge(s["g_psum"], 1)
                nc.vector.tensor_copy(gs[:], gps[:]).then_inc(s["g_done"], 1)
                for c in range(C):
                    dve.wait_ge(s["d_psum"], c + 1)
                    nc.vector.scalar_tensor_tensor(out=wj[:, c, :], in0=dps[:, c, :], scalar=ADAPT, in1=wb[:, c, :],
                                                   op0=ALU.mult, op1=ALU.add).then_inc(s["d_done"], 1)

            @block.tensor
            def _(pe):
                pe.wait_ge(s["sum_done"], E1 - 1)
                for c in range(C):
                    mm = nc.tensor.matmul(gps[:], mf[:, 0, c, :], fo[:, c, :], start=(c == 0), stop=(c == C - 1))
                mm.then_inc(s["g_psum"], 1)
                pe.wait_ge(s["g_done"], 1)
                for c in range(C):
                    nc.tensor.matmul(dps[:, c, :], enc[:, c * P:(c + 1) * P], gs[:], start=True, stop=True).then_inc(s["d_psum"], 1)
        clear(nc, s)


IN1 = (NORM_SEMS + " q_psum v_psum qhi_done qlo_done kv_done k_t_psum khi_done klo_done v_done")


def queries1(nc, s, x_in, b, t, k):
    with ExitStack() as ctx:
        nm = f"qk{b}_"
        sb = lambda n, sh, d=F32: ctx.enter_context(nc.sbuf_tensor(nm + n, sh, d))
        ps = lambda n, sh: ctx.enter_context(nc.psum_tensor(nm + n, sh, F32))
        own = semaphores(ctx, nc, nm, "w_in keys_in x_in0 x_in1")
        w_in, keys_in, x_sem = own["w_in"], own["keys_in"], (own["x_in0"], own["x_in1"])
        wq, wkv = sb("wq", [P, C, D]), sb("wkv", [P, C, 2 * HD])
        xt, xn = sb("xt", [P, 2, D]), sb("xn", [P, 2, D])
        st, mv = sb("st", [P, 2, 6]), sb("mv", [P, 2, 4])
        h_t = sb("h_t", [P, 2, C, P])
        kv = sb("kv", [P, 2, HD])
        k_hi, k_lo = sb("k_hi", [HD, S], F32R), sb("k_lo", [HD, S], F32R)
        hps, qps, vps, tps = ps("hps", [P, C, P]), ps("qps", [P, 2, C, P]), ps("vps", [P, 2, 512]), ps("tps", [P, 512])
        with nc.Block() as block:
            @block.sync
            def _(sp):
                sp.dma_start(wq[:], t["wq1"].rearrange("(k p) n -> p k n", p=P)).then_inc(w_in, 16)
                sp.dma_start(wkv[:], t["wkv1"].rearrange("(k p) n -> p k n", p=P)).then_inc(w_in, 16)

                def load(n0, slot, turn):
                    n = n0 + b * TILES
                    sp.wait_ge(s["xn_done"], at(n - 1))
                    sp.dma_start(xt[:, slot, :], x_in[bass.ds(n * P, P), :]).then_inc(x_sem[slot], 16)
                in_pairs(sp, 0, TILES, load)
                sp.wait_ge(s["klo_done"], at((b + 1) * TILES))
                for blk in range(4):
                    sp.dma_start(words(k.keys[HD * blk:HD * (blk + 1), :]), words((k_hi, k_lo)[blk % 2][:])).then_inc(keys_in, 16)
                sp.wait_ge(keys_in, 64)

            @block.tensor
            def _(pe):
                pe.wait_ge(w_in, 32)

                def tile(n0, slot, turn):
                    n = n0 + b * TILES
                    norm_tensor(nc, pe, s, n, slot, xn, k.ident, hps)
                    pe.wait_ge(s["h_done"], at(C * n + C))
                    pe.wait_ge(s["kv_done"], at(n - 1))
                    pe.wait_ge(s["v_done"], at(n - 1))
                    for c in range(C):
                        mm = nc.tensor.matmul(vps[:, slot, 0:2 * HD], h_t[:, slot, c, :], wkv[:, c, :], start=(c == 0), stop=(c == C - 1))
                    mm.then_inc(s["v_psum"], 1)
                    pe.wait_ge(s["qlo_done"], at(n - 1))
                    for m in range(C):
                        for c in range(C):
                            mm = nc.tensor.matmul(qps[:, slot, m, :], wq[:, c, m * P:(m + 1) * P], h_t[:, slot, c, :], start=(c == 0), stop=(c == C - 1))
                    mm.then_inc(s["q_psum"], 1)
                    pe.wait_ge(s["kv_done"], at(n + 1))
                    pe.wait_ge(s["klo_done"], at(n))
                    nc.tensor.transpose(tps[0:HD, 0:P], kv[:, slot, :], k.ident[:]).then_inc(s["k_t_psum"], 1)
                in_pairs(pe, 0, TILES, tile)

            @block.scalar
            def _(act):
                def tile(n0, slot, turn):
                    n = n0 + b * TILES
                    norm_scalar(nc, act, s, n, slot, mv, k.ln_eps)
                    modulate(nc, act, s, n, slot, hps, h_t, k.mod_t, 0, b, s["q_psum"])
                    act.wait_ge(s["q_psum"], at(n + 1))
                    nc.scalar.activation(k.qp_hi[:, :, bass.ds(n0 * P, P)], qps[:, slot, :, :], ACT.Copy, scale=SCALE1).then_inc(s["qhi_done"], 1)
                in_pairs(act, 0, TILES, tile)

            @block.vector
            def _(dve):
                def tile(n0, slot, turn):
                    n = n0 + b * TILES
                    dve.wait_ge(x_sem[slot], turn * 16 + 16)
                    norm_vector(nc, dve, s, n, slot, xt[:, slot, :], st, mv, xn)
                    dve.wait_ge(s["v_psum"], at(n + 1))
                    dve.wait_ge(s["k_t_psum"], at(n - 1))
                    nc.vector.tensor_copy(kv[:, slot, :], vps[:, slot, 0:HD]).then_inc(s["kv_done"], 1)
                    nc.vector.tensor_copy(k.vn[:, bass.ds(n0, 1), 0:HD].rearrange("p a n -> p (a n)"), vps[:, slot, HD:2 * HD]).then_inc(s["v_done"], 1)
                    dve.wait_ge(s["qhi_done"], at(n + 1))
                    nc.vector.scalar_tensor_tensor(out=k.qp_lo[:, :, bass.ds(n0 * P, P)], in0=qps[:, slot, :, :], scalar=SCALE1,
                                                   in1=k.qp_hi[:, :, bass.ds(n0 * P, P)].bitcast(F32), op0=ALU.mult, op1=ALU.subtract).then_inc(s["qlo_done"], 1)
                    dve.wait_ge(s["k_t_psum"], at(n + 1))
                    kt = tps[0:HD, 0:P]
                    nc.vector.tensor_copy(k_hi[:, bass.ds(n0 * P, P)], kt).then_inc(s["khi_done"], 1)
                    dve.wait_ge(s["khi_done"], at(n + 1))
                    nc.vector.tensor_tensor(k_lo[:, bass.ds(n0 * P, P)], kt, k_hi[:, bass.ds(n0 * P, P)].bitcast(F32), ALU.subtract).then_inc(s["klo_done"], 1)
                in_pairs(dve, 0, TILES, tile)
        clear(nc, own)


M_AT1 = {1: 3, 2: 5, 3: 5, 4: 5, 5: 5, 6: 5, 7: 5, 8: 5, 9: 5, 10: 5}
ATT1 = ("q_in0 q_in1 m_in0 m_in1 "
        "passed sc_ready exp_done pv_done u_copied u_turned rd_done out_done mx_ready mx_done mx_joined mt_ready mrow_done")


def attention1(nc, s, k, b, q_dram):
    with ExitStack() as ctx:
        nm = f"as{b}_"
        sb = lambda n, sh, d=F32: ctx.enter_context(nc.sbuf_tensor(nm + n, sh, d))
        ps = lambda n, sh: ctx.enter_context(nc.psum_tensor(nm + n, sh, F32))
        q = k.q_slots
        own = semaphores(ctx, nc, nm, "q_out")
        q_out = own["q_out"]
        prob = sb("prob", [P, RING, HALF])
        junk = sb("junk", [P, 2, HALF])
        mxd, mxf = sb("mxd", [P, G, TILES]), sb("mxf", [P, G, TILES // 2])
        mrow = sb("mrow", [G * TILES, P], F32R)
        u_sb, rd = sb("u_sb", [P, HALF]), sb("rd", [P, 4, G, 1])
        scp = [ps(f"scp{i}", [P, HALF]) for i in range(BANKS)]
        mxp = [ps(f"mxp{i}", [P, HALF]) for i in range(2)]
        op, tp, mt = ps("op", [P, HALF]), ps("tp", [P, 4, G, 2 * HD]), ps("mt", [P, HALF])
        q_in, m_in = (s["q_in0"], s["q_in1"]), (s["m_in0"], s["m_in1"])
        g0 = b * NG
        MOVES = 16 * 4

        def steps(eng, step):
            step(-1, 1, -1, False, True)
            in_pairs(eng, 0, NG - 2, lambda t, slot, turn: step(t, slot, turn, True, True))
            step(NG - 2, 0, NG // 2 - 1, True, True)
            step(NG - 1, 1, NG // 2 - 1, True, False)

        with nc.Block() as block:
            @block.sync
            def _(sp):
                def spread(chunk):
                    for part, src in enumerate((k.qp_hi, k.qp_lo)):
                        sp.dma_start(q_dram[part, chunk], words(src[:, chunk, :])).then_inc(q_out, 16)
                    sp.wait_ge(q_out, 32 * (chunk + 1))

                def move(t, slot, turn, half):
                    for blk in range(4):
                        sp.dma_start(words(q[slot][HD * blk:HD * (blk + 1), :, :]),
                                     q_dram[blk // 2, bass.ds(turn, 1), HD * G * half:HD * G * (half + 1), :]
                                     .rearrange("c (j d) s -> d (c j) s", d=HD)).then_inc(q_in[slot], 16)

                def step(t, slot, turn, scores, maxima):
                    if maxima:
                        sp.wait_ge(s["sc_ready"], at((t + g0) * UNITS))
                        move(t + 1, 1 - slot, turn + slot, 1 - slot)
                        sp.wait_ge(s["mrow_done"], at(t + g0 + 2))
                        sp.dma_start(words(q[1 - slot][MR:MR + 1, :, :]), words(mrow[:])).then_inc(m_in[1 - slot], 16)
                for chunk in range(C):
                    spread(chunk)
                steps(sp, step)

            @block.scalar
            def _(act):
                def copy_out(t, hf):
                    act.wait_ge(s["pv_done"], at(t * QUADS + (12 if hf else 4)))
                    act.wait_ge(s["u_turned"], at(2 * t + hf))
                    nc.scalar.activation(u_sb[:], op[:], ACT.Copy).then_inc(s["u_copied"], 1)

                def step(t, slot, turn, scores, maxima):
                    t = t + g0
                    for n in range(QUADS):
                        qc, kt = QK[n]
                        if scores:
                            act.wait_ge(s["pv_done"], at(t * QUADS + n - 2))
                            for u in range(G * n, G * n + G):
                                c0 = max(kt - 4 * qc, 0) * P
                                act.wait_ge(s["sc_ready"], at(t * UNITS + u + 1))
                                nc.scalar.activation(prob[:, u % RING, c0:HALF], scp[u % BANKS][:, c0:HALF], ACT.Exp).then_inc(s["exp_done"], 1)
                        if scores and n == 5:
                            copy_out(t, 0)
                    if maxima:
                        act.wait_ge(s["mt_ready"], at(t + 2))
                        if scores:
                            act.wait_ge(m_in[slot], 16 * (turn + b * NG // 2 + 1))
                        nc.scalar.activation(mrow[:], mt[0:G * TILES, 0:P], ACT.Copy, scale=-1.0).then_inc(s["mrow_done"], 1)
                    if scores:
                        copy_out(t, 1)
                steps(act, step)

            @block.vector
            def _(dve):
                def maximum(t, u, j, qt, part):
                    w = (qt % 4 + 1) * P
                    if u == 0:
                        dve.wait_ge(s["mt_ready"], at(t))
                    dve.wait_ge(s["mx_ready"], at(t * UNITS + u + 1))
                    if qt >= 4 and part == 0:
                        nc.vector.reduce_max(mxf[:, j, qt - 4:qt - 3], mxp[u % 2][:], AX_X).then_inc(s["mx_done"], 1)
                    else:
                        dve.wait_ge(s["mx_done"], at(t * UNITS + u - 1))
                        apart(dve, s["passed"])
                        nc.vector.tensor_tensor_reduce(out=junk[:, u % 2, 0:w], in0=mxp[u % 2][:, 0:w], in1=k.causal[:, HALF - w:HALF],
                                                       scale=1.0, scalar=LOWEST, op0=ALU.add, op1=ALU.max,
                                                       accum_out=mxd[:, j, qt:qt + 1]).then_inc(s["mx_done"], 1)

                def finish(t, hf):
                    m = 2 * (t + g0) + hf
                    dve.wait_ge(s["u_turned"], at(m + 1))
                    dve.wait_ge(s["out_done"], at(m))
                    nc.vector.reciprocal(rd[:], tp[:, :, :, HD:HD + 1]).then_inc(s["rd_done"], 1)
                    dve.wait_ge(s["rd_done"], at(m + 1))
                    nc.vector.tensor_tensor(k.att[:, 4 * hf:4 * hf + 4, bass.ds(t * G * HD, G * HD)].rearrange("p q (j d) -> p q j d", j=G),
                                            tp[:, :, :, 0:HD], rd[:].to_broadcast([P, 4, G, HD]), ALU.mult).then_inc(s["out_done"], 1)

                def step(t, slot, turn, scores, maxima):
                    for n in range(QUADS):
                        for kind, *piece in work(n, M_AT1, scores, maxima, ()):
                            if kind == "max":
                                maximum(t + g0 + 1, *piece)
                        if scores and n == 7:
                            finish(t, 0)
                        if maxima and n == max(M_AT1):
                            dve.wait_ge(s["mx_done"], at((t + g0 + 2) * UNITS))
                            nc.vector.tensor_tensor(mxd[:, :, TILES // 2:TILES], mxd[:, :, TILES // 2:TILES], mxf[:], ALU.max).then_inc(s["mx_joined"], 1)
                    if scores:
                        finish(t, 1)
                steps(dve, step)

            @block.tensor
            def _(pe):
                def score(t, slot, n, j):
                    qc, kt = QK[n]
                    u = G * n + j
                    c0 = min(max(kt - 4 * qc, 0) * P, HALF - 2 * P)
                    diag = kt >= 4 * qc
                    out = scp[u % BANKS][:, c0:HALF]
                    pe.wait_ge(s["exp_done"], at(t * UNITS + u + 1 - BANKS))
                    mm = nc.tensor.matmul(out, k.keys[:, kt * P:(kt + 1) * P], q[slot][:, j, HALF * qc + c0:HALF * (qc + 1)], start=True, stop=not diag)
                    if diag:
                        first = P if kt % 4 < 3 else 0
                        mm = nc.tensor.matmul(out[:, 0:2 * P], k.ident_r[:], k.after_r[:, first:first + 2 * P], start=False, stop=True)
                    mm.then_inc(s["sc_ready"], 1)

                def maximum(t, slot, u, j, qt, part):
                    k0 = HALF if qt >= 4 and part == 1 else 0
                    w = HALF if qt >= 4 and part == 0 else max((qt % 4 + 1) * P, 2 * P)
                    pe.wait_ge(s["mx_done"], at(t * UNITS + u - 1))
                    nc.tensor.matmul(mxp[u % 2][:, 0:w], q[slot][0:KR, j, qt * P:(qt + 1) * P], k.keys[0:KR, k0:k0 + w],
                                     start=True, stop=True).then_inc(s["mx_ready"], 1)

                def values(t, n):
                    qc, kt = QK[n]
                    c0 = max(kt - 4 * qc, 0) * P
                    pe.wait_ge(s["exp_done"], at(t * UNITS + G * n + G))
                    if kt == 0:
                        pe.wait_ge(s["u_copied"], at(2 * t + qc))
                    for j in range(G):
                        mm = nc.tensor.matmul(op[2 * HD * j:2 * HD * (j + 1), c0:HALF], k.vn[:, kt, :], prob[:, (G * n + j) % RING, c0:HALF],
                                              start=(kt == 0), stop=(kt == 4 * qc + 3))
                    mm.then_inc(s["pv_done"], 1)

                def turn_out(t, hf):
                    pe.wait_ge(s["u_copied"], at(2 * t + hf + 1))
                    pe.wait_ge(s["out_done"], at(2 * t + hf))
                    for i in range(4):
                        tr = nc.tensor.transpose(tp[:, i, :, :].rearrange("p j d -> p (j d)"), u_sb[:, i * P:(i + 1) * P], k.ident[:])
                    tr.then_inc(s["u_turned"], 1)

                def turn_maxima(t):
                    pe.wait_ge(s["mx_joined"], at(t + 1))
                    pe.wait_ge(s["mrow_done"], at(t))
                    nc.tensor.transpose(mt[0:G * TILES, 0:P], mxd[:].rearrange("p j q -> p (j q)"), k.ident[:]).then_inc(s["mt_ready"], 1)

                def step(t, slot, turn, scores, maxima):
                    t, turn = t + g0, turn + b * NG // 2
                    for n in range(QUADS + 2):
                        if scores and n == 0:
                            pe.wait_ge(q_in[slot], MOVES * (turn + 1))
                            pe.wait_ge(m_in[slot], 16 * (turn + 1))
                        for kind, *piece in work(n, M_AT1, scores, maxima, ()):
                            if kind == "score":
                                score(t, slot, n, piece[0])
                            if kind == "max":
                                if piece[0] == 0:
                                    pe.wait_ge(q_in[1 - slot], MOVES * (turn + slot + 1))
                                maximum(t + 1, 1 - slot, *piece)
                            if kind == "values":
                                if piece[0] == 0 and n == QUADS - 1 and maxima:
                                    turn_maxima(t + 1)
                                if piece[0] == 0:
                                    values(t, n - 2)
                        if scores and n == 7:
                            turn_out(t, 0)
                    if maxima and not scores:
                        turn_maxima(t + 1)
                    if scores:
                        turn_out(t, 1)
                steps(pe, step)
        clear(nc, own)


FF1 = (NORM_SEMS + OUT_SEMS + " at_psum at_done")


def feed1(nc, s, k, b, x_in, w_dram, t, x_out):
    with ExitStack() as ctx:
        nm = f"fg{b}_"
        sb = lambda n, sh, d=F32: ctx.enter_context(nc.sbuf_tensor(nm + n, sh, d))
        ps = lambda n, sh: ctx.enter_context(nc.psum_tensor(nm + n, sh, F32))
        own = semaphores(ctx, nc, nm, "w_in x_in0 x_in1 a_in0 a_in1 x_out0 x_out1")
        w_in, x_sem, a_sem, st_sem = own["w_in"], (own["x_in0"], own["x_in1"]), (own["a_in0"], own["a_in1"]), (own["x_out0"], own["x_out1"])
        wo, wf, bias = sb("wo", [P, C, D]), sb("wf", [P, C, D]), sb("bias", [P, D])
        an, a_t = sb("an", [P, 2, D]), sb("a_t", [P, 2, C, P])
        xt, x1, xn = sb("xt", [P, 2, D]), sb("x1", [P, 2, D]), sb("xn", [P, 2, D])
        fo = sb("fo", [P, 2, D])
        st, mv = sb("st", [P, 2, 6]), sb("mv", [P, 2, 4])
        h_t = sb("h_t", [P, 2, C, P])
        yps, fps = ps("yps", [P, 2, D]), ps("fps", [P, 2, D])
        hps, aps = ps("hps", [P, C, P]), ps("aps", [P, C, P])
        with nc.Block() as block:
            @block.sync
            def _(sp):
                for sem in st_sem:
                    sp.sem_inc(sem, 16)
                sp.dma_start(wo[:], t["wo1"].rearrange("(k p) n -> p k n", p=P)).then_inc(w_in, 16)
                sp.dma_start(wf[:], w_dram.rearrange("(k p) n -> p k n", p=P)).then_inc(w_in, 16)
                sp.dma_start(bias[:], t["b_base1"]).then_inc(w_in, 16)

                def load(n0, slot, turn):
                    n = n0 + b * TILES
                    sp.wait_ge(s["at_psum"], at(n - 1))
                    sp.dma_start(an[:, slot, :], k.att[:, bass.ds(n0, 1), :].rearrange("p a n -> p (a n)")).then_inc(a_sem[slot], 16)
                    sp.wait_ge(s["x1_done"], at(n - 1))
                    sp.dma_start(xt[:, slot, :], x_in[bass.ds(n * P, P), :]).then_inc(x_sem[slot], 16)

                def store(n0, slot):
                    n = n0 + b * TILES
                    sp.wait_ge(s["x2_done"], at(n + 1))
                    sp.dma_start(x_out[bass.ds(n * P, P), :], fo[:, slot, :]).then_inc(st_sem[slot], 16)

                def load_store(n0, slot, turn):
                    load(n0, slot, turn)
                    store(n0 - 2, slot)
                for n0 in range(2):
                    load(n0, n0, 0)
                in_pairs(sp, 2, TILES, load_store)
                for n0 in range(TILES - 2, TILES):
                    store(n0, n0 % 2)
                for sem in st_sem:
                    sp.wait_ge(sem, 16 * TILES // 2 + 16)

            @block.tensor
            def _(pe):
                def project(n0, slot, turn):
                    n = n0 + b * TILES
                    pe.wait_ge(a_sem[slot], turn * 16 + 16)
                    pe.wait_ge(s["at_done"], at(n))
                    for c in range(C):
                        tr = nc.tensor.transpose(aps[:, c, :], an[:, slot, c * P:(c + 1) * P], k.ident[:])
                    tr.then_inc(s["at_psum"], 1)
                    pe.wait_ge(s["at_done"], at(n + 1))
                    pe.wait_ge(s["gated"], at(n - 1))
                    for c in range(C):
                        mm = nc.tensor.matmul(yps[:, slot, :], a_t[:, slot, c, :], wo[:, c, :], start=(c == 0), stop=(c == C - 1))
                    mm.then_inc(s["y_psum"], 1)

                def feed(n0, slot, turn):
                    n = n0 + b * TILES
                    norm_tensor(nc, pe, s, n, slot, xn, k.ident, hps)
                    pe.wait_ge(s["h_done"], at(C * n + C))
                    pe.wait_ge(s["biased"], at(n - 1))
                    for c in range(C):
                        mm = nc.tensor.matmul(fps[:, slot, :], h_t[:, slot, c, :], wf[:, c, :], start=(c == 0), stop=(c == C - 1))
                    mm.then_inc(s["f_psum"], 1)

                def both(n0, slot, turn):
                    project(n0 + 1, 1 - slot, turn + slot)
                    feed(n0, slot, turn)
                pe.wait_ge(w_in, 48)
                project(0, 0, 0)
                in_pairs(pe, 0, TILES - 2, both)
                both(TILES - 2, 0, TILES // 2 - 1)
                feed(TILES - 1, 1, TILES // 2 - 1)

            @block.scalar
            def _(act):
                def copy_att(n0, slot):
                    n = n0 + b * TILES
                    act.wait_ge(s["at_psum"], at(n + 1))
                    act.wait_ge(s["y_psum"], at(n - 1))
                    nc.scalar.activation(a_t[:, slot, :, :], aps[:], ACT.Copy).then_inc(s["at_done"], 1)

                def tile(n0, slot, turn, more=True):
                    n = n0 + b * TILES
                    if more:
                        copy_att(n0 + 1, 1 - slot)
                    norm_scalar(nc, act, s, n, slot, mv, k.ln_eps)
                    modulate(nc, act, s, n, slot, hps, h_t, k.mod_t, 2, b, s["f_psum"])
                copy_att(0, 0)
                in_pairs(act, 0, TILES - 2, tile)
                tile(TILES - 2, 0, TILES // 2 - 1)
                tile(TILES - 1, 1, TILES // 2 - 1, more=False)

            @block.vector
            def _(dve):
                def tile(n0, slot, turn):
                    n = n0 + b * TILES
                    x1s, fos = x1[:, slot, :], fo[:, slot, :]
                    dve.wait_ge(s["y_psum"], at(n + 1))
                    nc.vector.tensor_tensor(x1s, yps[:, slot, :], k.gates[:, 0, b, :], ALU.mult).then_inc(s["gated"], 1)
                    dve.wait_ge(s["gated"], at(n + 1))
                    dve.wait_ge(x_sem[slot], turn * 16 + 16)
                    nc.vector.tensor_tensor(x1s, x1s, xt[:, slot, :], ALU.add).then_inc(s["x1_done"], 1)
                    dve.wait_ge(s["x1_done"], at(n + 1))
                    norm_vector(nc, dve, s, n, slot, x1s, st, mv, xn)
                    dve.wait_ge(s["f_psum"], at(n + 1))
                    dve.wait_ge(st_sem[slot], turn * 16 + 16)
                    nc.vector.tensor_tensor(fos, fps[:, slot, :], bias[:], ALU.add).then_inc(s["biased"], 1)
                    dve.wait_ge(s["biased"], at(n + 1))
                    nc.vector.tensor_tensor(fos, fos, k.gates[:, 1, b, :], ALU.mult).then_inc(s["gated2"], 1)
                    dve.wait_ge(s["gated2"], at(n + 1))
                    nc.vector.tensor_tensor(fos, fos, x1s, ALU.add).then_inc(s["x2_done"], 1)
                dve.wait_ge(w_in, 48)
                in_pairs(dve, 0, TILES, tile)
        clear(nc, own)


class Kept:
    pass


def constants(nc, k, t):
    with ExitStack() as ctx:
        s = semaphores(ctx, nc, "co_", "filled ident_done causal_done after_done rounded")
        after = ctx.enter_context(nc.sbuf_tensor("co_after", [P, 3 * P], F32))
        with nc.Block() as block:
            @block.vector
            def _(dve):
                dve.wait_ge(s["ident_done"], 1)
                nc.vector.tensor_copy(k.ident_r[:], k.ident[:]).then_inc(s["rounded"], 1)
                dve.wait_ge(s["after_done"], 1)
                nc.vector.tensor_copy(k.after_r[:], after[:]).then_inc(s["rounded"], 1)

            @block.gpsimd
            def _(pool):
                pool.memset(k.ident[:], 0.0).then_inc(s["filled"], 1)
                pool.memset(k.causal[:], 0.0).then_inc(s["filled"], 1)
                pool.memset(k.ones[:], 1.0).then_inc(s["filled"], 1)
                pool.memset(k.zeros[:], 0.0).then_inc(s["filled"], 1)
                pool.memset(k.ln_eps[:], LN_EPS).then_inc(s["filled"], 1)
                pool.memset(after[:], 0.0).then_inc(s["filled"], 1)
                for e in range(E):
                    pool.memset(k.count[:, e:e + 1], float(e + 1)).then_inc(s["filled"], 1)
                pool.wait_ge(s["filled"], 6 + E)
                pool.affine_select(out=k.ident[:], in_=k.ident[:], compare_op=ALU.not_equal, fill=1.0, base=0,
                                   pattern=[[-1, P]], channel_multiplier=1).then_inc(s["ident_done"], 1)
                pool.affine_select(out=k.causal[:, HALF - P:HALF], in_=k.causal[:, HALF - P:HALF], compare_op=ALU.is_ge, fill=BELOW,
                                   base=0, pattern=[[-1, P]], channel_multiplier=1).then_inc(s["causal_done"], 1)
                pool.affine_select(out=after[:, P:2 * P], in_=after[:, P:2 * P], compare_op=ALU.is_ge, fill=BELOW,
                                   base=0, pattern=[[1, P]], channel_multiplier=-1).then_inc(s["after_done"], 1)
        clear(nc, s)


def layer0(nc, k, t, x_in, x_mid, scratch):
    with ExitStack() as ctx:
        sb = lambda n, sh, d=F32: ctx.enter_context(nc.sbuf_tensor("l0_" + n, sh, d))
        k.mod_t, k.gates = sb("mod", [P, 4, C, B]), sb("gates", [P, 2, B, D])
        modulation(nc, "m0_", t["c0"], t["wmod0"], k.mod_t, k.gates)
        join_weights(nc, t, scratch["wq0"], scratch["wout0"])
        sa = semaphores(ctx, nc, "a0_", IN0)
        sc = semaphores(ctx, nc, "c0_", FF0)
        st = semaphores(ctx, nc, "t0_", ATT0)
        for s in (sa, sc, st):
            prime(nc, s)
        k.o_t = sb("o_t", [P, NG, S])
        for b in range(B):
            with ExitStack() as inner:
                si = lambda n, sh, d=F32: inner.enter_context(nc.sbuf_tensor(f"l0b{b}_" + n, sh, d))
                k.qa_t = si("qa_t", [QA, S])
                k.khi, k.klo = si("khi", [KR + 1, S], F32R), si("klo", [KR, S], F32R)
                k.cn = si("cn", [P, TILES, LAT])
                k.cos_t, k.sin_t = si("cos_t", [P, S]), si("sin_t", [P, S])
                with ExitStack() as first:
                    sf = lambda n, sh, d=F32: first.enter_context(nc.sbuf_tensor(f"l0b{b}_" + n, sh, d))
                    k.cos_n, k.sin_n = sf("cos_n", [P, TILES, RH]), sf("sin_n", [P, TILES, RH])
                    k.kv_ln = sf("kv_ln", [P, LAT])
                    sems = semaphores(first, nc, f"l0b{b}_", "table_in one_row")
                    with nc.Block() as block:
                        @block.sync
                        def _(sp):
                            for dst, name in ((k.cos_t, "cos_t"), (k.sin_t, "sin_t"), (k.cos_n, "cos_n"), (k.sin_n, "sin_n"), (k.kv_ln, "kv_ln")):
                                sp.dma_start(dst[:], t[name]).then_inc(sems["table_in"], 16)
                            sp.wait_ge(sems["table_in"], 80)

                        @block.vector
                        def _(dve):
                            nc.vector.memset(k.khi[MR:MR + 1, :].bitcast(F32), 1.0).then_inc(sems["one_row"], 1)
                    clear(nc, sems)
                    latents(nc, sa, x_in, b, t, k)
                attention0(nc, st, k, b, scratch["wq0"])
            feed0(nc, sc, k, b, x_in, scratch["wout0"], t, x_mid)
        clear(nc, sa, sc, st)


def layer1(nc, k, t, x_in, out, scratch):
    with ExitStack() as ctx:
        sb = lambda n, sh, d=F32: ctx.enter_context(nc.sbuf_tensor("l1_" + n, sh, d))
        k.mod_t, k.gates = sb("mod", [P, 4, C, B]), sb("gates", [P, 2, B, D])
        modulation(nc, "m1_", t["c1"], t["wmod1"], k.mod_t, k.gates)
        join_feed1(nc, t, scratch["w_feed1"])
        sa = semaphores(ctx, nc, "a1_", IN1)
        sc = semaphores(ctx, nc, "c1_", FF1)
        st = semaphores(ctx, nc, "t1_", ATT1)
        for s in (sa, sc, st):
            prime(nc, s)
        k.att = sb("att", [P, TILES, D])
        k.vn = sb("vn", [P, TILES, 2 * HD])
        k.keys = sb("keys", [KR + 1, S], F32R)
        k.q_slots = [sb(f"q{i}", [KR + 1, G, S], F32R) for i in range(2)]
        k.qp_hi, k.qp_lo = sb("qp_hi", [P, C, S], F32R), sb("qp_lo", [P, C, S], F32R)
        filled = ctx.enter_context(nc.semaphore("l1_filled"))
        with nc.Block() as block:
            @block.vector
            def _(dve):
                nc.vector.memset(k.vn[:, :, HD:2 * HD], 1.0).then_inc(filled, 1)
                nc.vector.memset(k.keys[4 * HD:KR, :].bitcast(F32), 0.0).then_inc(filled, 1)
                nc.vector.memset(k.keys[MR:MR + 1, :].bitcast(F32), 1.0).then_inc(filled, 1)
                for q in k.q_slots:
                    nc.vector.memset(q[4 * HD:KR, :, :].bitcast(F32), 0.0).then_inc(filled, 1)
        for b in range(B):
            queries1(nc, sa, x_in, b, t, k)
            attention1(nc, st, k, b, scratch["queries1"])
            feed1(nc, sc, k, b, x_in, scratch["w_feed1"], t, out)


def build(nc, t, out, scratch, upto=9):
    nc.disable_value_cache = True
    with ExitStack() as ctx:
        sb = lambda n, sh, d=F32: ctx.enter_context(nc.sbuf_tensor(n, sh, d))
        k = Kept()
        k.ident, k.causal, k.ones = sb("ident", [P, P]), sb("causal", [P, HALF]), sb("ones", [P, LAT])
        k.ident_r, k.after_r = sb("ident_r", [P, P], F32R), sb("after_r", [P, 3 * P], F32R)
        k.zeros, k.count, k.ln_eps = sb("zeros", [P, E]), sb("count", [P, E]), sb("ln_eps", [P, 1])
        constants(nc, k, t)
        layer0(nc, k, t, t["x"], out if upto == 0 else scratch["x_mid"], scratch)
        if upto > 0:
            layer1(nc, k, t, scratch["x_mid"], out, scratch)


def rope_tables():
    base, factor, orig = 10000.0, 128.0, 1024
    corr = lambda r: ROPE * math.log(orig / (r * 2 * math.pi)) / (2 * math.log(base))
    low, high = max(math.floor(corr(32.0)), 0), min(math.ceil(corr(1.0)), ROPE - 1)
    hi = high + 0.001 if low == high else float(high)
    ramp = np.clip((np.arange(RH, dtype=np.float32) - low) / (hi - low), 0.0, 1.0)
    keep = 1.0 - ramp
    extra = 1.0 / base ** (np.arange(0, ROPE, 2, dtype=np.float32) / ROPE)
    inv = extra / factor * (1.0 - keep) + extra * keep
    f = np.outer(np.arange(S, dtype=np.float32), inv)
    return np.cos(f).astype(np.float32), np.sin(f).astype(np.float32)


def fourier():
    n = D
    eye = np.eye(n)
    spectrum = np.concatenate([eye[:, :1] * math.sqrt(n), (eye[:, 1:n - 1:2] - 1j * eye[:, 2:n:2][:, :(n - 1) // 2]) * math.sqrt(n / 2),
                               eye[:, -1:] * math.sqrt(n)], axis=-1)
    return np.fft.irfft(spectrum, n=n, axis=-1).astype(np.float32)


def lay_out(i):
    a = {n: np.asarray(v) for n, v in i.items()}
    col = lambda c: np.ascontiguousarray(c.T.reshape(C, P, B).transpose(1, 0, 2))
    rows = lambda v: np.broadcast_to(v.reshape(1, -1), (P, v.size))
    cos, sin = rope_tables()
    kv = a["L0_attn_wkv_a"]
    wqb = a["L0_attn_wq_b"].reshape(H, NOPE + ROPE, QA)
    wkvb = a["L0_attn_wkv_b"].reshape(H, NOPE + VD, LAT)
    pe = wqb[:, NOPE:].reshape(NG, G, RH, 2, QA)
    o = {
        "x": a["L0_attn_x"].reshape(B * S, D),
        "c0": col(a["L0_c"]), "wmod0": a["L0_wmod"], "c1": col(a["L1_c"]), "wmod1": a["L1_wmod"],
        "w_a": np.concatenate([a["L0_attn_wq_a"].T, kv[:LAT].T, kv[LAT::2].T, kv[LAT + 1::2].T], axis=1),
        "q_ln": a["L0_attn_q_a_ln_w"].reshape(QA, 1), "kv_ln": rows(a["L0_attn_kv_a_ln_w"]),
        "wqb_nope": wqb[:, :NOPE].transpose(1, 0, 2), "wk_b": wkvb[:, :NOPE].transpose(1, 0, 2), "wv_b": wkvb[:, NOPE:].transpose(1, 0, 2),
        "wqb_rope": pe.transpose(4, 0, 3, 1, 2).reshape(QA, NG, 2, P),
        "wo_t": a["L0_attn_wo"].T.reshape(H, VD, D),
        "cos_t": np.tile(cos.T, (G, 1)), "sin_t": np.tile(sin.T, (G, 1)),
        "cos_n": cos.reshape(TILES, P, RH).transpose(1, 0, 2), "sin_n": sin.reshape(TILES, P, RH).transpose(1, 0, 2),
        "w_base0": a["L0_ffn_W_base"].T, "b_base0": rows(a["L0_ffn_b_base"]), "b_router": rows(a["L0_ffn_b_router"]),
        "w_low0": np.concatenate([a["L0_ffn_lora_A"].transpose(1, 0, 2).reshape(D, E * R), a["L0_ffn_W_router"].T], axis=1),
        "lora_b": a["L0_ffn_lora_B"].reshape(E * R, D),
        "wq1": a["L1_attn_wq"], "wkv1": np.concatenate([a["L1_attn_wk"], a["L1_attn_wv"]], axis=1), "wo1": a["L1_attn_wo"],
        "w_base1": a["L1_ffn_W_base"].T, "b_base1": rows(a["L1_ffn_b_base"]),
        "enc": np.concatenate([a["L1_ffn_enc0"], a["L1_ffn_enc1"]], axis=0),
        "coefs": np.concatenate([a["L1_ffn_coefs0"], a["L1_ffn_coefs1"]], axis=2).reshape(E1, C, P, LOW).transpose(2, 0, 1, 3),
        "masks": np.concatenate([a["L1_ffn_mask0"], a["L1_ffn_mask1"]], axis=2).reshape(E1, C, P, LOW).transpose(2, 0, 1, 3),
        "fourier": fourier(),
    }
    o = {n: np.ascontiguousarray(v) for n, v in o.items()}
    o["masks"] = o["masks"].view(np.int32)
    return o


SCRATCH = {"wq0": (NG, QA, 3 * P), "wout0": (NG, P, D), "x_mid": (B * S, D), "w_feed1": (D, D), "queries1": (2, C, P, S)}


def kernel(**inputs):
    import concourse.bacc as bacc
    from concourse.bass_utils import run_bass_kernel_spmd

    nc = bacc.Bacc("TRN2", target_bir_lowering=False, num_devices=1)
    arrays = lay_out(inputs)
    t = {n: nc.dram_tensor(f"in_{n}", v.shape, mybir.dt.from_np(v.dtype), kind="ExternalInput").ap() for n, v in arrays.items()}
    scratch = {n: nc.dram_tensor(f"scratch_{n}", shape, F32, kind="Internal").ap() for n, shape in SCRATCH.items()}
    out = nc.dram_tensor("out", (B * S, D), F32, kind="ExternalOutput").ap()
    build(nc, t, out, scratch)
    r = run_bass_kernel_spmd(nc, [{f"in_{n}": v for n, v in arrays.items()}], core_ids=[0])
    return r.results[0]["out"].reshape(B, S, D)
```

```python
import math
from contextlib import ExitStack

import numpy as np

import concourse.bass as bass
from concourse import mybir

F32 = mybir.dt.float32
F32R = mybir.dt.float32r
U8 = mybir.dt.uint8
I32 = mybir.dt.int32
ALU = mybir.AluOpType
ACT = mybir.ActivationFunctionType
AX_X = mybir.AxisListType.X

P = 128
B, S, D = 2, 1024, 512
C = D // P
H = 32
NOPE, ROPE, VD, LAT = 64, 64, 128, 32
RH = ROPE // 2
QA = 128
HD = 16
G = 4
NG = H // G
TILES = S // P
HALF = 512
E, R = 8, 16
R0, R1, E1 = 32, 8, 3
LOW = R0 + R1
LN_EPS, RMS_EPS = 1e-5, 1e-6
MSCALE = 0.1 * math.log(128.0) + 1.0
SCALE0 = (NOPE + ROPE) ** -0.5 * MSCALE * MSCALE
SCALE1 = HD ** -0.5
ADAPT = 16.0 / 32.0
LOWEST = -3.0e38
BELOW = -1.0e38
KR = LAT + ROPE
MR = KR
CREDIT = 64


def at(n):
    return n + CREDIT


def semaphores(ctx, nc, prefix, names):
    return {name: ctx.enter_context(nc.semaphore(prefix + name)) for name in names.split()}


def words(ap):
    return ap.bitcast(F32)


def apart(eng, passed):
    eng.sem_inc(passed)


def in_pairs(eng, first, last, body):
    if last - first >= 4:
        with eng.Fori(0, (last - first) // 2) as i:
            for slot in (0, 1):
                body(i * 2 + (first + slot), slot, i + first // 2)
    else:
        for k in range(first, last):
            body(k, k % 2, k // 2)


def modulation(nc, name, c_t, wmod, mod_t, gates):
    with ExitStack() as ctx:
        sb = lambda n, s, d=F32: ctx.enter_context(nc.sbuf_tensor(name + n, s, d))
        s = semaphores(ctx, nc, name, "c_in gate_a_in gate_b_in cols_in exp_done one_plus sigm silu_done spread gate_psum gate_max gate_min "
                 "gate_pos gate_neg gate_done cols_psum cols_done ones_set")
        cin, ex, sg = sb("cin", [P, C, B]), sb("ex", [P, C, B]), sb("sg", [P, C, B])
        silu = sb("silu", [P, C, B])
        rep = sb("rep", [P, B, C, P])
        w = sb("w", [P, C, 6 * D])
        hi, lo = sb("hi", [P, 4, D]), sb("lo", [P, 4, D])
        gps = ctx.enter_context(nc.psum_tensor(name + "gps", [P, 4, D], F32))
        cps = ctx.enter_context(nc.psum_tensor(name + "cps", [P, D], F32))
        KIND = (0, 1, 3, 4)
        GATE = (2, 5)
        with nc.Block() as block:
            @block.sync
            def _(sp):
                sp.dma_start(cin[:], c_t).then_inc(s["c_in"], 16)
                for part, arrived in ((GATE[0], "gate_a_in"), (GATE[1], "gate_b_in"), *((part, "cols_in") for part in KIND)):
                    sp.dma_start(w[:, :, part * D:(part + 1) * D],
                                 wmod[:, part * D:(part + 1) * D].rearrange("(k p) n -> p k n", p=P)).then_inc(s[arrived], 16)

            @block.scalar
            def _(act):
                act.wait_ge(s["c_in"], 16)
                nc.scalar.activation(ex[:], cin[:], ACT.Exp, scale=-1.0).then_inc(s["exp_done"], 1)

            @block.vector
            def _(dve):
                dve.wait_ge(s["exp_done"], 1)
                nc.vector.tensor_scalar(ex[:], ex[:], 1.0, None, ALU.add).then_inc(s["one_plus"], 1)
                dve.wait_ge(s["one_plus"], 1)
                nc.vector.reciprocal(sg[:], ex[:]).then_inc(s["sigm"], 1)
                dve.wait_ge(s["sigm"], 1)
                nc.vector.tensor_tensor(silu[:], cin[:], sg[:], ALU.mult).then_inc(s["silu_done"], 1)
                dve.wait_ge(s["silu_done"], 1)
                for b in range(B):
                    for k in range(C):
                        nc.vector.tensor_copy(rep[:, b, k, :], silu[:, k, b:b + 1].to_broadcast([P, P])).then_inc(s["spread"], 1)
                for n in range(4):
                    g = gps[:, n, :]
                    dve.wait_ge(s["gate_psum"], n + 1)
                    nc.vector.tensor_scalar(hi[:, n, :], g, 0.25, None, ALU.max).then_inc(s["gate_max"], 1)
                    nc.vector.tensor_scalar(lo[:, n, :], g, -0.25, None, ALU.min).then_inc(s["gate_min"], 1)
                    dve.wait_ge(s["gate_max"], n + 1)
                    nc.vector.scalar_tensor_tensor(out=hi[:, n, :], in0=g, scalar=0.0, in1=hi[:, n, :],
                                                   op0=ALU.is_ge, op1=ALU.mult).then_inc(s["gate_pos"], 1)
                    dve.wait_ge(s["gate_min"], n + 1)
                    nc.vector.scalar_tensor_tensor(out=lo[:, n, :], in0=g, scalar=0.0, in1=lo[:, n, :],
                                                   op0=ALU.is_lt, op1=ALU.mult).then_inc(s["gate_neg"], 1)
                    dve.wait_ge(s["gate_pos"], n + 1)
                    dve.wait_ge(s["gate_neg"], n + 1)
                    nc.vector.tensor_tensor(gates[:, n // B, n % B, :], hi[:, n, :], lo[:, n, :], ALU.add).then_inc(s["gate_done"], 1)
                dve.wait_ge(s["cols_psum"], 1)
                cols = cps[:, 0:4 * C * B].rearrange("p (q k b) -> p q k b", q=4, k=C)
                for q in range(4):
                    nc.vector.tensor_scalar(mod_t[:, q, :, :], cols[:, q, :, :], float(q % 2), None, ALU.add).then_inc(s["cols_done"], 1)

            @block.tensor
            def _(pe):
                pe.wait_ge(s["spread"], B * C)
                for n in range(4):
                    if n % B == 0:
                        pe.wait_ge(s[("gate_a_in", "gate_b_in")[n // B]], 16)
                    for k in range(C):
                        mm = nc.tensor.matmul(gps[:, n, :], rep[:, n % B, k, :], w[:, k, GATE[n // B] * D:(GATE[n // B] + 1) * D],
                                              start=(k == 0), stop=(k == C - 1))
                    mm.then_inc(s["gate_psum"], 1)
                pe.wait_ge(s["cols_in"], 16 * len(KIND))
                for q in range(4):
                    for m in range(C):
                        o = (q * C + m) * B
                        for k in range(C):
                            mm = nc.tensor.matmul(cps[:, o:o + B], w[:, k, KIND[q] * D + m * P:KIND[q] * D + (m + 1) * P],
                                                  silu[:, k, :], start=(k == 0), stop=(k == C - 1))
                mm.then_inc(s["cols_psum"], 1)
        clear(nc, s)


def join_weights(nc, t, wq_dram, wout_dram):
    with ExitStack() as ctx:
        sb = lambda n, s, d=F32: ctx.enter_context(nc.sbuf_tensor("jw_" + n, s, d))
        s = semaphores(ctx, nc, "jw_", "small_in wo_in0 wo_in1 lat_psum lat_done rope_done wq_out vo_psum vo_done vo_out0 vo_out1")
        wo_in, vo_out = (s["wo_in0"], s["wo_in1"]), (s["vo_out0"], s["vo_out1"])
        nope = sb("nope", [NOPE, H, QA])
        wk = sb("wk", [NOPE, H, LAT])
        wv = sb("wv", [VD, H, LAT])
        rope = sb("rope", [QA, NG, 2, P])
        lnw = sb("lnw", [QA, 1])
        wo = sb("wo", [VD, 2, G, D])
        wq = sb("wq", [QA, NG, 3, P])
        vo = sb("vo", [P, 2, D])
        lps = ctx.enter_context(nc.psum_tensor("jw_lps", [P, 2, 512], F32))
        vps = ctx.enter_context(nc.psum_tensor("jw_vps", [P, 2, 512], F32))
        with nc.Block() as block:
            @block.sync
            def _(sp):
                for dst, src in ((nope, t["wqb_nope"]), (wk, t["wk_b"]), (wv, t["wv_b"]), (rope, t["wqb_rope"]), (lnw, t["q_ln"])):
                    sp.dma_start(dst[:], src).then_inc(s["small_in"], 16)
                def store(g):
                    sp.wait_ge(s["vo_done"], g + 1)
                    sp.dma_start(wout_dram[g], vo[:, g % 2, :]).then_inc(vo_out[g % 2], 16)

                for g in range(NG):
                    if g >= 2:
                        sp.wait_ge(s["vo_psum"], g - 1)
                    sp.dma_start(wo[:, g % 2, :, :], t["wo_t"][g * G:(g + 1) * G].rearrange("h p n -> p h n")).then_inc(wo_in[g % 2], 16)
                    if g >= 2:
                        store(g - 2)
                for g in range(NG - 2, NG):
                    store(g)
                sp.wait_ge(s["lat_done"], 2)
                sp.wait_ge(s["rope_done"], 1)
                sp.dma_start(wq_dram.rearrange("g p n -> p g n"), wq[:].rearrange("p g a n -> p g (a n)")).then_inc(s["wq_out"], 16)
                for sem in vo_out:
                    sp.wait_ge(sem, 16 * NG // 2)
                sp.wait_ge(s["wq_out"], 16)

            @block.tensor
            def _(pe):
                pe.wait_ge(s["small_in"], 80)
                for h in range(H):
                    o = (h % 16) * LAT
                    mm = nc.tensor.matmul(lps[:, h // 16, o:o + LAT], nope[:, h, :], wk[:, h, :], start=True, stop=True)
                mm.then_inc(s["lat_psum"], 1)
                for g in range(NG):
                    pe.wait_ge(wo_in[g % 2], 16 * (g // 2 + 1))
                    if g >= 2:
                        pe.wait_ge(s["vo_done"], g - 1)
                    for j in range(G):
                        mm = nc.tensor.matmul(vps[LAT * j:LAT * (j + 1), g % 2, :], wv[:, g * G + j, :], wo[:, g % 2, j, :],
                                              start=True, stop=True)
                    mm.then_inc(s["vo_psum"], 1)

            @block.vector
            def _(dve):
                dve.wait_ge(s["small_in"], 80)
                nc.vector.tensor_scalar(wq[:, :, 1:3, :], rope[:], lnw[:, 0:1], SCALE0, ALU.mult, ALU.mult).then_inc(s["rope_done"], 1)
                dve.wait_ge(s["lat_psum"], 1)
                for c in range(2):
                    nc.vector.tensor_scalar(wq[:, 4 * c:4 * c + 4, 0, :], lps[:, c, :].rearrange("p (g n) -> p g n", n=P),
                                            lnw[:, 0:1], SCALE0, ALU.mult, ALU.mult).then_inc(s["lat_done"], 1)

            @block.scalar
            def _(act):
                for g in range(NG):
                    act.wait_ge(s["vo_psum"], g + 1)
                    if g >= 2:
                        act.wait_ge(vo_out[g % 2], 16 * (g // 2))
                    nc.scalar.activation(vo[:, g % 2, :], vps[:, g % 2, :], ACT.Copy).then_inc(s["vo_done"], 1)
        clear(nc, s)


NORM_SEMS = "stats_done meanvar_done std_done rstd_done xn_done h_psum h_done"
HALVES = 2
TH = TILES // HALVES


def tiles(h):
    return range(TH * h, TH * (h + 1))


def norm_tensors(sb, ps, banks):
    return (sb("st", [P, TILES, 6]), sb("mv", [P, TILES, 2]), sb("sd", [P, 2, TILES, 1]), sb("xn", [P, TILES, D]),
            sb("h_t", [P, TILES, C, P]), ps("hps", [P, banks, C, P]))


def half_stats(nc, dve, s, b, h, st, mv):
    dve.wait_ge(s["stats_done"], at(b * TILES + TH * (h + 1)))
    for n0 in tiles(h):
        nc.vector.bn_aggr(mv[:, n0, :], st[:, n0, :]).then_inc(s["meanvar_done"], 1)


def half_deviation(nc, act, s, b, h, mv, sd, eps):
    act.wait_ge(s["meanvar_done"], at(b * TILES + TH * (h + 1)))
    ts = slice(TH * h, TH * (h + 1))
    nc.scalar.activation(sd[:, 0, ts, :], mv[:, ts, 1:2], ACT.Sqrt, bias=eps[:, 0:1]).then_inc(s["std_done"], 1)


def half_norm(nc, dve, s, b, h, x, mv, sd, xn):
    ts = slice(TH * h, TH * (h + 1))
    dve.wait_ge(s["std_done"], at(b * HALVES + h + 1))
    nc.vector.reciprocal(sd[:, 1, ts, :], sd[:, 0, ts, :]).then_inc(s["rstd_done"], 1)
    dve.wait_ge(s["rstd_done"], at(b * HALVES + h + 1))
    for n0 in tiles(h):
        nc.vector.tensor_scalar(xn[:, n0, :], x[:, n0, :], mv[:, n0, 0:1], sd[:, 1, n0, :], ALU.subtract, ALU.mult).then_inc(s["xn_done"], 1)


def turn_normed(nc, pe, s, b, n0, xn, ident, hps, banks):
    n = n0 + b * TILES
    pe.wait_ge(s["xn_done"], at(n + 1))
    pe.wait_ge(s["h_done"], at(C * (n + 1 - banks)))
    for c in range(C):
        tr = nc.tensor.transpose(hps[:, n0 % banks, c, :], xn[:, n0, c * P:(c + 1) * P], ident[:])
    tr.then_inc(s["h_psum"], 1)


def modulate(nc, act, s, b, n0, hps, banks, h_t, mod_t, kind):
    act.wait_ge(s["h_psum"], at(n0 + b * TILES + 1))
    for c in range(C):
        nc.scalar.activation(h_t[:, n0, c, :], hps[:, n0 % banks, c, :], ACT.Identity, bias=mod_t[:, kind, c, b:b + 1],
                             scale=mod_t[:, kind + 1, c, b:b + 1]).then_inc(s["h_done"], 1)


def clear(nc, *groups):
    with nc.Block() as block:
        @block.sync
        def _(sp):
            for sems in groups:
                for sem in sems.values():
                    sp.sem_clear(sem)


def prime(nc, sems):
    with nc.Block() as block:
        @block.sync
        def _(sp):
            for name, sem in sems.items():
                if "_in" not in name:
                    sp.sem_inc(sem, CREDIT)


IN0 = (NORM_SEMS + " a_psum ss_done raw_done ms_done rms_done rr_done qa_done c_done cn_done ropes_done k_done "
       "lat_t_psum qat_done khi_done klo_done")


def latents(nc, s, x_in, b, t, k):
    with ExitStack() as ctx:
        nm = f"la{b}_"
        sb = lambda n, sh, d=F32: ctx.enter_context(nc.sbuf_tensor(nm + n, sh, d))
        ps = lambda n, sh: ctx.enter_context(nc.psum_tensor(nm + n, sh, F32))
        own = semaphores(ctx, nc, nm, "w_in x_in0 x_in1")
        w_in, x_in_sem = own["w_in"], (own["x_in0"], own["x_in1"])
        W = QA + LAT + ROPE
        w = sb("w", [P, C, W])
        xt = sb("xt", [P, TILES, D])
        st, mv, sd, xn, h_t, hps = norm_tensors(sb, ps, 2)
        sq = sb("sq", [P, TILES, QA + LAT])
        ss, rr = sb("ss", [P, HALVES, 2, TH, 1]), sb("rr", [P, HALVES, 3, 2, TH, 1])
        raw = sb("raw", [P, HALVES, TH, W])
        qa, kk = sb("qa", [P, HALVES, TH, QA]), sb("kk", [P, HALVES, TH, KR])
        cr = sb("cr", [P, HALVES, TH, LAT])
        tm = sb("tm", [P, HALVES, 4, TH, RH])
        aps = ps("aps", [P, TH, 512])
        tq, tk = ps("tq", [P, HALF]), ps("tk", [P, HALF])
        X1, X2 = QA + LAT, QA + LAT + RH
        with nc.Block() as block:
            @block.sync
            def _(sp):
                for h in range(HALVES):
                    sp.dma_start(xt[:, TH * h:TH * (h + 1), :], x_in[b * S + HALF * h:b * S + HALF * (h + 1), :].rearrange("(n p) d -> p n d", p=P)).then_inc(x_in_sem[h], 16)
                    if h == 0:
                        sp.dma_start(w[:], t["w_a"].rearrange("(k p) n -> p k n", p=P)).then_inc(w_in, 16)

            @block.tensor
            def _(pe):
                def products(n0):
                    n = n0 + b * TILES
                    pe.wait_ge(s["h_done"], at(C * n + C))
                    pe.wait_ge(s["raw_done"], at(n + 1 - TH))
                    for c in range(C):
                        mm = nc.tensor.matmul(aps[:, n0 % TH, 0:W], h_t[:, n0, c, :], w[:, c, :], start=(c == 0), stop=(c == C - 1))
                    mm.then_inc(s["a_psum"], 1)

                def turn(h):
                    g = h + b * HALVES
                    pe.wait_ge(s["qa_done"], at(g + 1))
                    pe.wait_ge(s["k_done"], at(2 * g + 2))
                    pe.wait_ge(s["cn_done"], at(2 * g + 2))
                    pe.wait_ge(s["qat_done"], at(g))
                    pe.wait_ge(s["klo_done"], at(g))
                    for i in range(TH):
                        nc.tensor.transpose(tq[:, i * P:(i + 1) * P], qa[:, h, i, :], k.ident[:])
                        tr = nc.tensor.transpose(tk[0:KR, i * P:(i + 1) * P], kk[:, h, i, :], k.ident[:])
                    tr.then_inc(s["lat_t_psum"], 1)

                def normed(n0):
                    turn_normed(nc, pe, s, b, n0, xn, k.ident, hps, 2)
                normed(0)
                for n0 in range(1, TILES):
                    normed(n0)
                    if n0 == 1:
                        pe.wait_ge(w_in, 16)
                    products(n0 - 1)
                products(TILES - 1)
                for h in range(HALVES):
                    turn(h)

            @block.scalar
            def _(act):
                def squares(n0):
                    h, i = n0 // TH, n0 % TH
                    act.wait_ge(s["raw_done"], at(n0 + b * TILES + 1))
                    nc.scalar.activation(sq[:, n0, 0:QA], raw[:, h, i, 0:QA], ACT.Square, accum_out=ss[:, h, 0, i, :]).then_inc(s["ss_done"], 1)
                    nc.scalar.activation(sq[:, n0, QA:QA + LAT], raw[:, h, i, QA:QA + LAT], ACT.Square, accum_out=ss[:, h, 1, i, :]).then_inc(s["ss_done"], 1)

                def roots(h):
                    act.wait_ge(s["ms_done"], at(2 * (h + b * HALVES) + 2))
                    nc.scalar.activation(rr[:, h, 1], rr[:, h, 0], ACT.Sqrt).then_inc(s["rms_done"], 1)

                def query_out(h):
                    act.wait_ge(s["lat_t_psum"], at(h + b * HALVES + 1))
                    nc.scalar.activation(k.qa_t[:, HALF * h:HALF * (h + 1)], tq[:], ACT.Copy).then_inc(s["qat_done"], 1)
                for h in range(HALVES):
                    half_deviation(nc, act, s, b, h, mv, sd, k.ln_eps)
                for n0 in range(TILES):
                    modulate(nc, act, s, b, n0, hps, 2, h_t, k.mod_t, 0)
                    if n0 > 0:
                        squares(n0 - 1)
                    if n0 == TH:
                        roots(0)
                squares(TILES - 1)
                roots(1)
                for h in range(HALVES):
                    query_out(h)

            @block.vector
            def _(dve):
                def rms(h):
                    g = h + b * HALVES
                    for n0 in tiles(h):
                        dve.wait_ge(s["a_psum"], at(n0 + b * TILES + 1))
                        nc.vector.tensor_copy(raw[:, h, n0 - TH * h, :], aps[:, n0 % TH, 0:W]).then_inc(s["raw_done"], 1)
                    dve.wait_ge(s["ss_done"], at(2 * TH * (g + 1)))
                    for kind, width in enumerate((QA, LAT)):
                        nc.vector.tensor_scalar(rr[:, h, 0, kind], ss[:, h, kind], 1.0 / width, RMS_EPS, ALU.mult, ALU.add).then_inc(s["ms_done"], 1)
                    dve.wait_ge(s["raw_done"], at(TH * (g + 1)))
                    x1, x2 = raw[:, h, :, X1:X1 + RH], raw[:, h, :, X2:X2 + RH]
                    cs, sn = k.cos_n[:, TH * h:TH * (h + 1), :], k.sin_n[:, TH * h:TH * (h + 1), :]
                    for m, (a, c) in enumerate(((x1, cs), (x2, sn), (x2, cs), (x1, sn))):
                        nc.vector.tensor_tensor(tm[:, h, m], a, c, ALU.mult).then_inc(s["ropes_done"], 1)
                    dve.wait_ge(s["ropes_done"], at(4 * g + 4))
                    nc.vector.tensor_tensor(kk[:, h, :, LAT:LAT + RH], tm[:, h, 0], tm[:, h, 1], ALU.subtract).then_inc(s["k_done"], 1)
                    nc.vector.tensor_tensor(kk[:, h, :, LAT + RH:KR], tm[:, h, 2], tm[:, h, 3], ALU.add).then_inc(s["k_done"], 1)
                    dve.wait_ge(s["rms_done"], at(g + 1))
                    nc.vector.reciprocal(rr[:, h, 2], rr[:, h, 1]).then_inc(s["rr_done"], 1)
                    dve.wait_ge(s["rr_done"], at(g + 1))
                    nc.vector.tensor_tensor(cr[:, h], raw[:, h, :, QA:QA + LAT], rr[:, h, 2, 1].to_broadcast([P, TH, LAT]), ALU.mult).then_inc(s["c_done"], 1)
                    nc.vector.tensor_tensor(qa[:, h], raw[:, h, :, 0:QA], rr[:, h, 2, 0].to_broadcast([P, TH, QA]), ALU.mult).then_inc(s["qa_done"], 1)
                    dve.wait_ge(s["c_done"], at(g + 1))
                    for dst in (kk[:, h, :, 0:LAT], k.cn[:, TH * h:TH * (h + 1), :]):
                        nc.vector.tensor_tensor(dst, cr[:, h], k.kv_ln[:].unsqueeze(1).to_broadcast([P, TH, LAT]), ALU.mult).then_inc(s["cn_done"], 1)

                def keys(h):
                    g, cols = h + b * HALVES, slice(HALF * h, HALF * (h + 1))
                    dve.wait_ge(s["lat_t_psum"], at(g + 1))
                    nc.vector.tensor_copy(k.khi[0:KR, cols], tk[0:KR, :]).then_inc(s["khi_done"], 1)
                    dve.wait_ge(s["khi_done"], at(g + 1))
                    nc.vector.tensor_tensor(k.klo[0:KR, cols], tk[0:KR, :], k.khi[0:KR, cols].bitcast(F32), ALU.subtract).then_inc(s["klo_done"], 1)
                for h in range(HALVES):
                    dve.wait_ge(x_in_sem[h], 16)
                    for n0 in tiles(h):
                        nc.vector.bn_stats(st[:, n0, :], xt[:, n0, :]).then_inc(s["stats_done"], 1)
                    half_stats(nc, dve, s, b, h, st, mv)
                    half_norm(nc, dve, s, b, h, xt, mv, sd, xn)
                for h in range(HALVES):
                    rms(h)
                for h in range(HALVES):
                    keys(h)
        clear(nc, own)


UNITS = G * (4 + 8)
QUADS = UNITS // G
RING = 12
BANKS0, BANKS1 = 2, 3
MBANKS = 3
QK = [(qc, kt) for qc in range(2) for kt in range(4 * qc + 4)]
MU = [(j, qt, part) for j in range(G) for qt in range(TILES) for part in range(1 + qt // 4)]
M_AT = {2: 6, 3: 6, 4: 6, 5: 6, 6: 6, 7: 6, 8: 6, 9: 6}
P_AT = {4: (0,), 5: (1,), 6: (2,), 7: (3,), 8: (4,), 9: (5,)}
PJ = 6

ATT0 = ("q_in0 q_in1 lo_in0 lo_in1 m_in0 m_in1 wq_in0 wq_in1 "
        "passed sc_ready exp_done pv_done o_copied d_copied rd_done out_done mx_ready mx_done mx_joined "
        "mt_ready mrow_done pj_ready terms_done rot_done qhi_done qlo_done lat_hi lat_lo")


def steps(eng, step):
    step(-2, 0, -1, False, False, True)
    step(-1, 1, -1, False, True, True)
    in_pairs(eng, 0, NG - 2, lambda t, slot, turn: step(t, slot, turn, True, True, True))
    step(NG - 2, 0, NG // 2 - 1, True, True, False)
    step(NG - 1, 1, NG // 2 - 1, True, False, False)


def work(n, max_at, scores, maxima, queries):
    lo = sum(max_at.get(i, 0) for i in range(n))
    units = [("max", u, *MU[u]) for u in range(lo, lo + max_at.get(n, 0))] if maxima else []
    pieces = [("queries", u) for u in queries]
    for j in range(G):
        if scores and n < QUADS:
            pieces.append(("score", j))
        pieces += units[:2 if j == 0 else 1]
        units = units[2 if j == 0 else 1:]
    for bank in range(2):
        if scores and n >= 2:
            pieces.append(("values", bank))
        pieces += units[:1]
        units = units[1:]
    return pieces + units


def attention0(nc, s, k, b, wq_dram):
    with ExitStack() as ctx:
        nm = f"at{b}_"
        sb = lambda n, sh, d=F32: ctx.enter_context(nc.sbuf_tensor(nm + n, sh, d))
        ps = lambda n, sh: ctx.enter_context(nc.psum_tensor(nm + n, sh, F32))
        qhi = [sb(f"qhi{i}", [KR + 1, G, S], F32R) for i in range(2)]
        qlo = [sb(f"qlo{i}", [KR, G, S], F32R) for i in range(2)]
        shi, slo = sb("shi", [P, 3, S], F32R), sb("slo", [P, 3, S], F32R)
        tm = sb("tm", [P, 4, HALF])
        wq = sb("wq", [QA, 2, 3, P])
        prob = sb("prob", [P, RING, HALF])
        junk = sb("junk", [P, 2, HALF])
        mxd, mxf = sb("mxd", [P, G, TILES]), sb("mxf", [P, G, TILES // 2])
        mrow = sb("mrow", [G * TILES, P], F32R)
        o_sb, d_sb = sb("o_sb", [P, HALF]), sb("d_sb", [P, HALF])
        scp = [ps(f"scp{i}", [P, HALF]) for i in range(BANKS0)]
        mxp = [ps(f"mxp{i}", [P, HALF]) for i in range(MBANKS)]
        op, dp, pj = ps("op", [P, HALF]), ps("dp", [P, HALF]), ps("pj", [P, HALF])
        q_in, lo_in, m_in, wq_in = (s["q_in0"], s["q_in1"]), (s["lo_in0"], s["lo_in1"]), (s["m_in0"], s["m_in1"]), (s["wq_in0"], s["wq_in1"])
        g0 = b * NG
        MOVES = 16 * 3 * G

        def moved(slot, turn):
            return 1 - slot, MOVES * (turn + b * NG // 2 + slot + 1)

        with nc.Block() as block:
            @block.sync
            def _(sp):
                def step(t, slot, turn, scores, maxima, project):
                    if project:
                        sp.wait_ge(s["pj_ready"], at(PJ * (t + g0 + 1)))
                        sp.dma_start(wq[:, slot, :, :].rearrange("p a n -> p (a n)"),
                                     wq_dram[bass.ds(t + 2, 1)].rearrange("g p n -> p (g n)")).then_inc(wq_in[slot], 16)
                    if maxima:
                        o, t = 1 - slot, t + g0
                        sp.wait_ge(s["sc_ready"], at(t * UNITS))
                        sp.wait_ge(s["lat_hi"], at(2 * t + 4))
                        sp.wait_ge(s["qhi_done"], at(4 * t + 8))
                        for j in range(G):
                            for blk in range(3):
                                sp.dma_start(words(qhi[o][LAT * blk:LAT * (blk + 1), j, :]), words(shi[LAT * j:LAT * (j + 1), blk, :])).then_inc(q_in[o], 16)
                        sp.wait_ge(s["lat_lo"], at(2 * t + 4))
                        sp.wait_ge(s["qlo_done"], at(4 * t + 8))
                        for j in range(G):
                            for blk in range(3):
                                sp.dma_start(words(qlo[o][LAT * blk:LAT * (blk + 1), j, :]), words(slo[LAT * j:LAT * (j + 1), blk, :])).then_inc(lo_in[o], 16)
                        sp.wait_ge(s["mrow_done"], at(t + 2))
                        sp.dma_start(words(qhi[o][MR:MR + 1, :, :]), words(mrow[:])).then_inc(m_in[o], 16)
                steps(sp, step)

            @block.gpsimd
            def _(pool):
                def rotate(t, hf, slot, turn, maxima):
                    n = 2 * t + hf
                    cols = slice(HALF * hf, HALF * (hf + 1))
                    pool.wait_ge(s["terms_done"], at(4 * n + 4))
                    nc.gpsimd.tensor_tensor(tm[:, 0, :], tm[:, 0, :], tm[:, 2, :], ALU.subtract).then_inc(s["rot_done"], 1)
                    nc.gpsimd.tensor_tensor(tm[:, 1, :], tm[:, 1, :], tm[:, 3, :], ALU.add).then_inc(s["rot_done"], 1)
                    if maxima:
                        o, count = moved(slot, turn)
                        pool.wait_ge(lo_in[o], count)
                    pool.wait_ge(s["qhi_done"], at(2 * n + 2))
                    for m in range(2):
                        nc.gpsimd.tensor_tensor(slo[:, 1 + m, cols], tm[:, m, :], shi[:, 1 + m, cols].bitcast(F32),
                                                ALU.subtract).then_inc(s["qlo_done"], 1)

                def step(t, slot, turn, scores, maxima, project):
                    t = t + g0
                    for n in range(QUADS):
                        for u in P_AT.get(n, ()) if project else ():
                            if u % 3 == 2:
                                rotate(t + 2, u // 3, slot, turn, maxima)
                steps(pool, step)

            @block.scalar
            def _(act):
                def copy_out(t, hf):
                    act.wait_ge(s["pv_done"], at(t * QUADS + (12 if hf else 4)))
                    act.wait_ge(s["out_done"], at(2 * t + hf))
                    nc.scalar.activation(d_sb[:], dp[:], ACT.Copy).then_inc(s["d_copied"], 1)
                    nc.scalar.activation(o_sb[:], op[:], ACT.Copy).then_inc(s["o_copied"], 1)

                def step(t, slot, turn, scores, maxima, project):
                    t = t + g0
                    for n in range(QUADS):
                        qc, kt = QK[n]
                        if maxima and n == QUADS - 1:
                            act.wait_ge(s["mt_ready"], at(t + 2))
                            if scores:
                                act.wait_ge(m_in[slot], 16 * (turn + b * NG // 2 + 1))
                            nc.scalar.activation(mrow[:], pj[0:G * TILES, 0:P], ACT.Copy, scale=-1.0).then_inc(s["mrow_done"], 1)
                        if scores:
                            act.wait_ge(s["pv_done"], at(t * QUADS + n - 2))
                            for u in range(G * n, G * n + G):
                                c0 = max(kt - 4 * qc, 0) * P
                                act.wait_ge(s["sc_ready"], at(t * UNITS + u + 1))
                                nc.scalar.activation(prob[:, u % RING, c0:HALF], scp[u % BANKS0][:, c0:HALF], ACT.Exp).then_inc(s["exp_done"], 1)
                        for u in P_AT.get(n - 1, ()) if project else ():
                            if u % 3 == 2:
                                m = 2 * (t + 2) + u // 3
                                act.wait_ge(s["rot_done"], at(2 * m + 2))
                                if maxima:
                                    o, count = moved(slot, turn)
                                    act.wait_ge(q_in[o], count)
                                for r in range(2):
                                    nc.scalar.activation(shi[:, 1 + r, HALF * (u // 3):HALF * (u // 3 + 1)], tm[:, r, :], ACT.Copy).then_inc(s["qhi_done"], 1)
                        if scores and n == 5:
                            copy_out(t, 0)
                    if scores:
                        copy_out(t, 1)
                steps(act, step)

            @block.vector
            def _(dve):
                def maximum(t, u, j, qt, part):
                    w = (qt % 4 + 1) * P
                    if u == 0:
                        dve.wait_ge(s["mt_ready"], at(t))
                    dve.wait_ge(s["mx_ready"], at(t * UNITS + u + 1))
                    if qt >= 4 and part == 0:
                        nc.vector.reduce_max(mxf[:, j, qt - 4:qt - 3], mxp[u % MBANKS][:], AX_X).then_inc(s["mx_done"], 1)
                    else:
                        dve.wait_ge(s["mx_done"], at(t * UNITS + u - 1))
                        apart(dve, s["passed"])
                        nc.vector.tensor_tensor_reduce(out=junk[:, u % 2, 0:w], in0=mxp[u % MBANKS][:, 0:w], in1=k.causal[:, HALF - w:HALF],
                                                       scale=1.0, scalar=LOWEST, op0=ALU.add, op1=ALU.max,
                                                       accum_out=mxd[:, j, qt:qt + 1]).then_inc(s["mx_done"], 1)

                def projected(t, u, slot, turn, maxima):
                    hf, part = u // 3, u % 3
                    n = 2 * t + hf
                    cols = slice(HALF * hf, HALF * (hf + 1))
                    dve.wait_ge(s["pj_ready"], at(PJ * t + u + 1))
                    if part == 0:
                        if maxima:
                            o, count = moved(slot, turn)
                            dve.wait_ge(q_in[o], count)
                            dve.wait_ge(lo_in[o], count)
                        nc.vector.tensor_copy(shi[:, 0, cols], pj[:]).then_inc(s["lat_hi"], 1)
                        dve.wait_ge(s["lat_hi"], at(n + 1))
                        nc.vector.tensor_tensor(slo[:, 0, cols], pj[:], shi[:, 0, cols].bitcast(F32), ALU.subtract).then_inc(s["lat_lo"], 1)
                    else:
                        if part == 1:
                            dve.wait_ge(s["qlo_done"], at(2 * n))
                        for place, tab in ((0, k.cos_t), (3, k.sin_t)) if part == 1 else ((2, k.sin_t), (1, k.cos_t)):
                            nc.vector.tensor_tensor(tm[:, place, :], pj[:], tab[:, cols], ALU.mult).then_inc(s["terms_done"], 1)

                def finish(t, hf):
                    m = 2 * (t + g0) + hf
                    dve.wait_ge(s["d_copied"], at(m + 1))
                    nc.vector.reciprocal(d_sb[:], d_sb[:]).then_inc(s["rd_done"], 1)
                    dve.wait_ge(s["rd_done"], at(m + 1))
                    dve.wait_ge(s["o_copied"], at(m + 1))
                    nc.vector.tensor_tensor(k.o_t[:, bass.ds(t, 1), HALF * hf:HALF * (hf + 1)].rearrange("p a n -> p (a n)"),
                                            o_sb[:], d_sb[:], ALU.mult).then_inc(s["out_done"], 1)

                def step(t, slot, turn, scores, maxima, project):
                    for n in range(QUADS):
                        for kind, *piece in work(n, M_AT, scores, maxima, P_AT.get(n, ()) if project else ()):
                            if kind == "queries":
                                projected(t + g0 + 2, piece[0], slot, turn, maxima)
                            if kind == "max":
                                maximum(t + g0 + 1, *piece)
                        if maxima and n == max(M_AT):
                            dve.wait_ge(s["mx_done"], at((t + g0 + 2) * UNITS))
                            nc.vector.tensor_tensor(mxd[:, :, TILES // 2:TILES], mxd[:, :, TILES // 2:TILES], mxf[:], ALU.max).then_inc(s["mx_joined"], 1)
                        if scores and n == 10:
                            finish(t, 0)
                    if scores:
                        finish(t, 1)
                steps(dve, step)

            @block.tensor
            def _(pe):
                def score(t, slot, n, j):
                    qc, kt = QK[n]
                    u = G * n + j
                    c0 = min(max(kt - 4 * qc, 0) * P, HALF - 2 * P)
                    cols = slice(HALF * qc + c0, HALF * (qc + 1))
                    ks = slice(kt * P, (kt + 1) * P)
                    out = scp[u % BANKS0][:, c0:HALF]
                    pe.wait_ge(s["exp_done"], at(t * UNITS + u + 1 - BANKS0))
                    nc.tensor.matmul(out, k.khi[0:KR + 1, ks], qhi[slot][0:KR + 1, j, cols], start=True, stop=False)
                    if kt >= 4 * qc:
                        first = P if kt % 4 < 3 else 0
                        nc.tensor.matmul(out[:, 0:2 * P], k.ident_r[:], k.after_r[:, first:first + 2 * P], start=False, stop=False)
                    nc.tensor.matmul(out, k.khi[0:KR, ks], qlo[slot][0:KR, j, cols], start=False, stop=False)
                    nc.tensor.matmul(out, k.klo[0:KR, ks], qhi[slot][0:KR, j, cols], start=False, stop=True).then_inc(s["sc_ready"], 1)

                def maximum(t, slot, u, j, qt, part):
                    k0 = HALF if qt >= 4 and part == 1 else 0
                    w = HALF if qt >= 4 and part == 0 else max((qt % 4 + 1) * P, 2 * P)
                    pe.wait_ge(s["mx_done"], at(t * UNITS + u + 1 - MBANKS))
                    nc.tensor.matmul(mxp[u % MBANKS][:, 0:w], qhi[slot][0:KR, j, qt * P:(qt + 1) * P], k.khi[0:KR, k0:k0 + w],
                                     start=True, stop=True).then_inc(s["mx_ready"], 1)

                def values(t, n, part):
                    qc, kt = QK[n]
                    c0 = max(kt - 4 * qc, 0) * P
                    bank, left = ((op, k.cn[:, kt, :]), (dp, k.ones[:]))[part]
                    pe.wait_ge(s["exp_done"], at(t * UNITS + G * n + G))
                    if kt == 0:
                        pe.wait_ge((s["o_copied"], s["d_copied"])[part], at(2 * t + qc))
                    for j in range(G):
                        mm = nc.tensor.matmul(bank[LAT * j:LAT * (j + 1), c0:HALF], left, prob[:, (G * n + j) % RING, c0:HALF],
                                              start=(kt == 0), stop=(kt == 4 * qc + 3))
                    if part == 1:
                        mm.then_inc(s["pv_done"], 1)

                def project_q(t, slot, turn, u):
                    hf, part = u // 3, u % 3
                    pe.wait_ge(s["mrow_done"], at(t - 1))
                    if part == 1:
                        pe.wait_ge(s["lat_lo"], at(2 * t + hf + 1))
                    else:
                        pe.wait_ge(s["terms_done"], at(4 * (2 * t + hf) + (2 if part else 0)))
                    if u == 0:
                        pe.wait_ge(wq_in[slot], 16 * (turn + b * NG // 2 + 2))
                    nc.tensor.matmul(pj[:], wq[:, slot, part, :], k.qa_t[:, HALF * hf:HALF * (hf + 1)], start=True, stop=True).then_inc(s["pj_ready"], 1)

                def step(t, slot, turn, scores, maxima, project):
                    t = t + g0
                    for n in range(QUADS + 2):
                        if maxima and n == QUADS - 1:
                            pe.wait_ge(s["mx_joined"], at(t + 2))
                            pe.wait_ge(s["terms_done"], at(8 * (t + (3 if project else 2))))
                            nc.tensor.transpose(pj[0:G * TILES, 0:P], mxd[:].rearrange("p j q -> p (j q)"), k.ident[:]).then_inc(s["mt_ready"], 1)
                        if scores and n == 0:
                            pe.wait_ge(q_in[slot], MOVES * (turn + b * NG // 2 + 1))
                            pe.wait_ge(lo_in[slot], MOVES * (turn + b * NG // 2 + 1))
                            pe.wait_ge(m_in[slot], 16 * (turn + b * NG // 2 + 1))
                        for kind, *piece in work(n, M_AT, scores, maxima, P_AT.get(n, ()) if project else ()):
                            if kind == "queries":
                                project_q(t + 2, slot, turn, piece[0])
                            if kind == "score":
                                score(t, slot, n, piece[0])
                            if kind == "max":
                                if piece[0] == 0:
                                    o, count = moved(slot, turn)
                                    pe.wait_ge(q_in[o], count)
                                maximum(t + 1, 1 - slot, *piece)
                            if kind == "values":
                                values(t, n - 2, piece[0])
                steps(pe, step)


OUT_SEMS = " y_psum gated x1_done f_psum biased gated2 x2_done"
FF0 = (NORM_SEMS + OUT_SEMS + " l_psum z_done zs_done cum_done kz_done sup_done kn_done eq_done sel_done ts_done rk_done tau_done "
       "zt_done ew_done lw_done lt_psum lt_done")


def first_residual(nc, dve, s, b, n0, x_in_sem, yps, xt, x1, st, gates):
    n = n0 + b * TILES
    dve.wait_ge(s["y_psum"], at(n + 1))
    nc.vector.tensor_tensor(x1[:, n0, :], yps[:, n0 % 2, :], gates[:, 0, b, :], ALU.mult).then_inc(s["gated"], 1)
    dve.wait_ge(s["gated"], at(n + 1))
    if n0 % TH == 0:
        dve.wait_ge(x_in_sem[n0 // TH], 16)
    nc.vector.tensor_tensor(x1[:, n0, :], x1[:, n0, :], xt[:, n0, :], ALU.add).then_inc(s["x1_done"], 1)
    dve.wait_ge(s["x1_done"], at(n + 1))
    nc.vector.bn_stats(st[:, n0, :], x1[:, n0, :]).then_inc(s["stats_done"], 1)


def second_residual(nc, dve, s, b, n0, fps, bias, x1, out, gates):
    n = n0 + b * TILES
    dve.wait_ge(s["f_psum"], at(n + 1))
    nc.vector.tensor_tensor(out[:, n0, :], fps[:, n0 % 2, :], bias[:], ALU.add).then_inc(s["biased"], 1)
    dve.wait_ge(s["biased"], at(n + 1))
    nc.vector.tensor_tensor(out[:, n0, :], out[:, n0, :], gates[:, 1, b, :], ALU.mult).then_inc(s["gated2"], 1)
    dve.wait_ge(s["gated2"], at(n + 1))
    nc.vector.tensor_tensor(out[:, n0, :], out[:, n0, :], x1[:, n0, :], ALU.add).then_inc(s["x2_done"], 1)


def load_x(sp, b, xt, x_in, x_in_sem):
    for h in range(HALVES):
        sp.dma_start(xt[:, TH * h:TH * (h + 1), :], x_in[b * S + HALF * h:b * S + HALF * (h + 1), :].rearrange("(n p) d -> p n d", p=P)).then_inc(x_in_sem[h], 16)


def store_x(sp, s, b, out, x_out, x_out_sem):
    for n0 in range(TILES):
        n = n0 + b * TILES
        sp.wait_ge(s["x2_done"], at(n + 1))
        sp.dma_start(x_out[n * P:(n + 1) * P, :], out[:, n0, :]).then_inc(x_out_sem, 16)
    sp.wait_ge(x_out_sem, 16 * TILES)


def feed0(nc, s, k, b, x_in, wout_dram, t, x_out):
    with ExitStack() as ctx:
        nm = f"ff{b}_"
        sb = lambda n, sh, d=F32: ctx.enter_context(nc.sbuf_tensor(nm + n, sh, d))
        ps = lambda n, sh: ctx.enter_context(nc.psum_tensor(nm + n, sh, F32))
        own = semaphores(ctx, nc, nm, "wo_in w_in x_in0 x_in1 x_out")
        wo_in, w_in, x_in_sem, x_out_sem = own["wo_in"], own["w_in"], (own["x_in0"], own["x_in1"]), own["x_out"]
        wo = sb("wo", [P, NG, D])
        wb, wl, lb = sb("wb", [P, C, D]), sb("wl", [P, C, P + E]), sb("lb", [P, D])
        bias, rbias = sb("bias", [P, D]), sb("rbias", [P, E])
        xt, x1 = sb("xt", [P, TILES, D]), sb("x1", [P, TILES, D])
        st, mv, sd, xn, h_t, hps = norm_tensors(sb, ps, 1)
        r = sb("r", [P, HALVES, 9, TH, E])
        rc = sb("rc", [P, HALVES, 4, TH, 1])
        low, low_t = sb("low", [P, HALVES, TH, P]), sb("low_t", [P, HALVES, TH, P])
        yps, fps = ps("yps", [P, 2, D]), ps("fps", [P, 2, D])
        lps, tps = ps("lps", [P, TH, 256]), ps("tps", [P, TH, P])
        with nc.Block() as block:
            @block.sync
            def _(sp):
                for half in range(2):
                    sp.dma_start(wo[:, 4 * half:4 * half + 4, :], wout_dram[4 * half:4 * half + 4].rearrange("g p n -> p g n")).then_inc(wo_in, 16)
                load_x(sp, b, xt, x_in, x_in_sem)
                for dst, name in ((wl, "w_low0"), (wb, "w_base0")):
                    sp.dma_start(dst[:], t[name].rearrange("(k p) n -> p k n", p=P)).then_inc(w_in, 16)
                for dst, name in ((lb, "lora_b"), (bias, "b_base0"), (rbias, "b_router")):
                    sp.dma_start(dst[:], t[name]).then_inc(w_in, 16)
                store_x(sp, s, b, xt, x_out, x_out_sem)

            @block.tensor
            def _(pe):
                def project(n0):
                    n = n0 + b * TILES
                    pe.wait_ge(s["gated"], at(n - 1))
                    for g in range(NG):
                        mm = nc.tensor.matmul(yps[:, n0 % 2, :], k.o_t[:, g, n0 * P:(n0 + 1) * P], wo[:, g, :], start=(g == 0), stop=(g == NG - 1))
                    mm.then_inc(s["y_psum"], 1)

                def low_products(h):
                    pe.wait_ge(s["z_done"], at(h + b * HALVES))
                    pe.wait_ge(s["lw_done"], at(h + b * HALVES))
                    for i, n0 in enumerate(tiles(h)):
                        turn_normed(nc, pe, s, b, n0, xn, k.ident, hps, 1)
                        pe.wait_ge(s["h_done"], at(C * (n0 + b * TILES + 1)))
                        for c in range(C):
                            mm = nc.tensor.matmul(lps[:, i, 0:P + E], h_t[:, n0, c, :], wl[:, c, :], start=(c == 0), stop=(c == C - 1))
                    mm.then_inc(s["l_psum"], 1)

                def base(n0):
                    pe.wait_ge(s["biased"], at(n0 + b * TILES - 1))
                    for c in range(C):
                        nc.tensor.matmul(fps[:, n0 % 2, :], h_t[:, n0, c, :], wb[:, c, :], start=(c == 0), stop=False)

                def adapt(n0):
                    nc.tensor.matmul(fps[:, n0 % 2, :], low_t[:, n0 // TH, n0 % TH, :], lb[:], start=False, stop=True).then_inc(s["f_psum"], 1)

                def feed(h):
                    g, first = h + b * HALVES, TH * h
                    base(first)
                    base(first + 1)
                    pe.wait_ge(s["lw_done"], at(g + 1))
                    pe.wait_ge(s["lt_done"], at(g))
                    for i in range(TH):
                        tr = nc.tensor.transpose(tps[:, i, :], low[:, h, i, :], k.ident[:])
                    tr.then_inc(s["lt_psum"], 1)
                    pe.wait_ge(s["lt_done"], at(g + 1))
                    adapt(first)
                    adapt(first + 1)
                    for n0 in range(first + 2, first + TH):
                        base(n0)
                        adapt(n0)
                pe.wait_ge(wo_in, 32)
                for n0 in range(TH + 2):
                    project(n0)
                pe.wait_ge(w_in, 16 * 5)
                low_products(0)
                for n0 in range(TH + 2, TILES):
                    project(n0)
                feed(0)
                low_products(1)
                feed(1)

            @block.scalar
            def _(act):
                def low_out(h):
                    act.wait_ge(s["lt_psum"], at(h + b * HALVES + 1))
                    nc.scalar.activation(low_t[:, h], tps[:], ACT.Copy).then_inc(s["lt_done"], 1)
                for h in range(HALVES):
                    half_deviation(nc, act, s, b, h, mv, sd, k.ln_eps)
                    if h > 0:
                        low_out(h - 1)
                    for n0 in tiles(h):
                        modulate(nc, act, s, b, n0, hps, 1, h_t, k.mod_t, 2)
                low_out(HALVES - 1)

            @block.vector
            def _(dve):
                def experts(h):
                    g = h + b * HALVES
                    z, zs, cum, kz, sup, eq, sel, zt, ew = (r[:, h, i] for i in range(9))
                    kn, ts, rk, tau = (rc[:, h, i] for i in range(4))
                    count = k.count[:].unsqueeze(1).to_broadcast([P, TH, E])
                    dve.wait_ge(s["l_psum"], at(g + 1))
                    nc.vector.tensor_tensor(z, lps[:, :, P:P + E], rbias[:].unsqueeze(1).to_broadcast([P, TH, E]), ALU.add).then_inc(s["z_done"], 1)
                    dve.wait_ge(s["z_done"], at(g + 1))
                    for i in range(TH):
                        nc.vector.max(zs[:, i, :], z[:, i, :]).then_inc(s["zs_done"], 1)
                    dve.wait_ge(s["zs_done"], at(TH * g + TH))
                    for i in range(TH):
                        nc.vector.tensor_tensor_scan(cum[:, i, :], zs[:, i, :], k.zeros[:, 0:E], 0.0, ALU.add, ALU.add).then_inc(s["cum_done"], 1)
                    nc.vector.tensor_tensor(kz, zs, count, ALU.mult).then_inc(s["kz_done"], 1)
                    dve.wait_ge(s["cum_done"], at(TH * g + TH))
                    dve.wait_ge(s["kz_done"], at(g + 1))
                    nc.vector.scalar_tensor_tensor(out=sup, in0=kz, scalar=1.0, in1=cum, op0=ALU.add, op1=ALU.is_gt).then_inc(s["sup_done"], 1)
                    dve.wait_ge(s["sup_done"], at(g + 1))
                    nc.vector.reduce_sum(kn, sup, AX_X).then_inc(s["kn_done"], 1)
                    dve.wait_ge(s["kn_done"], at(g + 1))
                    nc.vector.reciprocal(rk, kn).then_inc(s["rk_done"], 1)
                    nc.vector.tensor_tensor(eq, count, kn.to_broadcast([P, TH, E]), ALU.is_equal).then_inc(s["eq_done"], 1)
                    dve.wait_ge(s["eq_done"], at(g + 1))
                    nc.vector.tensor_tensor(sel, eq, cum, ALU.mult).then_inc(s["sel_done"], 1)
                    dve.wait_ge(s["sel_done"], at(g + 1))
                    nc.vector.reduce_sum(ts, sel, AX_X).then_inc(s["ts_done"], 1)
                    dve.wait_ge(s["ts_done"], at(g + 1))
                    dve.wait_ge(s["rk_done"], at(g + 1))
                    nc.vector.scalar_tensor_tensor(out=tau, in0=ts, scalar=-1.0, in1=rk, op0=ALU.add, op1=ALU.mult).then_inc(s["tau_done"], 1)
                    dve.wait_ge(s["tau_done"], at(g + 1))
                    nc.vector.tensor_tensor(zt, z, tau.to_broadcast([P, TH, E]), ALU.subtract).then_inc(s["zt_done"], 1)
                    dve.wait_ge(s["zt_done"], at(g + 1))
                    nc.vector.tensor_scalar(ew, zt, 0.0, None, ALU.max).then_inc(s["ew_done"], 1)
                    dve.wait_ge(s["ew_done"], at(g + 1))
                    nc.vector.tensor_tensor(low[:, h].rearrange("p t (e r) -> p t e r", r=R), lps[:, :, 0:P].rearrange("p t (e r) -> p t e r", r=R),
                                            ew.unsqueeze(3).to_broadcast([P, TH, E, R]), ALU.mult).then_inc(s["lw_done"], 1)

                def first(n0):
                    first_residual(nc, dve, s, b, n0, x_in_sem, yps, xt, x1, st, k.gates)

                def second(n0):
                    second_residual(nc, dve, s, b, n0, fps, bias, x1, xt, k.gates)
                for n0 in tiles(0):
                    first(n0)
                half_stats(nc, dve, s, b, 0, st, mv)
                half_norm(nc, dve, s, b, 0, x1, mv, sd, xn)
                first(TH)
                first(TH + 1)
                dve.wait_ge(w_in, 16 * 5)
                experts(0)
                for n0 in range(TH + 2, TILES):
                    first(n0)
                half_stats(nc, dve, s, b, 1, st, mv)
                half_norm(nc, dve, s, b, 1, x1, mv, sd, xn)
                for n0 in tiles(0):
                    second(n0)
                experts(1)
                for n0 in tiles(1):
                    second(n0)
        clear(nc, own)


def join_feed1(nc, t, w_dram):
    with ExitStack() as ctx:
        sb = lambda n, sh, d=F32: ctx.enter_context(nc.sbuf_tensor("jf_" + n, sh, d))
        s = semaphores(ctx, nc, "jf_", "in_done mask_done w_done sum_done g_psum g_done d_psum d_done w_out")
        co, mw, mf = sb("co", [P, E1, C, LOW]), sb("mw", [P, E1, C, LOW // 4], I32), sb("mf", [P, E1, C, LOW])
        fo, wb, wj = sb("fo", [P, C, D]), sb("wb", [P, C, D]), sb("wj", [P, C, D])
        enc, gs = sb("enc", [LOW, D]), sb("gs", [LOW, D])
        gps = ctx.enter_context(nc.psum_tensor("jf_gps", [LOW, D], F32))
        dps = ctx.enter_context(nc.psum_tensor("jf_dps", [P, C, D], F32))
        with nc.Block() as block:
            @block.sync
            def _(sp):
                for dst, src in ((co, t["coefs"]), (mw, t["masks"]), (enc, t["enc"]), (fo, t["fourier"].rearrange("(k p) n -> p k n", p=P)),
                                 (wb, t["w_base1"].rearrange("(k p) n -> p k n", p=P))):
                    sp.dma_start(dst[:], src).then_inc(s["in_done"], 16)
                sp.wait_ge(s["d_done"], C)
                sp.dma_start(w_dram.rearrange("(k p) n -> p k n", p=P), wj[:]).then_inc(s["w_out"], 16)
                sp.wait_ge(s["w_out"], 16)

            @block.vector
            def _(dve):
                dve.wait_ge(s["in_done"], 80)
                nc.vector.tensor_copy(mf[:].rearrange("p e c r -> p (e c r)"), mw[:].rearrange("p e c r -> p (e c r)").bitcast(U8)).then_inc(s["mask_done"], 1)
                dve.wait_ge(s["mask_done"], 1)
                nc.vector.tensor_tensor(mf[:], mf[:], co[:], ALU.mult).then_inc(s["w_done"], 1)
                dve.wait_ge(s["w_done"], 1)
                for e in range(1, E1):
                    nc.vector.tensor_tensor(mf[:, 0], mf[:, 0], mf[:, e], ALU.add).then_inc(s["sum_done"], 1)
                    dve.wait_ge(s["sum_done"], e)
                dve.wait_ge(s["g_psum"], 1)
                nc.vector.tensor_copy(gs[:], gps[:]).then_inc(s["g_done"], 1)
                for c in range(C):
                    dve.wait_ge(s["d_psum"], c + 1)
                    nc.vector.scalar_tensor_tensor(out=wj[:, c, :], in0=dps[:, c, :], scalar=ADAPT, in1=wb[:, c, :],
                                                   op0=ALU.mult, op1=ALU.add).then_inc(s["d_done"], 1)

            @block.tensor
            def _(pe):
                pe.wait_ge(s["sum_done"], E1 - 1)
                for c in range(C):
                    mm = nc.tensor.matmul(gps[:], mf[:, 0, c, :], fo[:, c, :], start=(c == 0), stop=(c == C - 1))
                mm.then_inc(s["g_psum"], 1)
                pe.wait_ge(s["g_done"], 1)
                for c in range(C):
                    nc.tensor.matmul(dps[:, c, :], enc[:, c * P:(c + 1) * P], gs[:], start=True, stop=True).then_inc(s["d_psum"], 1)
        clear(nc, s)


IN1 = (NORM_SEMS + " q_psum v_psum qhi_done qlo_done kv_done k_t_psum khi_done klo_done v_done")


def queries1(nc, s, x_in, b, t, k, q_dram):
    with ExitStack() as ctx:
        nm = f"qk{b}_"
        sb = lambda n, sh, d=F32: ctx.enter_context(nc.sbuf_tensor(nm + n, sh, d))
        ps = lambda n, sh: ctx.enter_context(nc.psum_tensor(nm + n, sh, F32))
        own = semaphores(ctx, nc, nm, "w_in keys_in q_out x_in0 x_in1")
        q_out = own["q_out"]
        w_in, keys_in, x_in_sem = own["w_in"], own["keys_in"], (own["x_in0"], own["x_in1"])
        wq, wkv = sb("wq", [P, C, D]), sb("wkv", [P, C, 2 * HD])
        xt = sb("xt", [P, TILES, D])
        st, mv, sd, xn, h_t, hps = norm_tensors(sb, ps, 2)
        kv = sb("kv", [P, TILES, HD])
        k_hi, k_lo = sb("k_hi", [HD, S], F32R), sb("k_lo", [HD, S], F32R)
        qps, vps, tps = ps("qps", [P, 4, HALF]), ps("vps", [P, TILES, 64]), ps("tps", [P, HALF])
        with nc.Block() as block:
            @block.sync
            def _(sp):
                for h in range(HALVES):
                    sp.dma_start(xt[:, TH * h:TH * (h + 1), :], x_in[b * S + HALF * h:b * S + HALF * (h + 1), :].rearrange("(n p) d -> p n d", p=P)).then_inc(x_in_sem[h], 16)
                    if h == 0:
                        sp.dma_start(wkv[:], t["wkv1"].rearrange("(k p) n -> p k n", p=P)).then_inc(w_in, 16)
                        sp.dma_start(wq[:], t["wq1"].rearrange("(k p) n -> p k n", p=P)).then_inc(w_in, 16)
                for h in range(HALVES):
                    for m in range(C):
                        sp.wait_ge(s["qlo_done"], at(C * (h + b * HALVES) + m + 1))
                        for part, src in enumerate((k.qp_hi, k.qp_lo)):
                            sp.dma_start(q_dram[part, m, :, HALF * h:HALF * (h + 1)], words(src[:, m, HALF * h:HALF * (h + 1)])).then_inc(q_out, 16)
                sp.wait_ge(s["klo_done"], at((b + 1) * HALVES))
                for blk in range(4):
                    sp.dma_start(words(k.keys[HD * blk:HD * (blk + 1), :]), words((k_hi, k_lo)[blk % 2][:])).then_inc(keys_in, 16)
                sp.wait_ge(keys_in, 64)
                sp.wait_ge(q_out, 16 * 2 * HALVES * C)

            @block.tensor
            def _(pe):
                def half(h):
                    g = h + b * HALVES
                    for n0 in tiles(h):
                        turn_normed(nc, pe, s, b, n0, xn, k.ident, hps, 2)
                    pe.wait_ge(s["kv_done"], at(g))
                    pe.wait_ge(s["v_done"], at(g))
                    for n0 in tiles(h):
                        pe.wait_ge(s["h_done"], at(C * (n0 + b * TILES + 1)))
                        for c in range(C):
                            mm = nc.tensor.matmul(vps[:, n0, 0:2 * HD], h_t[:, n0, c, :], wkv[:, c, :], start=(c == 0), stop=(c == C - 1))
                    mm.then_inc(s["v_psum"], 1)
                    for m in range(C):
                        pe.wait_ge(s["qlo_done"], at(C * (g - 1) + m + 1))
                        for c in range(C):
                            mm = nc.tensor.matmul(qps[:, m, :], wq[:, c, m * P:(m + 1) * P], h_t[:, TH * h:TH * (h + 1), c, :], start=(c == 0), stop=(c == C - 1))
                        mm.then_inc(s["q_psum"], 1)
                    pe.wait_ge(s["kv_done"], at(g + 1))
                    pe.wait_ge(s["klo_done"], at(g))
                    for n0 in tiles(h):
                        tr = nc.tensor.transpose(tps[0:HD, (n0 - TH * h) * P:(n0 - TH * h + 1) * P], kv[:, n0, :], k.ident[:])
                    tr.then_inc(s["k_t_psum"], 1)
                pe.wait_ge(w_in, 32)
                for h in range(HALVES):
                    half(h)

            @block.scalar
            def _(act):
                for h in range(HALVES):
                    half_deviation(nc, act, s, b, h, mv, sd, k.ln_eps)
                for h in range(HALVES):
                    g = h + b * HALVES
                    for n0 in tiles(h):
                        modulate(nc, act, s, b, n0, hps, 2, h_t, k.mod_t, 0)
                    for m in range(C):
                        act.wait_ge(s["q_psum"], at(C * g + m + 1))
                        nc.scalar.activation(k.qp_hi[:, m, HALF * h:HALF * (h + 1)], qps[:, m, :], ACT.Copy, scale=SCALE1).then_inc(s["qhi_done"], 1)

            @block.vector
            def _(dve):
                for h in range(HALVES):
                    dve.wait_ge(x_in_sem[h], 16)
                    for n0 in tiles(h):
                        nc.vector.bn_stats(st[:, n0, :], xt[:, n0, :]).then_inc(s["stats_done"], 1)
                    half_stats(nc, dve, s, b, h, st, mv)
                    half_norm(nc, dve, s, b, h, xt, mv, sd, xn)
                for h in range(HALVES):
                    g, ts, cols = h + b * HALVES, slice(TH * h, TH * (h + 1)), slice(HALF * h, HALF * (h + 1))
                    dve.wait_ge(s["v_psum"], at(g + 1))
                    nc.vector.tensor_copy(kv[:, ts, :], vps[:, ts, 0:HD]).then_inc(s["kv_done"], 1)
                    nc.vector.tensor_copy(k.vn[:, ts, 0:HD], vps[:, ts, HD:2 * HD]).then_inc(s["v_done"], 1)
                    for m in range(C):
                        dve.wait_ge(s["qhi_done"], at(C * g + m + 1))
                        nc.vector.scalar_tensor_tensor(out=k.qp_lo[:, m, cols], in0=qps[:, m, :], scalar=SCALE1, in1=k.qp_hi[:, m, cols].bitcast(F32),
                                                       op0=ALU.mult, op1=ALU.subtract).then_inc(s["qlo_done"], 1)
                    dve.wait_ge(s["k_t_psum"], at(g + 1))
                    nc.vector.tensor_copy(k_hi[:, cols], tps[0:HD, :]).then_inc(s["khi_done"], 1)
                    dve.wait_ge(s["khi_done"], at(g + 1))
                    nc.vector.tensor_tensor(k_lo[:, cols], tps[0:HD, :], k_hi[:, cols].bitcast(F32), ALU.subtract).then_inc(s["klo_done"], 1)
        clear(nc, own)


M_AT1 = {1: 3, 2: 5, 3: 5, 4: 5, 5: 5, 6: 5, 7: 5, 8: 5, 9: 5, 10: 5}
ATT1 = ("q_in0 q_in1 m_in0 m_in1 "
        "passed sc_ready exp_done pv_done u_copied u_turned rd_done out_done mx_ready mx_done mx_joined mt_ready mrow_done")


def attention1(nc, s, k, b, q_dram):
    with ExitStack() as ctx:
        nm = f"as{b}_"
        sb = lambda n, sh, d=F32: ctx.enter_context(nc.sbuf_tensor(nm + n, sh, d))
        ps = lambda n, sh: ctx.enter_context(nc.psum_tensor(nm + n, sh, F32))
        q = k.q_slots
        prob = sb("prob", [P, RING, HALF])
        junk = sb("junk", [P, 2, HALF])
        mxd, mxf = sb("mxd", [P, G, TILES]), sb("mxf", [P, G, TILES // 2])
        mrow = sb("mrow", [G * TILES, P], F32R)
        u_sb, rd = sb("u_sb", [P, HALF]), sb("rd", [P, 4, G, 1])
        scp = [ps(f"scp{i}", [P, HALF]) for i in range(BANKS1)]
        mxp = [ps(f"mxp{i}", [P, HALF]) for i in range(MBANKS)]
        op, tp = ps("op", [P, HALF]), ps("tp", [P, 4, G, 2 * HD])
        mt = mxp[0]
        q_in, m_in = (s["q_in0"], s["q_in1"]), (s["m_in0"], s["m_in1"])
        g0 = b * NG
        MOVES = 16 * 4

        def steps(eng, step):
            step(-1, 1, -1, False, True)
            in_pairs(eng, 0, NG - 2, lambda t, slot, turn: step(t, slot, turn, True, True))
            step(NG - 2, 0, NG // 2 - 1, True, True)
            step(NG - 1, 1, NG // 2 - 1, True, False)

        with nc.Block() as block:
            @block.sync
            def _(sp):
                def move(t, slot, turn, half):
                    for blk in range(4):
                        sp.dma_start(words(q[slot][HD * blk:HD * (blk + 1), :, :]),
                                     q_dram[blk // 2, bass.ds(turn, 1), HD * G * half:HD * G * (half + 1), :]
                                     .rearrange("c (j d) s -> d (c j) s", d=HD)).then_inc(q_in[slot], 16)

                def step(t, slot, turn, scores, maxima):
                    if maxima:
                        sp.wait_ge(s["sc_ready"], at((t + g0) * UNITS))
                        move(t + 1, 1 - slot, turn + slot, 1 - slot)
                        sp.wait_ge(s["mrow_done"], at(t + g0 + 2))
                        sp.dma_start(words(q[1 - slot][MR:MR + 1, :, :]), words(mrow[:])).then_inc(m_in[1 - slot], 16)
                steps(sp, step)

            @block.scalar
            def _(act):
                def copy_out(t, hf):
                    act.wait_ge(s["pv_done"], at(t * QUADS + (12 if hf else 4)))
                    act.wait_ge(s["u_turned"], at(2 * t + hf))
                    nc.scalar.activation(u_sb[:], op[:], ACT.Copy).then_inc(s["u_copied"], 1)

                def step(t, slot, turn, scores, maxima):
                    t = t + g0
                    for n in range(QUADS):
                        qc, kt = QK[n]
                        if scores:
                            act.wait_ge(s["pv_done"], at(t * QUADS + n - 2))
                            for u in range(G * n, G * n + G):
                                c0 = max(kt - 4 * qc, 0) * P
                                act.wait_ge(s["sc_ready"], at(t * UNITS + u + 1))
                                nc.scalar.activation(prob[:, u % RING, c0:HALF], scp[u % BANKS1][:, c0:HALF], ACT.Exp).then_inc(s["exp_done"], 1)
                        if scores and n == 5:
                            copy_out(t, 0)
                    if maxima:
                        act.wait_ge(s["mt_ready"], at(t + 2))
                        if scores:
                            act.wait_ge(m_in[slot], 16 * (turn + b * NG // 2 + 1))
                        nc.scalar.activation(mrow[:], mt[0:G * TILES, 0:P], ACT.Copy, scale=-1.0).then_inc(s["mrow_done"], 1)
                    if scores:
                        copy_out(t, 1)
                steps(act, step)

            @block.vector
            def _(dve):
                def maximum(t, u, j, qt, part):
                    w = (qt % 4 + 1) * P
                    if u == 0:
                        dve.wait_ge(s["mt_ready"], at(t))
                    dve.wait_ge(s["mx_ready"], at(t * UNITS + u + 1))
                    if qt >= 4 and part == 0:
                        nc.vector.reduce_max(mxf[:, j, qt - 4:qt - 3], mxp[u % MBANKS][:], AX_X).then_inc(s["mx_done"], 1)
                    else:
                        dve.wait_ge(s["mx_done"], at(t * UNITS + u - 1))
                        apart(dve, s["passed"])
                        nc.vector.tensor_tensor_reduce(out=junk[:, u % 2, 0:w], in0=mxp[u % MBANKS][:, 0:w], in1=k.causal[:, HALF - w:HALF],
                                                       scale=1.0, scalar=LOWEST, op0=ALU.add, op1=ALU.max,
                                                       accum_out=mxd[:, j, qt:qt + 1]).then_inc(s["mx_done"], 1)

                def finish(t, hf):
                    m = 2 * (t + g0) + hf
                    dve.wait_ge(s["u_turned"], at(m + 1))
                    dve.wait_ge(s["out_done"], at(m))
                    nc.vector.reciprocal(rd[:], tp[:, :, :, HD:HD + 1]).then_inc(s["rd_done"], 1)
                    dve.wait_ge(s["rd_done"], at(m + 1))
                    nc.vector.tensor_tensor(k.att[:, 4 * hf:4 * hf + 4, bass.ds(t * G * HD, G * HD)].rearrange("p q (j d) -> p q j d", j=G),
                                            tp[:, :, :, 0:HD], rd[:].to_broadcast([P, 4, G, HD]), ALU.mult).then_inc(s["out_done"], 1)

                def step(t, slot, turn, scores, maxima):
                    for n in range(QUADS):
                        for kind, *piece in work(n, M_AT1, scores, maxima, ()):
                            if kind == "max":
                                maximum(t + g0 + 1, *piece)
                        if scores and n == 7:
                            finish(t, 0)
                        if maxima and n == max(M_AT1):
                            dve.wait_ge(s["mx_done"], at((t + g0 + 2) * UNITS))
                            nc.vector.tensor_tensor(mxd[:, :, TILES // 2:TILES], mxd[:, :, TILES // 2:TILES], mxf[:], ALU.max).then_inc(s["mx_joined"], 1)
                    if scores:
                        finish(t, 1)
                steps(dve, step)

            @block.tensor
            def _(pe):
                def score(t, slot, n, j):
                    qc, kt = QK[n]
                    u = G * n + j
                    c0 = min(max(kt - 4 * qc, 0) * P, HALF - 2 * P)
                    diag = kt >= 4 * qc
                    out = scp[u % BANKS1][:, c0:HALF]
                    pe.wait_ge(s["exp_done"], at(t * UNITS + u + 1 - BANKS1))
                    mm = nc.tensor.matmul(out, k.keys[:, kt * P:(kt + 1) * P], q[slot][:, j, HALF * qc + c0:HALF * (qc + 1)], start=True, stop=not diag)
                    if diag:
                        first = P if kt % 4 < 3 else 0
                        mm = nc.tensor.matmul(out[:, 0:2 * P], k.ident_r[:], k.after_r[:, first:first + 2 * P], start=False, stop=True)
                    mm.then_inc(s["sc_ready"], 1)

                def maximum(t, slot, u, j, qt, part):
                    k0 = HALF if qt >= 4 and part == 1 else 0
                    w = HALF if qt >= 4 and part == 0 else max((qt % 4 + 1) * P, 2 * P)
                    pe.wait_ge(s["mx_done"], at(t * UNITS + u + 1 - MBANKS))
                    nc.tensor.matmul(mxp[u % MBANKS][:, 0:w], q[slot][0:KR, j, qt * P:(qt + 1) * P], k.keys[0:KR, k0:k0 + w],
                                     start=True, stop=True).then_inc(s["mx_ready"], 1)

                def values(t, n):
                    qc, kt = QK[n]
                    c0 = max(kt - 4 * qc, 0) * P
                    pe.wait_ge(s["exp_done"], at(t * UNITS + G * n + G))
                    if kt == 0:
                        pe.wait_ge(s["u_copied"], at(2 * t + qc))
                    for j in range(G):
                        mm = nc.tensor.matmul(op[2 * HD * j:2 * HD * (j + 1), c0:HALF], k.vn[:, kt, :], prob[:, (G * n + j) % RING, c0:HALF],
                                              start=(kt == 0), stop=(kt == 4 * qc + 3))
                    mm.then_inc(s["pv_done"], 1)

                def turn_out(t, hf):
                    pe.wait_ge(s["u_copied"], at(2 * t + hf + 1))
                    pe.wait_ge(s["out_done"], at(2 * t + hf))
                    for i in range(4):
                        tr = nc.tensor.transpose(tp[:, i, :, :].rearrange("p j d -> p (j d)"), u_sb[:, i * P:(i + 1) * P], k.ident[:])
                    tr.then_inc(s["u_turned"], 1)

                def turn_maxima(t):
                    pe.wait_ge(s["mx_joined"], at(t + 1))
                    pe.wait_ge(s["mrow_done"], at(t))
                    nc.tensor.transpose(mt[0:G * TILES, 0:P], mxd[:].rearrange("p j q -> p (j q)"), k.ident[:]).then_inc(s["mt_ready"], 1)

                def step(t, slot, turn, scores, maxima):
                    t, turn = t + g0, turn + b * NG // 2
                    for n in range(QUADS + 2):
                        if scores and n == 0:
                            pe.wait_ge(q_in[slot], MOVES * (turn + 1))
                            pe.wait_ge(m_in[slot], 16 * (turn + 1))
                        for kind, *piece in work(n, M_AT1, scores, maxima, ()):
                            if kind == "score":
                                score(t, slot, n, piece[0])
                            if kind == "max":
                                if piece[0] == 0:
                                    pe.wait_ge(q_in[1 - slot], MOVES * (turn + slot + 1))
                                    pe.wait_ge(s["mrow_done"], at(t + 1))
                                maximum(t + 1, 1 - slot, *piece)
                            if kind == "values":
                                if piece[0] == 0 and n == QUADS - 1 and maxima:
                                    turn_maxima(t + 1)
                                if piece[0] == 0:
                                    values(t, n - 2)
                        if scores and n == 7:
                            turn_out(t, 0)
                    if maxima and not scores:
                        turn_maxima(t + 1)
                    if scores:
                        turn_out(t, 1)
                steps(pe, step)


FF1 = (NORM_SEMS + OUT_SEMS + " at_psum at_done")


def feed1(nc, s, k, b, x_in, w_dram, t, x_out):
    with ExitStack() as ctx:
        nm = f"fg{b}_"
        sb = lambda n, sh, d=F32: ctx.enter_context(nc.sbuf_tensor(nm + n, sh, d))
        ps = lambda n, sh: ctx.enter_context(nc.psum_tensor(nm + n, sh, F32))
        own = semaphores(ctx, nc, nm, "wo_in w_in x_in0 x_in1 x_out")
        wo_in, w_in, x_in_sem, x_out_sem = own["wo_in"], own["w_in"], (own["x_in0"], own["x_in1"]), own["x_out"]
        wo, wf, bias = sb("wo", [P, C, D]), sb("wf", [P, C, D]), sb("bias", [P, D])
        a_t = sb("a_t", [P, 2, C, P])
        xt, x1 = sb("xt", [P, TILES, D]), sb("x1", [P, TILES, D])
        st, mv, sd, xn, h_t, hps = norm_tensors(sb, ps, 2)
        yps, fps, aps = ps("yps", [P, 2, D]), ps("fps", [P, 2, D]), ps("aps", [P, 2, C, P])
        with nc.Block() as block:
            @block.sync
            def _(sp):
                sp.dma_start(wo[:], t["wo1"].rearrange("(k p) n -> p k n", p=P)).then_inc(wo_in, 16)
                load_x(sp, b, xt, x_in, x_in_sem)
                sp.dma_start(wf[:], w_dram.rearrange("(k p) n -> p k n", p=P)).then_inc(w_in, 16)
                sp.dma_start(bias[:], t["b_base1"]).then_inc(w_in, 16)
                store_x(sp, s, b, xt, x_out, x_out_sem)

            @block.tensor
            def _(pe):
                def turn(n0):
                    n = n0 + b * TILES
                    pe.wait_ge(s["at_done"], at(n - 1))
                    for c in range(C):
                        tr = nc.tensor.transpose(aps[:, n0 % 2, c, :], k.att[:, n0, c * P:(c + 1) * P], k.ident[:])
                    tr.then_inc(s["at_psum"], 1)

                def project(n0):
                    n = n0 + b * TILES
                    if n0 + 1 < TILES:
                        turn(n0 + 1)
                    pe.wait_ge(s["at_done"], at(n + 1))
                    pe.wait_ge(s["gated"], at(n - 1))
                    for c in range(C):
                        mm = nc.tensor.matmul(yps[:, n0 % 2, :], a_t[:, n0 % 2, c, :], wo[:, c, :], start=(c == 0), stop=(c == C - 1))
                    mm.then_inc(s["y_psum"], 1)

                def feed(h):
                    for n0 in tiles(h):
                        n = n0 + b * TILES
                        pe.wait_ge(s["h_done"], at(C * n + C))
                        pe.wait_ge(s["biased"], at(n - 1))
                        for c in range(C):
                            mm = nc.tensor.matmul(fps[:, n0 % 2, :], h_t[:, n0, c, :], wf[:, c, :], start=(c == 0), stop=(c == C - 1))
                        mm.then_inc(s["f_psum"], 1)

                def normed(h):
                    for n0 in tiles(h):
                        turn_normed(nc, pe, s, b, n0, xn, k.ident, hps, 2)
                turn(0)
                pe.wait_ge(wo_in, 16)
                for n0 in range(TH + 2):
                    project(n0)
                normed(0)
                for n0 in range(TH + 2, TILES):
                    project(n0)
                pe.wait_ge(w_in, 32)
                feed(0)
                normed(1)
                feed(1)

            @block.scalar
            def _(act):
                def copy_att(n0):
                    n = n0 + b * TILES
                    act.wait_ge(s["at_psum"], at(n + 1))
                    act.wait_ge(s["y_psum"], at(n - 1))
                    nc.scalar.activation(a_t[:, n0 % 2, :, :], aps[:, n0 % 2], ACT.Copy).then_inc(s["at_done"], 1)
                for n0 in range(TH + 2):
                    copy_att(n0)
                half_deviation(nc, act, s, b, 0, mv, sd, k.ln_eps)
                copy_att(TH + 2)
                for n0 in tiles(0):
                    modulate(nc, act, s, b, n0, hps, 2, h_t, k.mod_t, 2)
                copy_att(TH + 3)
                half_deviation(nc, act, s, b, 1, mv, sd, k.ln_eps)
                for n0 in tiles(1):
                    modulate(nc, act, s, b, n0, hps, 2, h_t, k.mod_t, 2)

            @block.vector
            def _(dve):
                def first(n0):
                    first_residual(nc, dve, s, b, n0, x_in_sem, yps, xt, x1, st, k.gates)
                for n0 in tiles(0):
                    first(n0)
                half_stats(nc, dve, s, b, 0, st, mv)
                half_norm(nc, dve, s, b, 0, x1, mv, sd, xn)
                for n0 in tiles(1):
                    first(n0)
                half_stats(nc, dve, s, b, 1, st, mv)
                half_norm(nc, dve, s, b, 1, x1, mv, sd, xn)
                dve.wait_ge(w_in, 32)
                for n0 in range(TILES):
                    second_residual(nc, dve, s, b, n0, fps, bias, x1, xt, k.gates)
        clear(nc, own)


class Kept:
    pass


def constants(nc, k, t):
    with ExitStack() as ctx:
        s = semaphores(ctx, nc, "co_", "filled ident_done causal_done after_done rounded")
        after = ctx.enter_context(nc.sbuf_tensor("co_after", [P, 3 * P], F32))
        with nc.Block() as block:
            @block.vector
            def _(dve):
                dve.wait_ge(s["ident_done"], 1)
                nc.vector.tensor_copy(k.ident_r[:], k.ident[:]).then_inc(s["rounded"], 1)
                dve.wait_ge(s["after_done"], 1)
                nc.vector.tensor_copy(k.after_r[:], after[:]).then_inc(s["rounded"], 1)

            @block.gpsimd
            def _(pool):
                pool.memset(k.ident[:], 0.0).then_inc(s["filled"], 1)
                pool.memset(k.causal[:], 0.0).then_inc(s["filled"], 1)
                pool.memset(k.ones[:], 1.0).then_inc(s["filled"], 1)
                pool.memset(k.zeros[:], 0.0).then_inc(s["filled"], 1)
                pool.memset(k.ln_eps[:], LN_EPS).then_inc(s["filled"], 1)
                pool.memset(after[:], 0.0).then_inc(s["filled"], 1)
                for e in range(E):
                    pool.memset(k.count[:, e:e + 1], float(e + 1)).then_inc(s["filled"], 1)
                pool.wait_ge(s["filled"], 6 + E)
                pool.affine_select(out=k.ident[:], in_=k.ident[:], compare_op=ALU.not_equal, fill=1.0, base=0,
                                   pattern=[[-1, P]], channel_multiplier=1).then_inc(s["ident_done"], 1)
                pool.affine_select(out=k.causal[:, HALF - P:HALF], in_=k.causal[:, HALF - P:HALF], compare_op=ALU.is_ge, fill=BELOW,
                                   base=0, pattern=[[-1, P]], channel_multiplier=1).then_inc(s["causal_done"], 1)
                pool.affine_select(out=after[:, P:2 * P], in_=after[:, P:2 * P], compare_op=ALU.is_ge, fill=BELOW,
                                   base=0, pattern=[[1, P]], channel_multiplier=-1).then_inc(s["after_done"], 1)
        clear(nc, s)


def layer0(nc, k, t, x_in, x_mid, scratch):
    with ExitStack() as ctx:
        sb = lambda n, sh, d=F32: ctx.enter_context(nc.sbuf_tensor("l0_" + n, sh, d))
        k.mod_t, k.gates = sb("mod", [P, 4, C, B]), sb("gates", [P, 2, B, D])
        modulation(nc, "m0_", t["c0"], t["wmod0"], k.mod_t, k.gates)
        join_weights(nc, t, scratch["wq0"], scratch["wout0"])
        sa = semaphores(ctx, nc, "a0_", IN0)
        sc = semaphores(ctx, nc, "c0_", FF0)
        st = semaphores(ctx, nc, "t0_", ATT0)
        for s in (sa, sc, st):
            prime(nc, s)
        k.o_t = sb("o_t", [P, NG, S])
        for b in range(B):
            with ExitStack() as inner:
                si = lambda n, sh, d=F32: inner.enter_context(nc.sbuf_tensor(f"l0b{b}_" + n, sh, d))
                k.qa_t = si("qa_t", [QA, S])
                k.khi, k.klo = si("khi", [KR + 1, S], F32R), si("klo", [KR, S], F32R)
                k.cn = si("cn", [P, TILES, LAT])
                k.cos_t, k.sin_t = si("cos_t", [P, S]), si("sin_t", [P, S])
                with ExitStack() as first:
                    sf = lambda n, sh, d=F32: first.enter_context(nc.sbuf_tensor(f"l0b{b}_" + n, sh, d))
                    k.cos_n, k.sin_n = sf("cos_n", [P, TILES, RH]), sf("sin_n", [P, TILES, RH])
                    k.kv_ln = sf("kv_ln", [P, LAT])
                    sems = semaphores(first, nc, f"l0b{b}_", "table_in one_row")
                    with nc.Block() as block:
                        @block.sync
                        def _(sp):
                            for dst, name in ((k.cos_t, "cos_t"), (k.sin_t, "sin_t"), (k.cos_n, "cos_n"), (k.sin_n, "sin_n"), (k.kv_ln, "kv_ln")):
                                sp.dma_start(dst[:], t[name]).then_inc(sems["table_in"], 16)
                            sp.wait_ge(sems["table_in"], 80)

                        @block.vector
                        def _(dve):
                            nc.vector.memset(k.khi[MR:MR + 1, :].bitcast(F32), 1.0).then_inc(sems["one_row"], 1)
                    clear(nc, sems)
                    latents(nc, sa, x_in, b, t, k)
                attention0(nc, st, k, b, scratch["wq0"])
            feed0(nc, sc, k, b, x_in, scratch["wout0"], t, x_mid)
        clear(nc, sa, sc, st)


def layer1(nc, k, t, x_in, out, scratch):
    with ExitStack() as ctx:
        sb = lambda n, sh, d=F32: ctx.enter_context(nc.sbuf_tensor("l1_" + n, sh, d))
        k.mod_t, k.gates = sb("mod", [P, 4, C, B]), sb("gates", [P, 2, B, D])
        modulation(nc, "m1_", t["c1"], t["wmod1"], k.mod_t, k.gates)
        join_feed1(nc, t, scratch["w_feed1"])
        sa = semaphores(ctx, nc, "a1_", IN1)
        sc = semaphores(ctx, nc, "c1_", FF1)
        st = semaphores(ctx, nc, "t1_", ATT1)
        for s in (sa, sc, st):
            prime(nc, s)
        k.att = sb("att", [P, TILES, D])
        k.vn = sb("vn", [P, TILES, 2 * HD])
        k.keys = sb("keys", [KR + 1, S], F32R)
        k.q_slots = [sb(f"q{i}", [KR + 1, G, S], F32R) for i in range(2)]
        k.qp_hi, k.qp_lo = sb("qp_hi", [P, C, S], F32R), sb("qp_lo", [P, C, S], F32R)
        filled = ctx.enter_context(nc.semaphore("l1_filled"))
        with nc.Block() as block:
            @block.vector
            def _(dve):
                nc.vector.memset(k.vn[:, :, HD:2 * HD], 1.0).then_inc(filled, 1)
                nc.vector.memset(k.keys[4 * HD:KR, :].bitcast(F32), 0.0).then_inc(filled, 1)
                nc.vector.memset(k.keys[MR:MR + 1, :].bitcast(F32), 1.0).then_inc(filled, 1)
                for q in k.q_slots:
                    nc.vector.memset(q[4 * HD:KR, :, :].bitcast(F32), 0.0).then_inc(filled, 1)
        for b in range(B):
            queries1(nc, sa, x_in, b, t, k, scratch["queries1"])
            attention1(nc, st, k, b, scratch["queries1"])
            feed1(nc, sc, k, b, x_in, scratch["w_feed1"], t, out)


def build(nc, t, out, scratch, upto=9):
    nc.disable_value_cache = True
    with ExitStack() as ctx:
        sb = lambda n, sh, d=F32: ctx.enter_context(nc.sbuf_tensor(n, sh, d))
        k = Kept()
        k.ident, k.causal, k.ones = sb("ident", [P, P]), sb("causal", [P, HALF]), sb("ones", [P, LAT])
        k.ident_r, k.after_r = sb("ident_r", [P, P], F32R), sb("after_r", [P, 3 * P], F32R)
        k.zeros, k.count, k.ln_eps = sb("zeros", [P, E]), sb("count", [P, E]), sb("ln_eps", [P, 1])
        constants(nc, k, t)
        layer0(nc, k, t, t["x"], out if upto == 0 else scratch["x_mid"], scratch)
        if upto > 0:
            layer1(nc, k, t, scratch["x_mid"], out, scratch)


def rope_tables():
    base, factor, orig = 10000.0, 128.0, 1024
    corr = lambda r: ROPE * math.log(orig / (r * 2 * math.pi)) / (2 * math.log(base))
    low, high = max(math.floor(corr(32.0)), 0), min(math.ceil(corr(1.0)), ROPE - 1)
    hi = high + 0.001 if low == high else float(high)
    ramp = np.clip((np.arange(RH, dtype=np.float32) - low) / (hi - low), 0.0, 1.0)
    keep = 1.0 - ramp
    extra = 1.0 / base ** (np.arange(0, ROPE, 2, dtype=np.float32) / ROPE)
    inv = extra / factor * (1.0 - keep) + extra * keep
    f = np.outer(np.arange(S, dtype=np.float32), inv)
    return np.cos(f).astype(np.float32), np.sin(f).astype(np.float32)


def fourier():
    n = D
    eye = np.eye(n)
    spectrum = np.concatenate([eye[:, :1] * math.sqrt(n), (eye[:, 1:n - 1:2] - 1j * eye[:, 2:n:2][:, :(n - 1) // 2]) * math.sqrt(n / 2),
                               eye[:, -1:] * math.sqrt(n)], axis=-1)
    return np.fft.irfft(spectrum, n=n, axis=-1).astype(np.float32)


def lay_out(i):
    a = {n: np.asarray(v) for n, v in i.items()}
    col = lambda c: np.ascontiguousarray(c.T.reshape(C, P, B).transpose(1, 0, 2))
    rows = lambda v: np.broadcast_to(v.reshape(1, -1), (P, v.size))
    cos, sin = rope_tables()
    kv = a["L0_attn_wkv_a"]
    wqb = a["L0_attn_wq_b"].reshape(H, NOPE + ROPE, QA)
    wkvb = a["L0_attn_wkv_b"].reshape(H, NOPE + VD, LAT)
    pe = wqb[:, NOPE:].reshape(NG, G, RH, 2, QA)
    o = {
        "x": a["L0_attn_x"].reshape(B * S, D),
        "c0": col(a["L0_c"]), "wmod0": a["L0_wmod"], "c1": col(a["L1_c"]), "wmod1": a["L1_wmod"],
        "w_a": np.concatenate([a["L0_attn_wq_a"].T, kv[:LAT].T, kv[LAT::2].T, kv[LAT + 1::2].T], axis=1),
        "q_ln": a["L0_attn_q_a_ln_w"].reshape(QA, 1), "kv_ln": rows(a["L0_attn_kv_a_ln_w"]),
        "wqb_nope": wqb[:, :NOPE].transpose(1, 0, 2), "wk_b": wkvb[:, :NOPE].transpose(1, 0, 2), "wv_b": wkvb[:, NOPE:].transpose(1, 0, 2),
        "wqb_rope": pe.transpose(4, 0, 3, 1, 2).reshape(QA, NG, 2, P),
        "wo_t": a["L0_attn_wo"].T.reshape(H, VD, D),
        "cos_t": np.tile(cos.T, (G, 1)), "sin_t": np.tile(sin.T, (G, 1)),
        "cos_n": cos.reshape(TILES, P, RH).transpose(1, 0, 2), "sin_n": sin.reshape(TILES, P, RH).transpose(1, 0, 2),
        "w_base0": a["L0_ffn_W_base"].T, "b_base0": rows(a["L0_ffn_b_base"]), "b_router": rows(a["L0_ffn_b_router"]),
        "w_low0": np.concatenate([a["L0_ffn_lora_A"].transpose(1, 0, 2).reshape(D, E * R), a["L0_ffn_W_router"].T], axis=1),
        "lora_b": a["L0_ffn_lora_B"].reshape(E * R, D),
        "wq1": a["L1_attn_wq"], "wkv1": np.concatenate([a["L1_attn_wk"], a["L1_attn_wv"]], axis=1), "wo1": a["L1_attn_wo"],
        "w_base1": a["L1_ffn_W_base"].T, "b_base1": rows(a["L1_ffn_b_base"]),
        "enc": np.concatenate([a["L1_ffn_enc0"], a["L1_ffn_enc1"]], axis=0),
        "coefs": np.concatenate([a["L1_ffn_coefs0"], a["L1_ffn_coefs1"]], axis=2).reshape(E1, C, P, LOW).transpose(2, 0, 1, 3),
        "masks": np.concatenate([a["L1_ffn_mask0"], a["L1_ffn_mask1"]], axis=2).reshape(E1, C, P, LOW).transpose(2, 0, 1, 3),
        "fourier": fourier(),
    }
    o = {n: np.ascontiguousarray(v) for n, v in o.items()}
    o["masks"] = o["masks"].view(np.int32)
    return o


SCRATCH = {"wq0": (NG, QA, 3 * P), "wout0": (NG, P, D), "x_mid": (B * S, D), "w_feed1": (D, D), "queries1": (2, C, P, S)}


def kernel(**inputs):
    import concourse.bacc as bacc
    from concourse.bass_utils import run_bass_kernel_spmd

    nc = bacc.Bacc("TRN2", target_bir_lowering=False, num_devices=1)
    arrays = lay_out(inputs)
    t = {n: nc.dram_tensor(f"in_{n}", v.shape, mybir.dt.from_np(v.dtype), kind="ExternalInput").ap() for n, v in arrays.items()}
    scratch = {n: nc.dram_tensor(f"scratch_{n}", shape, F32, kind="Internal").ap() for n, shape in SCRATCH.items()}
    out = nc.dram_tensor("out", (B * S, D), F32, kind="ExternalOutput").ap()
    build(nc, t, out, scratch)
    r = run_bass_kernel_spmd(nc, [{f"in_{n}": v for n, v in arrays.items()}], core_ids=[0])
    return r.results[0]["out"].reshape(B, S, D)
```
